# Optimizing a Trainium2 kernel written in Bass

```python
import numpy as np
import jax
import jax.numpy as jnp

def _softmax(x, axis=-1):
    return jax.nn.softmax(x, axis=axis)

def _gelu(x):
    return jax.nn.gelu(x, approximate=True)

def _silu(x):
    return jax.nn.silu(x)

def _sigmoid(x):
    return jax.nn.sigmoid(x)

def _layernorm(x, axis=-1, eps=1e-05):
    m = jnp.mean(x, axis=axis, keepdims=True)
    v = jnp.var(x, axis=axis, keepdims=True)
    return (x - m) / jnp.sqrt(v + eps)

def _scatter_add(tgt, idx, src, axis=0):
    return tgt.at[idx].add(src)

def _segment_sum(src, seg, n):
    return jax.ops.segment_sum(src, seg, n)
kernel_name = 'mk_recurrent_d2_jaxref_r8_3c6b36'

def setup_inputs(seed: int=0):
    np.random.seed(seed)
    _w = jnp.asarray

    def _L0_attn_setup():
        import jax, jax.numpy as jnp
        import numpy as np
        NUM_HEADS = 16

        def _l2_normalize_complex(z):
            n = jnp.sqrt(jnp.sum(jnp.abs(z) ** 2, axis=-1, keepdims=True))
            return z / n
        key = jax.random.key(seed)
        k1, k2, k3, k4 = jax.random.split(key, 4)
        B, S, D = (4, 512, 256)
        scale = 1.0 / np.sqrt(D)
        return {'x': jax.random.normal(k1, (B, S, D), dtype=jnp.float32), 'W_q': jax.random.normal(k2, (D, D), dtype=jnp.float32) * scale, 'W_kv': jax.random.normal(k3, (D, D), dtype=jnp.float32) * scale, 'W_o': jax.random.normal(k4, (D, D), dtype=jnp.float32) * scale}
    _L0_attn_in = _L0_attn_setup()

    def _L0_ffn_setup():
        import jax, jax.numpy as jnp
        import numpy as np
        B, S, H = (2, 128, 256)
        E, K, F = (64, 8, 96)
        CAP = 64
        key = jax.random.key(seed)
        k1, k2, k3, k4, k5 = jax.random.split(key, 5)
        scale_h = 1.0 / np.sqrt(H)
        scale_f = 1.0 / np.sqrt(F)
        return {'hidden_states': jax.random.normal(k1, (B, S, H), jnp.float32), 'router_w': jax.random.normal(k2, (E, H), jnp.float32) * scale_h, 'w_gate': jax.random.normal(k3, (E, H, F), jnp.float32) * scale_h, 'w_up': jax.random.normal(k4, (E, H, F), jnp.float32) * scale_h, 'w_down': jax.random.normal(k5, (E, F, H), jnp.float32) * scale_f}
    _L0_ffn_in = _L0_ffn_setup()

    def _L1_attn_setup():
        import jax, jax.numpy as jnp
        import numpy as np
        import math
        B, L, D = (2, 256, 256)
        H, DH = (16, 128)
        R = 16
        WIN = 64
        EPS = 1e-06

        def _lora_proj(h, Wb, A, Bm, scale):
            return h @ Wb.T + h @ A.T @ Bm.T * scale

        def _rope_freqs(seq_len, d_head):
            half = d_head // 2
            theta = 1.0 / 10000.0 ** (jnp.arange(half, dtype=jnp.float32) / half)
            freqs = jnp.arange(seq_len, dtype=jnp.float32)[:, None] * theta[None, :]
            emb = jnp.concatenate([freqs, freqs], axis=-1)
            return (jnp.cos(emb), jnp.sin(emb))

        def _apply_rope(x, cos, sin):
            half = x.shape[-1] // 2
            x1, x2 = (x[..., :half], x[..., half:])
            rotated = jnp.concatenate([-x2, x1], axis=-1)
            return x * cos[None, None] + rotated * sin[None, None]
        key = jax.random.key(seed)
        ks = jax.random.split(key, 16)

        def rn(k, shape, s=1.0):
            return jax.random.normal(k, shape, dtype=jnp.float32) * s
        d_in_std = 1.0 / math.sqrt(D)
        return {'x': rn(ks[0], (B, L, D)), 'norm_w': jnp.ones((D,), jnp.float32), 'wq': rn(ks[1], (H * DH, D), d_in_std), 'wk': rn(ks[2], (H * DH, D), d_in_std), 'wv': rn(ks[3], (H * DH, D), d_in_std), 'wo': rn(ks[4], (D, H * DH), d_in_std), 'qA': rn(ks[5], (R, D), 0.02), 'qB': rn(ks[6], (H * DH, R), 0.02), 'kA': rn(ks[7], (R, D), 0.02), 'kB': rn(ks[8], (H * DH, R), 0.02), 'vA': rn(ks[9], (R, D), 0.02), 'vB': rn(ks[10], (H * DH, R), 0.02), 'oA': rn(ks[11], (R, H * DH), 0.02), 'oB': rn(ks[12], (D, R), 0.02)}
    _L1_attn_in = _L1_attn_setup()

    def _L1_ffn_setup():
        import jax, jax.numpy as jnp
        import numpy as np
        TOP_K = 4

        def _silu_and_mul(gu):
            g, u = jnp.split(gu, 2, axis=-1)
            return jax.nn.silu(g) * u
        key = jax.random.key(seed)
        ks = jax.random.split(key, 7)
        H, E, I, Is = (256, 16, 176, 704)
        s = 0.02
        return {'hidden_states': jax.random.normal(ks[0], (4, 128, H), dtype=jnp.float32), 'gate_w': jax.random.normal(ks[1], (E, H), dtype=jnp.float32) * s, 'sgate_w': jax.random.normal(ks[2], (1, H), dtype=jnp.float32) * s, 'w13': jax.random.normal(ks[3], (E, 2 * I, H), dtype=jnp.float32) * s, 'w2': jax.random.normal(ks[4], (E, H, I), dtype=jnp.float32) * s, 'shared_gate_up_w': jax.random.normal(ks[5], (2 * Is, H), dtype=jnp.float32) * s, 'shared_down_w': jax.random.normal(ks[6], (H, Is), dtype=jnp.float32) * s}
    _L1_ffn_in = _L1_ffn_setup()
    _d = {'L0_attn_x': _L0_attn_in['x'], 'L0_attn_W_q': _L0_attn_in['W_q'], 'L0_attn_W_kv': _L0_attn_in['W_kv'], 'L0_attn_W_o': _L0_attn_in['W_o'], 'L0_ffn_router_w': _L0_ffn_in['router_w'], 'L0_ffn_w_gate': _L0_ffn_in['w_gate'], 'L0_ffn_w_up': _L0_ffn_in['w_up'], 'L0_ffn_w_down': _L0_ffn_in['w_down'], 'L1_attn_norm_w': _L1_attn_in['norm_w'], 'L1_attn_wq': _L1_attn_in['wq'], 'L1_attn_wk': _L1_attn_in['wk'], 'L1_attn_wv': _L1_attn_in['wv'], 'L1_attn_wo': _L1_attn_in['wo'], 'L1_attn_qA': _L1_attn_in['qA'], 'L1_attn_qB': _L1_attn_in['qB'], 'L1_attn_kA': _L1_attn_in['kA'], 'L1_attn_kB': _L1_attn_in['kB'], 'L1_attn_vA': _L1_attn_in['vA'], 'L1_attn_vB': _L1_attn_in['vB'], 'L1_attn_oA': _L1_attn_in['oA'], 'L1_attn_oB': _L1_attn_in['oB'], 'L1_ffn_gate_w': _L1_ffn_in['gate_w'], 'L1_ffn_sgate_w': _L1_ffn_in['sgate_w'], 'L1_ffn_w13': _L1_ffn_in['w13'], 'L1_ffn_w2': _L1_ffn_in['w2'], 'L1_ffn_shared_gate_up_w': _L1_ffn_in['shared_gate_up_w'], 'L1_ffn_shared_down_w': _L1_ffn_in['shared_down_w']}
    _x0 = _d['L0_attn_x']
    _d['L0_attn_x'] = jax.random.normal(jax.random.fold_in(jax.random.key(seed), 1), (4, 512, 256), dtype=_x0.dtype)
    del _x0
    return _d

def reference(L0_attn_x, L0_attn_W_q, L0_attn_W_kv, L0_attn_W_o, L0_ffn_router_w, L0_ffn_w_gate, L0_ffn_w_up, L0_ffn_w_down, L1_attn_norm_w, L1_attn_wq, L1_attn_wk, L1_attn_wv, L1_attn_wo, L1_attn_qA, L1_attn_qB, L1_attn_kA, L1_attn_kB, L1_attn_vA, L1_attn_vB, L1_attn_oA, L1_attn_oB, L1_ffn_gate_w, L1_ffn_sgate_w, L1_ffn_w13, L1_ffn_w2, L1_ffn_shared_gate_up_w, L1_ffn_shared_down_w):

    def _L0_attn_ref(x, W_q, W_kv, W_o):
        import jax, jax.numpy as jnp
        import numpy as np
        NUM_HEADS = 16

        def _l2_normalize_complex(z):
            n = jnp.sqrt(jnp.sum(jnp.abs(z) ** 2, axis=-1, keepdims=True))
            return z / n
        B, S, D = x.shape
        H = NUM_HEADS
        hd = D // H
        q = (x @ W_q.T).reshape(B, S, H, hd)
        kv = (x @ W_kv.T).reshape(B, S, H, hd)
        qf = jnp.fft.fft(q, axis=-1)
        kvf = jnp.fft.fft(kv, axis=-1)
        qf = _l2_normalize_complex(qf)
        kvf = _l2_normalize_complex(kvf)
        kvf = jnp.cumsum(kvf, axis=1)
        qv = qf * kvf
        values_hat = jnp.fft.ifft(qv, axis=-1).real.astype(x.dtype)
        values_hat = values_hat.reshape(B, S, D)
        return values_hat @ W_o.T

    def _L0_ffn_ref(hidden_states, router_w, w_gate, w_up, w_down):
        import jax, jax.numpy as jnp
        import numpy as np
        B, S, H = (2, 128, 256)
        E, K, F = (64, 8, 96)
        CAP = 64
        b, s, h = hidden_states.shape
        T = b * s
        xf = hidden_states.reshape(T, h)
        logits = xf @ router_w.T
        scores = jax.nn.softmax(logits.astype(jnp.float32), axis=-1)
        topk_w, topk_idx = jax.lax.top_k(scores, K)
        topk_w = topk_w / (topk_w.sum(axis=-1, keepdims=True) + 1e-20)
        slot_expert = topk_idx.reshape(-1)
        slot_token = jnp.repeat(jnp.arange(T), K)
        onehot = jax.nn.one_hot(slot_expert, E, dtype=jnp.int32)
        pos = (jnp.cumsum(onehot, axis=0) * onehot).sum(-1) - 1
        valid = pos < CAP
        dest = jnp.where(valid, slot_expert * CAP + pos, E * CAP)
        buf = jnp.zeros((E * CAP + 1, h), xf.dtype).at[dest].set(xf[slot_token])
        xb = buf[:E * CAP].reshape(E, CAP, h)
        gate = jnp.einsum('ech,ehf->ecf', xb, w_gate)
        up = jnp.einsum('ech,ehf->ecf', xb, w_up)
        hmid = jax.nn.silu(gate) * up
        yb = jnp.einsum('ecf,efh->ech', hmid, w_down).reshape(E * CAP, h)
        yb = jnp.concatenate([yb, jnp.zeros((1, h), yb.dtype)], axis=0)
        slot_out = yb[dest] * topk_w.reshape(-1)[:, None].astype(yb.dtype)
        out = jnp.zeros((T, h), yb.dtype).at[slot_token].add(slot_out)
        return out.reshape(b, s, h)

    def _L1_attn_ref(x, norm_w, wq, wk, wv, wo, qA, qB, kA, kB, vA, vB, oA, oB):
        import jax, jax.numpy as jnp
        import numpy as np
        import math
        B, L, D = (2, 256, 256)
        H, DH = (16, 128)
        R = 16
        WIN = 64
        EPS = 1e-06

        def _lora_proj(h, Wb, A, Bm, scale):
            return h @ Wb.T + h @ A.T @ Bm.T * scale

        def _rope_freqs(seq_len, d_head):
            half = d_head // 2
            theta = 1.0 / 10000.0 ** (jnp.arange(half, dtype=jnp.float32) / half)
            freqs = jnp.arange(seq_len, dtype=jnp.float32)[:, None] * theta[None, :]
            emb = jnp.concatenate([freqs, freqs], axis=-1)
            return (jnp.cos(emb), jnp.sin(emb))

        def _apply_rope(x, cos, sin):
            half = x.shape[-1] // 2
            x1, x2 = (x[..., :half], x[..., half:])
            rotated = jnp.concatenate([-x2, x1], axis=-1)
            return x * cos[None, None] + rotated * sin[None, None]
        lora_scale = 1.0 / qA.shape[0]
        residual = x
        h = x * jax.lax.rsqrt(jnp.mean(x * x, axis=-1, keepdims=True) + EPS) * norm_w
        Q = _lora_proj(h, wq, qA, qB, lora_scale)
        K = _lora_proj(h, wk, kA, kB, lora_scale)
        V = _lora_proj(h, wv, vA, vB, lora_scale)
        b, l, _ = x.shape
        Q = Q.reshape(b, l, H, DH).transpose(0, 2, 1, 3)
        K = K.reshape(b, l, H, DH).transpose(0, 2, 1, 3)
        V = V.reshape(b, l, H, DH).transpose(0, 2, 1, 3)
        cos, sin = _rope_freqs(l, DH)
        Q = _apply_rope(Q, cos, sin)
        K = _apply_rope(K, cos, sin)
        i = jnp.arange(l)[:, None]
        j = jnp.arange(l)[None, :]
        valid = (j <= i) & (j >= i - WIN + 1)
        mask = jnp.where(valid, 0.0, -jnp.inf).astype(x.dtype)
        scores = jnp.einsum('bhqd,bhkd->bhqk', Q, K) / math.sqrt(DH)
        attn = jax.nn.softmax(scores + mask[None, None], axis=-1)
        out = jnp.einsum('bhqk,bhkd->bhqd', attn, V)
        out = out.transpose(0, 2, 1, 3).reshape(b, l, H * DH)
        out = _lora_proj(out, wo, oA, oB, lora_scale)
        return residual + out

    def _L1_ffn_ref(hidden_states, gate_w, sgate_w, w13, w2, shared_gate_up_w, shared_down_w):
        import jax, jax.numpy as jnp
        import numpy as np
        TOP_K = 4

        def _silu_and_mul(gu):
            g, u = jnp.split(gu, 2, axis=-1)
            return jax.nn.silu(g) * u
        B, S, H = hidden_states.shape
        x = hidden_states.reshape(-1, H)
        E = gate_w.shape[0]
        shared = _silu_and_mul(x @ shared_gate_up_w.T) @ shared_down_w.T
        shared = shared * jax.nn.sigmoid(x @ sgate_w.T)
        router_logits = x @ gate_w.T
        routing_weights = jax.nn.softmax(router_logits.astype(jnp.float32), axis=-1)
        topk_w, topk_ids = jax.lax.top_k(routing_weights, TOP_K)

        def body(acc, ew):
            w13_e, w2_e, e = ew
            coef = jnp.sum(jnp.where(topk_ids == e, topk_w, 0.0), axis=-1)
            h = _silu_and_mul(x @ w13_e.T)
            acc = acc + (h @ w2_e.T).astype(jnp.float32) * coef[:, None]
            return (acc, None)
        init = jnp.zeros((x.shape[0], H), dtype=jnp.float32)
        sparse_out, _ = jax.lax.scan(body, init, (w13, w2, jnp.arange(E)))
        out = shared + sparse_out.astype(x.dtype)
        return out.reshape(B, S, H)
    x = L0_attn_x
    xn = _layernorm(x, axis=-1)
    s = _L0_attn_ref(xn, L0_attn_W_q, L0_attn_W_kv, L0_attn_W_o)
    g = _silu(_L0_ffn_ref(xn, L0_ffn_router_w, L0_ffn_w_gate, L0_ffn_w_up, L0_ffn_w_down))
    x = x + s * g
    xn = _layernorm(x, axis=-1)
    s = _L1_attn_ref(xn, L1_attn_norm_w, L1_attn_wq, L1_attn_wk, L1_attn_wv, L1_attn_wo, L1_attn_qA, L1_attn_qB, L1_attn_kA, L1_attn_kB, L1_attn_vA, L1_attn_vB, L1_attn_oA, L1_attn_oB)
    g = _silu(_L1_ffn_ref(xn, L1_ffn_gate_w, L1_ffn_sgate_w, L1_ffn_w13, L1_ffn_w2, L1_ffn_shared_gate_up_w, L1_ffn_shared_down_w))
    x = x + s * g
    return x

_drawn_inputs = setup_inputs


def setup_inputs(seed=0):
    import zlib

    import numpy as np

    out = dict(_drawn_inputs(seed))
    spreads = {'L1_attn_norm_w': (1.0, 0.2)}
    factors = {}
    for name, (base, spread) in spreads.items():
        noise = np.random.default_rng([zlib.crc32(name.encode()), seed]).standard_normal(out[name].shape)
        drawn = base * np.exp(spread * noise) if base else spread * noise
        out[name] = jnp.asarray(drawn.astype(out[name].dtype))
    for name, factor in factors.items():
        out[name] = (out[name] * factor).astype(out[name].dtype)
    return out
```

```python
from contextlib import ExitStack

import concourse.bass as bass
import numpy as np
from concourse import mybir

F32 = mybir.dt.float32
BF16 = mybir.dt.bfloat16
U32 = mybir.dt.uint32
I32 = mybir.dt.int32
ALU = mybir.AluOpType
ACT = mybir.ActivationFunctionType
AX = mybir.AxisListType

P = 128
T = 2048
NB, SEQ, D = 4, 512, 256
NT = T // P
TPB = SEQ // P
DC = D // P
LN_EPS = 1e-5

H0, HD0 = 16, 16
E0, K0, CAP, F0 = 64, 8, 64, 96
PAIRS = E0 // 2
SLOTS = E0 * CAP
FULL = 8192

H1, DH, RANK, WIN = 16, 128, 16, 64
GH = 4
NG = H1 // GH
SCALE = DH ** -0.5
RMS_EPS = 1e-6
E1, K1, F1, FS = 16, 4, 176, 704
NS = FS // F1
EA = E1 + NS
KW = P + WIN


def constants():
    s = np.arange(P)
    c = {}
    c["ident"] = np.eye(P)
    c["tri"] = (s[:, None] <= s[None, :])
    c["tri_strict"] = (s[:, None] < s[None, :])
    c["iota"] = np.tile(s[None, :], (P, 1))
    c["pid"] = s[:, None]
    c["tile_id"] = np.tile(np.arange(NT)[None, :], (P, 1))
    n = np.arange(HD0)
    f = np.zeros((HD0, HD0))
    f[:, 0] = 0.25
    f[:, 8] = 0.25 * (-1.0) ** n
    for k in range(1, 8):
        f[:, k] = np.sqrt(2 / HD0) * np.cos(2 * np.pi * k * n / HD0)
        f[:, 8 + k] = np.sqrt(2 / HD0) * np.sin(2 * np.pi * k * n / HD0)
    back = f / 4 / np.sqrt(2)
    back[:, 0], back[:, 8] = f[:, 0] / 4, f[:, 8] / 4
    c["fwd"] = np.kron(np.eye(H0), f)
    c["back"] = np.kron(np.eye(H0), back)
    theta = (1.0 / 10000.0 ** (np.arange(DH // 2, dtype=np.float32) / np.float32(DH // 2))).astype(np.float32)
    ang = (np.arange(SEQ, dtype=np.float32)[None, :] * theta[:, None]).astype(np.float64)
    c["cos"] = np.concatenate([np.cos(ang), np.cos(ang)], 0)
    c["sin"] = np.concatenate([-np.sin(ang), np.sin(ang)], 0)
    q, k = s[:, None], np.arange(KW)[None, :] - WIN
    seen = (k <= q) & (k >= q - WIN + 1)
    c["mask_first"] = np.where(seen & (k >= 0), 0.0, -1e30)
    c["mask"] = np.where(seen, 0.0, -1e30)
    return {name: np.ascontiguousarray(a, dtype=np.float32) for name, a in c.items()}


def build(nc, io, dbg):
    ctx = ExitStack()
    with ctx:
        def sb(name, shape, dt=F32):
            return ctx.enter_context(nc.sbuf_tensor(name, shape, dt))

        def sem(name):
            return ctx.enter_context(nc.semaphore(name))

        def dram(name, shape, dt=F32):
            return nc.dram_tensor(name, shape, dt, kind="ExternalOutput" if name in dbg else "Internal").ap()

        xn_d = dram("xn_d", (T, D))
        y0_d = dram("y0_d", (SLOTS, D))
        wqk_d = dram("wqk_d", (NG, P, 2, DC, 512))
        hT_d = dram("hT_d", (NT, P, DC, P))
        xT_d = dram("xT_d", (NT, P, DC, P))

        ident = sb("ident", [P, P])
        tri = sb("tri", [P, P])
        ones = sb("ones", [P, P])
        zrow = sb("zrow", [1, 512])
        tri_bf = sb("tri_bf", [P, P], BF16)
        ones_bf = sb("ones_bf", [P, P], BF16)
        iota = sb("iota", [P, P])
        iota_bf = sb("iota_bf", [P, P], BF16)
        pid = sb("pid", [P, 1])
        tile_id = sb("tile_id", [P, NT])
        x_sb = sb("x_sb", [P, NT, D])
        s_sb = sb("s_sb", [P, NT, D])
        stat6 = sb("stat6", [P, NT, 6])
        st = sb("st", [P, 8, NT])
        rstd, nmr, rms, tmpa, tmpb, var = (st[:, k, :] for k in range(6))
        wqkv0 = sb("wqkv0", [P, DC, 2 * D])
        wo0 = sb("wo0", [P, DC, D])
        rtT = sb("rtT", [P, DC, E0])
        gtT = sb("gtT", [P, DC, E1 + 1])
        norm_w = sb("norm_w", [P, DC])
        wv_sb = sb("wv_sb", [P, DC, H1 * DH])
        wo_sb = sb("wo_sb", [P, H1, D])
        dest = sb("dest", [P, NT, K0], U32)
        w8 = sb("w8", [P, NT, K0])
        e8 = sb("e8", [P, NT, K0])
        pos8 = sb("pos8", [P, NT, K0])
        zsum = sb("zsum", [P, NT])
        rz = sb("rz", [P, NT])
        idx0 = sb("idx0", [P, PAIRS], U32)
        coef = sb("coef", [P, NT, EA])
        ARENA = 98 * 256
        arena = sb("arena", [P, ARENA])

        class Region:
            def __init__(self):
                self.at = 0

            def take(self, parts, *shape, dt=F32):
                n = int(np.prod(shape))
                words = n if dt in (F32, U32, I32) else (n + 1) // 2
                a = arena[0:parts, self.at:self.at + words]
                self.at += words
                assert self.at <= ARENA, self.at
                if dt is not F32:
                    a = a.bitcast(dt)
                if len(shape) == 2:
                    a = a.rearrange("p (a b) -> p a b", a=shape[0])
                if len(shape) == 3:
                    a = a.rearrange("p (a b c) -> p a b c", a=shape[0], b=shape[1])
                if len(shape) == 4:
                    a = a.rearrange("p (a b c d) -> p a b c d", a=shape[0], b=shape[1], c=shape[2])
                return a

        ps = [ctx.enter_context(nc.psum_tensor(f"ps{k}", [P, 512], F32)) for k in range(8)]

        turn = {e: sem(f"turn_{e}") for e in ("pe", "act", "dve", "pool", "sp")}
        stage = sem("stage")
        STAGES = [0]

        def rest(eng, name):
            eng.sem_inc(turn[name], 1)

        def stage_end(eng, k):
            eng.drain().then_inc(stage, 1)
            eng.wait_ge(stage, 5 * (k + 1))

        CR = 2

        def done(eng, s, t, per=1, cr=CR):
            eng.wait_ge(s, (t + 1 + cr) * per)

        def free(eng, s, t, per=1, cr=CR):
            eng.wait_ge(s, (t + 1) * per)

        names = {}

        def loop_sem(name, by, per=1, cr=CR):
            s = sem(name)
            names.setdefault(by, []).append((s, per * cr))
            return s

        class Landed:

            def __init__(self, name, n=1, buffers=2):
                self.s = [loop_sem(f"{name}{u}", "sp", 16 * n, 1) for u in range(buffers)]
                self.n, self.buffers = n, buffers

            def done(self, eng, t, u):
                eng.wait_ge(self.s[u], 16 * self.n // self.buffers * (t - u) + 32 * self.n)

            def free(self, eng, t, u):
                eng.wait_ge(self.s[u], 16 * self.n // self.buffers * (t - u) + 16 * self.n)

        consts_in, w0_in, lora_in, w0_mm, w0_cp = (sem(n) for n in ("consts_in", "w0_in", "lora_in", "w0_mm", "w0_cp"))
        lora_mm, lora_add, lora_scaled, wqk_out = (sem(n) for n in ("lora_mm", "lora_add", "lora_scaled", "wqk_out"))
        x_in, setup, setup2 = sem("x_in"), sem("setup"), sem("setup2")
        var_ready, std_ready, rstd_ready = sem("var_ready"), sem("std_ready"), sem("rstd_ready")
        xn_ready = loop_sem("xn_ready", "act")
        xn_stored = Landed("xn_stored")
        xnT_ps = loop_sem("xnT_ps", "pe")
        xnT_rd = loop_sem("xnT_rd", "act")
        qkv_ps = loop_sem("qkv_ps", "pe")
        qkv_rd = loop_sem("qkv_rd", "act")
        lg_rd = loop_sem("lg_rd", "act")
        sq_ready = loop_sem("sq_ready", "pool")
        ss_ready = loop_sem("ss_ready", "dve")
        top_ready = loop_sem("top_ready", "dve")
        ohe_ready = loop_sem("ohe_ready", "dve")
        pos_ps = loop_sem("pos_ps", "pe")
        pos_rd = loop_sem("pos_rd", "dve")
        exp_done = loop_sem("exp_done", "act")
        oh_ready = loop_sem("oh_ready", "dve")
        tab_mm = loop_sem("tab_mm", "pe")
        zero_bank, table_rd, nrm_sq, nrm_rt = sem("zero_bank"), sem("table_rd"), sem("nrm_sq"), sem("nrm_rt")
        kvn_ready = loop_sem("kvn_ready", "pool")
        cum_ps = loop_sem("cum_ps", "pe")
        prod_done = loop_sem("prod_done", "dve")
        y_ready = loop_sem("y_ready", "dve")
        yT_ps = loop_sem("yT_ps", "pe")
        yT_rd = loop_sem("yT_rd", "act")
        s0_ps = loop_sem("s0_ps", "pe")
        s0_rd = loop_sem("s0_rd", "act")
        ic_ready = loop_sem("ic_ready", "pool", 1, 4)
        xg_in = [sem(f"xg_in{u}") for u in range(4)]
        we_in = Landed("we_in", 3, 4)
        xgT_ps = loop_sem("xgT_ps", "pe", 1, 4)
        xgT_rd = loop_sem("xgT_rd", "act", 1, 4)
        gu_ps = loop_sem("gu_ps", "pe", 1, 4)
        sg_ready = loop_sem("sg_ready", "act", 1, 4)
        hm_ready = loop_sem("hm_ready", "dve", 1, 4)
        y0_ps = loop_sem("y0_ps", "pe", 1, 4)
        y0_rd = loop_sem("y0_rd", "dve", 1, 4)
        y0_out = Landed("y0_out", 1, 4)
        ic4_ready = loop_sem("ic4_ready", "pool")
        yg_in = [sem(f"yg_in{u}") for u in range(2)]
        zeroed = sem("zeroed")
        mix_done = loop_sem("mix_done", "dve")
        g_ready = loop_sem("g_ready", "act")
        x1_done = loop_sem("x1_done", "dve")
        xn2_ready = loop_sem("xn2_ready", "act")
        tr5_ps = loop_sem("tr5_ps", "pe")
        tr5_rd = loop_sem("tr5_rd", "act")
        tr5_out = Landed("tr5_out", 2)
        lg5_ps = loop_sem("lg5_ps", "pe")
        lg5_rd = loop_sem("lg5_rd", "act")
        top5_ready = loop_sem("top5_ready", "dve")
        exp5_done = loop_sem("exp5_done", "act")
        rt5_done = loop_sem("rt5_done", "dve")
        tabs_in, pads = sem("tabs_in"), sem("pads")
        h_in = loop_sem("h_in", "sp", 32, 1)
        proj_mm = loop_sem("proj_mm", "pe", 1, 2)
        swap_rd = loop_sem("swap_rd", "act", 1, 2)
        cos_rd = loop_sem("cos_rd", "dve", 1, 2)
        sin_done = loop_sem("sin_done", "pool", 1, 2)
        rope_done = loop_sem("rope_done", "dve", 1, 2)
        v_ps = loop_sem("v_ps", "pe", 1, 1)
        v_rd = loop_sem("v_rd", "act", 1, 1)
        sc_ps = loop_sem("sc_ps", "pe", 1, 1)
        sm_done = loop_sem("sm_done", "dve", 1, 1)
        pe_done = loop_sem("pe_done", "act", 1, 1)
        pn_done = loop_sem("pn_done", "pool", 1, 1)
        rs_done = loop_sem("rs_done", "dve", 1, 1)
        pt_ps = loop_sem("pt_ps", "pe", 1, 2)
        pt_rd = loop_sem("pt_rd", "act", 1, 2)
        ot_ps = loop_sem("ot_ps", "pe", 1, 1)
        ot_rd = loop_sem("ot_rd", "dve", 1, 1)
        op_ps = loop_sem("op_ps", "pe", 1, 1)
        op_rd = loop_sem("op_rd", "dve", 1, 1)
        w13_in = sem("w13_in")
        xT_in = Landed("xT_in")
        gu1_ps = loop_sem("gu1_ps", "pe")
        sg1_ready = loop_sem("sg1_ready", "act")
        h1_ready = loop_sem("h1_ready", "dve")
        h1T_ps = loop_sem("h1T_ps", "pe")
        h1T_rd = loop_sem("h1T_rd", "act")
        dn_mm = loop_sem("dn_mm", "pe")
        y1_ps = loop_sem("y1_ps", "pe", 1, 1)
        g1_ready = loop_sem("g1_ready", "act")
        fin_ready = loop_sem("fin_ready", "dve")
        out_done = Landed("out_done")

        RW = Region()
        w0_raw = RW.take(P, 3, DC, D)
        fwd = RW.take(P, DC, D)
        back = RW.take(P, DC, D)
        wqk_raw = RW.take(P, 2, DC, H1 * DH)
        lora_a = RW.take(RANK, 3, D)
        lora_b = RW.take(RANK, 3, H1 * DH)
        lora_oa = RW.take(RANK, H1 * DH)
        lora_ob = RW.take(RANK, D)

        R1 = Region()
        qkv = R1.take(P, NT, 2 * D)
        ss = R1.take(P, NT, 2 * H0)
        xn = R1.take(P, 2, D)
        xnT = R1.take(P, 2, DC, P)
        lg = R1.take(P, 2, E0)
        mx = R1.take(P, 2, 8)
        mi = R1.take(P, 2, 8, dt=U32)
        idf = R1.take(P, 2, 8)
        negm = R1.take(P, 2, 1)
        junk = R1.take(P, 2, E0)
        sq = R1.take(P, 2, 2 * D)
        ohe = R1.take(P, 2, K0, E0, dt=BF16)
        posb = R1.take(P, E0)
        base = R1.take(P, E0)
        prod = R1.take(P, K0, E0)
        dstf = R1.take(P, K0)
        badf = R1.take(P, K0)
        dsti = R1.take(P, K0, dt=I32)
        loi = R1.take(P, K0, dt=I32)
        hii = R1.take(P, K0, dt=I32)
        ohlo = R1.take(P, 2, K0, P, dt=BF16)
        ohhi = R1.take(P, K0, PAIRS, dt=BF16)
        tab_rhs = R1.take(P, 2, K0, 2 * PAIRS, dt=BF16)
        tabf = R1.take(P, 2, PAIRS)
        kvn = R1.take(P, TPB, D)
        qn = R1.take(P, 2, D)
        pa = R1.take(P, D)
        pb = R1.take(P, D)
        yy = R1.take(P, 2, D)
        yT = R1.take(P, 2, DC, P)

        R3 = Region()
        ic3 = R3.take(P, 4, 1, dt=U32)
        xg = R3.take(P, 4, D)
        xgT = R3.take(P, 4, DC, P)
        wgu_e = R3.take(P, 4, 2 * 2 * DC, F0)
        wd_e = R3.take(F0, 4, 2, D)
        sg0 = R3.take(F0, 4, P)
        hm0 = R3.take(F0, 4, P)
        y0 = R3.take(P, 4, D)
        ic4 = R3.take(P, 2 * K0, 1, dt=U32)
        yg = R3.take(P, 2, K0, D)
        mix = R3.take(P, 2, D)
        g0 = R3.take(P, 2, D)

        R5 = Region()
        xn2 = R5.take(P, 2, D)
        hh2 = R5.take(P, 2, D)
        tr5 = R5.take(P, 2, 2, DC, P)
        lg5 = R5.take(P, 2, E1 + 1)
        mx5 = R5.take(P, 2, 8)
        mi5 = R5.take(P, 2, 8, dt=U32)
        idf5 = R5.take(P, 2, 8)
        negm5 = R5.take(P, 2, 1)
        ex5 = R5.take(P, 2, E1)
        z5 = R5.take(P, 2, 2)
        oh5 = R5.take(P, K1, E1)
        mk5 = R5.take(P, E1)
        sc5 = R5.take(P, 2, 2)

        R6 = Region()
        cos = R6.take(P, SEQ)
        sin = R6.take(P, SEQ)
        mask0 = R6.take(P, KW)
        mask1 = R6.take(P, KW)
        wqk = R6.take(P, 2, DC, 512)
        hT = R6.take(P, TPB, DC, P)
        qk_c = R6.take(P, 2, SEQ)
        qk_s = R6.take(P, 2, SEQ)
        qr = R6.take(P, 2, SEQ)
        kr = R6.take(P, 2, WIN + SEQ)
        vv = R6.take(P, TPB, GH * DH)
        sm = R6.take(P, TPB, KW)
        mn = R6.take(P, TPB)
        pp = R6.take(P, TPB, 2 * P)
        rs = R6.take(P, TPB)
        ri = R6.take(P, TPB)
        pT = R6.take(P, 2, 2, 2, P)
        oT = R6.take(P, GH, SEQ)

        R7 = Region()
        w13 = R7.take(P, DC, EA, 2 * F1)
        w2a = R7.take(P, EA, D)
        w2b = R7.take(F1 - P, EA, D)
        xT = sb("xT", [P, 2, DC, P])
        sg1 = sb("sg1", [P, 2, F1])
        h1 = sb("h1", [P, 2, F1])
        h1T = sb("h1T", [P, 2, 2 * P])
        g1 = sb("g1", [P, 2, D])
        fin = sb("fin", [P, 2, D])

        block = ctx.enter_context(nc.Block())

        def flat(a):
            return a.rearrange("p a b -> p (a b)")

        def row(a):
            return a.rearrange("p a b -> p (a b)")

        def credit(eng, name):
            for s, n in names.get(name, []):
                eng.sem_inc(s, n)

        def pipelined(front, back, eng):
            front(0, 0)
            with eng.Fori(0, NT // 2 - 1) as i:
                front(2 * i + 1, 1)
                back(2 * i, 0)
                front(2 * i + 2, 0)
                back(2 * i + 1, 1)
            front(NT - 1, 1)
            back(NT - 2, 0)
            back(NT - 1, 1)

        @block.sync
        def _(sp):
            credit(sp, "sp")
            for t, name in ((ident, "ident"), (tri, "tri"), (iota, "iota"), (pid, "pid"), (tile_id, "tile_id")):
                sp.dma_start(t[:, :], io[name]).then_inc(consts_in, 16)
            for k, name in enumerate(("wq0", "wkv0", "wo0T")):
                sp.dma_start(w0_raw[:, k], io[name].rearrange("(c p) n -> p c n", p=P)).then_inc(w0_in, 16)
            sp.dma_start(fwd, io["fwd"].rearrange("(c p) n -> p c n", p=P)).then_inc(w0_in, 16)
            sp.dma_start(back, io["back"].rearrange("(c p) n -> p c n", p=P)).then_inc(w0_in, 16)
            sp.dma_start(x_sb[:, :, :], io["x"].rearrange("(n p) d -> p n d", p=P)).then_inc(x_in, 16)
            sp.dma_start(rtT[:, :, :], io["rtT"].rearrange("(c p) n -> p c n", p=P)).then_inc(x_in, 16)
            sp.dma_start(gtT[:, :, :], io["gtT"].rearrange("(c p) n -> p c n", p=P)).then_inc(x_in, 16)
            sp.dma_start(norm_w[:, :], io["norm_w"]).then_inc(lora_in, 16)
            for j, (wn, an, bn) in enumerate((("wqT", "qA", "qBT"), ("wkT", "kA", "kBT"), ("wvT", "vA", "vBT"))):
                dst = wqk_raw[:, j] if j < 2 else wv_sb[:, :, :]
                sp.dma_start(dst, io[wn].rearrange("(c p) n -> p c n", p=P)).then_inc(lora_in, 16)
                sp.dma_start(lora_a[:, j], io[an]).then_inc(lora_in, 16)
                sp.dma_start(lora_b[:, j], io[bn]).then_inc(lora_in, 16)
            sp.dma_start(wo_sb[:, :, :], io["woT"].rearrange("(h p) n -> p h n", p=P)).then_inc(lora_in, 16)
            sp.dma_start(lora_oa, io["oA"]).then_inc(lora_in, 16)
            sp.dma_start(lora_ob, io["oBT"]).then_inc(lora_in, 16)
            sp.wait_ge(lora_scaled, 24)
            for g in range(NG):
                sp.dma_start(wqk_d[g], wqk_raw[:, :, :, g * 512:(g + 1) * 512]).then_inc(wqk_out, 16)
            sp.wait_ge(wqk_out, 16 * NG)
            stage_end(sp, 0)

            with sp.Fori(0, NT // 2) as i:
                for u in range(2):
                    t = 2 * i + u
                    done(sp, xn_ready, t)
                    sp.dma_start(xn_d[bass.ds(t * P, P), :], xn[:, u]).then_inc(xn_stored.s[u], 16)
            for u in range(2):
                xn_stored.done(sp, NT - 2 + u, u)
            stage_end(sp, 1)
            stage_end(sp, 2)

            with sp.Fori(0, PAIRS // 4) as i:
                for u in range(4):
                    j = 4 * i + u
                    free(sp, y0_ps, j)
                    for g, name in ((0, "w_gate"), (1, "w_up")):
                        sp.dma_start(wgu_e[:, u, 4 * g:4 * g + 4, :],
                                     io[name][bass.ds(2 * j, 2)].rearrange("e (c p) f -> p (e c) f", p=P)).then_inc(we_in.s[u], 16)
                    sp.dma_start(wd_e[:, u], io["w_down"][bass.ds(2 * j, 2)].rearrange("e f d -> f e d")).then_inc(we_in.s[u], 16)
                for u in range(4):
                    j = 4 * i + u
                    done(sp, y0_rd, j, 1, 4)
                    sp.dma_start(y0_d[bass.ds(j * P, P), :], y0[:, u]).then_inc(y0_out.s[u], 16)
            for u in range(4):
                y0_out.done(sp, PAIRS - 4 + u, u)
            stage_end(sp, 3)
            stage_end(sp, 4)

            with sp.Fori(0, NT // 2) as i:
                for u in range(2):
                    t = 2 * i + u
                    done(sp, tr5_rd, t)
                    sp.dma_start(hT_d[bass.ds(t, 1)].rearrange("a p c n -> p (a c) n"), tr5[:, u, 0]).then_inc(tr5_out.s[u], 16)
                    sp.dma_start(xT_d[bass.ds(t, 1)].rearrange("a p c n -> p (a c) n"), tr5[:, u, 1]).then_inc(tr5_out.s[u], 16)
            for u in range(2):
                tr5_out.done(sp, NT - 2 + u, u)
            stage_end(sp, 5)

            for dst, name in ((cos, "cos"), (sin, "sin"), (mask0, "mask_first"), (mask1, "mask")):
                sp.dma_start(dst, io[name]).then_inc(tabs_in, 16)
            with sp.Fori(0, NB) as b:
                with sp.Fori(0, NG) as g:
                    n = NG * b + g
                    sp.wait_ge(proj_mm, 2 + n * 2 * GH)
                    sp.dma_start(wqk, wqk_d[bass.ds(g, 1)].rearrange("a p s c n -> p (a s) c n")).then_inc(h_in, 16)
                    sp.dma_start(hT, hT_d[bass.ds(b * TPB, TPB)].rearrange("n p c t -> p n c t")).then_inc(h_in, 16)
            stage_end(sp, 6)

            sp.dma_start(w13, io["w13T"].rearrange("(c p) e f -> p c e f", p=P)).then_inc(w13_in, 16)
            sp.dma_start(w2a, io["w2T"][:, 0:P, :].rearrange("e f d -> f e d")).then_inc(w13_in, 16)
            sp.dma_start(w2b, io["w2T"][:, P:F1, :].rearrange("e f d -> f e d")).then_inc(w13_in, 16)
            for u in range(2):
                sp.dma_start(xT[:, u], xT_d[u]).then_inc(xT_in.s[u], 16)
            with sp.Fori(0, NT // 2 - 1) as i:
                for u in range(2):
                    t = 2 * i + u
                    done(sp, y1_ps, t, 1, 1)
                    sp.dma_start(xT[:, u], xT_d[bass.ds(t + 2, 1)].rearrange("a p c n -> p (a c) n")).then_inc(xT_in.s[u], 16)
                    done(sp, fin_ready, t)
                    sp.dma_start(io["out"][bass.ds(t * P, P), :], fin[:, u]).then_inc(out_done.s[u], 16)
            for u in range(2):
                t = NT - 2 + u
                done(sp, fin_ready, t)
                sp.dma_start(io["out"][t * P:(t + 1) * P, :], fin[:, u]).then_inc(out_done.s[u], 16)
            for u in range(2):
                out_done.done(sp, NT - 2 + u, u)

        @block.tensor
        def _(pe):
            credit(pe, "pe")
            pe.wait_ge(consts_in, 80)
            pe.wait_ge(w0_in, 80)
            pe.wait_ge(setup, 3)
            for m in range(DC):
                for k, at in ((0, 0), (1, D)):
                    for c in range(DC):
                        pe.matmul(ps[m][:, at:at + D], w0_raw[:, k, c, m * P:(m + 1) * P], fwd[:, c],
                                  start=(c == 0), stop=(c == DC - 1))
                for c in range(DC):
                    last = pe.matmul(ps[2 + m][:, 0:D], back[:, c, m * P:(m + 1) * P], w0_raw[:, 2, c],
                                     start=(c == 0), stop=(c == DC - 1))
            last.then_inc(w0_mm, 1)
            pe.wait_ge(lora_in, 16 * 13)
            n = 0
            for j in range(3):
                for m in range(DC):
                    for q in range(4):
                        if n >= 4:
                            pe.wait_ge(lora_add, n - 3)
                        pe.matmul(ps[4 + n % 4][:, :], lora_a[:, j, m * P:(m + 1) * P], lora_b[:, j, q * 512:(q + 1) * 512],
                                  start=True, stop=True).then_inc(lora_mm, 1)
                        n += 1
            for h in range(0, H1, 2):
                pe.wait_ge(lora_add, n - 3)
                for k in range(2):
                    last = pe.matmul(ps[4 + n % 4][:, k * D:(k + 1) * D], lora_oa[:, (h + k) * P:(h + k + 1) * P], lora_ob,
                                     start=True, stop=True)
                last.then_inc(lora_mm, 1)
                n += 1
            stage_end(pe, 0)

            pe.matmul(ps[6][:, 0:2 * PAIRS], zrow[:, 0:P], zrow[:, 0:2 * PAIRS], start=True, stop=False, skip_group_check=True)

            def front(t, u):
                done(pe, xn_ready, t)
                free(pe, xnT_rd, t)
                for c in range(DC):
                    last = pe.transpose(ps[u][:, c * P:(c + 1) * P], xn[:, u, c * P:(c + 1) * P], ident[:, :])
                last.then_inc(xnT_ps, 1)
                done(pe, xnT_rd, t)
                free(pe, pos_rd, t)
                for c in range(DC):
                    pe.matmul(ps[4 + u][:, 0:E0], xnT[:, u, c], rtT[:, c, :], start=(c == 0), stop=(c == DC - 1))
                for c in range(DC):
                    last = pe.matmul(ps[2 + u][:, :], xnT[:, u, c], wqkv0[:, c, :], start=(c == 0), stop=(c == DC - 1))
                last.then_inc(qkv_ps, 1)

            def back_(t, u):
                done(pe, ohe_ready, t)
                done(pe, lg_rd, t)
                for k in range(K0):
                    pe.matmul(ps[4 + u][:, E0:2 * E0], tri_bf[:, :], ohe[:, u, k], start=(k == 0), stop=(k == K0 - 1))
                for k in range(K0):
                    last = pe.matmul(ps[4 + u][:, 2 * E0:3 * E0], ones_bf[:, :], ohe[:, u, k], start=(k == 0), stop=(k == K0 - 1))
                last.then_inc(pos_ps, 1)
                done(pe, oh_ready, t)
                for k in range(K0):
                    last = pe.matmul(ps[6][:, 0:2 * PAIRS], ohlo[:, u, k], tab_rhs[:, u, k], start=False, stop=False,
                                     skip_group_check=True)
                last.then_inc(tab_mm, 1)

            pipelined(front, back_, pe)
            pe.matmul(ps[6][:, 0:2 * PAIRS], zrow[:, 0:P], zrow[:, 0:2 * PAIRS], start=False, stop=True,
                      skip_group_check=True).then_inc(zero_bank, 1)
            stage_end(pe, 1)

            with pe.Fori(0, NB) as b:
                for tt in range(TPB):
                    t, u = TPB * b + tt, tt % 2
                    done(pe, kvn_ready, t)
                    free(pe, prod_done, t)
                    pe.matmul(ps[u][:, 0:D], tri[:, :], kvn[:, tt], start=True, stop=(tt == 0))
                    for j in range(tt):
                        last = pe.matmul(ps[u][:, 0:D], ones[:, :], kvn[:, j], start=False, stop=(j == tt - 1))
                    pe.drain().then_inc(cum_ps, 1)
                    done(pe, y_ready, t)
                    free(pe, yT_rd, t)
                    for c in range(DC):
                        last = pe.transpose(ps[2 + u][:, c * P:(c + 1) * P], yy[:, u, c * P:(c + 1) * P], ident[:, :])
                    last.then_inc(yT_ps, 1)
                    done(pe, yT_rd, t)
                    free(pe, s0_rd, t)
                    for c in range(DC):
                        last = pe.matmul(ps[4 + u][:, 0:D], yT[:, u, c], wo0[:, c, :], start=(c == 0), stop=(c == DC - 1))
                    last.then_inc(s0_ps, 1)
            stage_end(pe, 2)

            with pe.Fori(0, PAIRS // 4) as i:
                for u in range(4):
                    j, v = 4 * i + u, u % 2
                    pe.wait_ge(xg_in[u], 16 * (i + 1))
                    if u >= 2:
                        done(pe, xgT_rd, j - 2, 1, 4)
                    else:
                        pe.wait_ge(xgT_rd, j + 3)
                    for c in range(DC):
                        last = pe.transpose(ps[v][:, c * P:(c + 1) * P], xg[:, u, c * P:(c + 1) * P], ident[:, :])
                    last.then_inc(xgT_ps, 1)
                    we_in.done(pe, j, u)
                    done(pe, xgT_rd, j, 1, 4)
                    pe.wait_ge(hm_ready, j + 3)
                    for g in range(2):
                        for e in range(2):
                            at = (2 * g + e) * CAP
                            for c in range(DC):
                                last = pe.matmul(ps[2 + v][0:F0, at:at + CAP], wgu_e[:, u, 4 * g + 2 * e + c],
                                                 xgT[:, u, c, e * CAP:(e + 1) * CAP], start=(c == 0), stop=(c == DC - 1))
                    last.then_inc(gu_ps, 1)
                    done(pe, hm_ready, j, 1, 4)
                    pe.wait_ge(y0_rd, j + 3)
                    for e in range(2):
                        last = pe.matmul(ps[4 + v][e * CAP:(e + 1) * CAP, 0:D], hm0[:, u, e * CAP:(e + 1) * CAP],
                                         wd_e[:, u, e], start=True, stop=True)
                    last.then_inc(y0_ps, 1)
            stage_end(pe, 3)
            stage_end(pe, 4)

            def front5(t, u):
                done(pe, xn2_ready, t)
                free(pe, tr5_rd, t)
                for k, a in ((0, hh2), (1, xn2)):
                    for c in range(DC):
                        last = pe.transpose(ps[u][:, (2 * k + c) * P:(2 * k + c + 1) * P], a[:, u, c * P:(c + 1) * P], ident[:, :])
                last.then_inc(tr5_ps, 1)
                done(pe, tr5_rd, t)
                free(pe, lg5_rd, t)
                for c in range(DC):
                    last = pe.matmul(ps[2 + u][:, 0:E1 + 1], tr5[:, u, 1, c], gtT[:, c, :], start=(c == 0), stop=(c == DC - 1))
                last.then_inc(lg5_ps, 1)

            with pe.Fori(0, NT // 2) as i:
                for u in range(2):
                    front5(2 * i + u, u)
            stage_end(pe, 5)

            with pe.Fori(0, NB) as b:
                with pe.Fori(0, NG) as g:
                    n = NG * b + g

                    def project(hh):
                        h = n * GH + hh
                        for s in range(2):
                            pe.wait_ge(swap_rd, 2 * h + s + 1)
                            for c in range(DC):
                                last = pe.matmul(ps[s][:, :], wqk[:, s, c, hh * DH:(hh + 1) * DH], hT[:, :, c, :],
                                                 start=(c == 0), stop=(c == DC - 1))
                            last.then_inc(proj_mm, 1)

                    def values():
                        for q in range(TPB):
                            k = n * TPB + q
                            pe.wait_ge(v_rd, k + 1)
                            if q == 0:
                                pe.wait_ge(op_rd, 2 * n + 1)
                            for c in range(DC):
                                last = pe.matmul(ps[2][:, :], hT[:, q, c, :], wv_sb[:, c, bass.ds(g * 512, 512)],
                                                 start=(c == 0), stop=(c == DC - 1))
                            last.then_inc(v_ps, 1)

                    def scores(hh):
                        h = n * GH + hh
                        pe.wait_ge(rope_done, 2 * h + 4)
                        pe.wait_ge(sm_done, h + 1)
                        for q in range(TPB):
                            last = pe.matmul(ps[3 + q // 2][:, (q % 2) * KW:(q % 2 + 1) * KW], qr[:, hh % 2, q * P:(q + 1) * P],
                                             kr[:, hh % 2, q * P:q * P + KW], start=True, stop=True)
                        last.then_inc(sc_ps, 1)

                    def attend(hh):
                        h = n * GH + hh
                        pe.wait_ge(pn_done, h + 2)
                        for half in range(2):
                            k = 2 * h + half
                            pe.wait_ge(pt_rd, k + 1)
                            for q in range(2):
                                for c in range(2):
                                    last = pe.transpose(ps[5 + half][:, (2 * q + c) * P:(2 * q + c + 1) * P],
                                                        pp[:, 2 * half + q, c * P:(c + 1) * P], ident[:, :])
                            last.then_inc(pt_ps, 1)
                        pe.wait_ge(ot_rd, h + 1)
                        for q in range(TPB):
                            pe.wait_ge(pt_rd, 2 * h + q // 2 + 3)
                            last = pe.matmul(ps[7][:, q * P:(q + 1) * P], vv[:, q, hh * DH:(hh + 1) * DH], pT[:, q // 2, q % 2, 1],
                                             start=True, stop=(q == 0))
                            if q:
                                last = pe.matmul(ps[7][:, q * P:(q + 1) * P], vv[:, q - 1, hh * DH:(hh + 1) * DH],
                                                 pT[:, q // 2, q % 2, 0], start=False, stop=True)
                        last.then_inc(ot_ps, 1)

                    done(pe, h_in, n, 32, 1)
                    project(0)
                    values()
                    pe.wait_ge(v_rd, (n + 1) * TPB + 1)
                    for hh in range(GH):
                        scores(hh)
                        if hh + 1 < GH:
                            project(hh + 1)
                        attend(hh)
                    pe.wait_ge(ot_rd, (n + 1) * GH + 1)
                    for half in range(2):
                        pe.wait_ge(op_rd, 2 * n + half + 1)
                        for q in range(2):
                            for hh in range(GH):
                                last = pe.matmul(ps[2][:, q * D:(q + 1) * D], oT[:, hh, (2 * half + q) * P:(2 * half + q + 1) * P],
                                                 wo_sb[:, bass.ds(g * GH + hh, 1), :].rearrange("p a d -> p (a d)"),
                                                 start=(hh == 0), stop=(hh == GH - 1))
                        last.then_inc(op_ps, 1)
            stage_end(pe, 6)

            pe.wait_ge(w13_in, 48)
            with pe.Fori(0, NT // 2) as i:
                for u in range(2):
                    t = 2 * i + u
                    xT_in.done(pe, t, u)
                    free(pe, fin_ready, t)
                    pe.matmul(ps[6 + u][:, 0:D], zrow[:, 0:P], zrow[:, 0:D], start=True, stop=False, skip_group_check=True)
                    with pe.Fori(0, EA // 2) as j:
                        n = t * EA + 2 * j
                        for v in range(2):
                            e = 2 * j + v
                            free(pe, h1_ready, n + v)
                            for c in range(DC):
                                last = pe.matmul(ps[v][:, 0:2 * F1], xT[:, u, c, :], w13[:, c, bass.ds(e, 1), :].rearrange("p a f -> p (a f)"),
                                                 start=(c == 0), stop=(c == DC - 1))
                            last.then_inc(gu1_ps, 1)
                        for v in range(2):
                            done(pe, h1_ready, n + v)
                            free(pe, h1T_rd, n + v)
                            pe.transpose(ps[2 + v][:, 0:P], h1[:, v, 0:P], ident[:, :])
                            pe.transpose(ps[2 + v][0:F1 - P, P:2 * P], h1[:, v, P:F1], ident[:, :]).then_inc(h1T_ps, 1)
                        for v in range(2):
                            e = 2 * j + v
                            done(pe, h1T_rd, n + v)
                            pe.matmul(ps[6 + u][:, 0:D], h1T[:, v, 0:P], w2a[:, bass.ds(e, 1), :].rearrange("p a d -> p (a d)"),
                                      start=False, stop=False, skip_group_check=True)
                            pe.matmul(ps[6 + u][:, 0:D], h1T[0:F1 - P, v, P:2 * P],
                                      w2b[:, bass.ds(e, 1), :].rearrange("p a d -> p (a d)"),
                                      start=False, stop=False, skip_group_check=True).then_inc(dn_mm, 1)
                    pe.matmul(ps[6 + u][:, 0:D], zrow[:, 0:P], zrow[:, 0:D], start=False, stop=True,
                              skip_group_check=True).then_inc(y1_ps, 1)

        @block.scalar
        def _(act):
            credit(act, "act")
            for n in range(24):
                j, m, q = n // 8, n // 4 % 2, n % 4
                act.wait_ge(lora_add, n + 1)
                a = (wqk_raw[:, j, m] if j < 2 else wv_sb[:, m, :])[:, q * 512:(q + 1) * 512]
                nc.scalar.activation(a, a, ACT.Copy, scale=norm_w[:, m:m + 1]).then_inc(lora_scaled, 1)
            act.wait_ge(var_ready, 1)
            nc.scalar.activation(tmpa, var, ACT.Sqrt).then_inc(std_ready, 1)
            stage_end(act, 0)

            def front(t, u):
                free(act, xnT_ps, t)
                xn_stored.free(act, t, u)
                nc.scalar.activation(xn[:, u], row(x_sb[:, bass.ds(t, 1), :]), ACT.Identity,
                                     bias=nmr[:, bass.ds(t, 1)], scale=rstd[:, bass.ds(t, 1)]).then_inc(xn_ready, 1)
                done(act, xnT_ps, t)
                free(act, qkv_ps, t)
                nc.scalar.activation(flat(xnT[:, u]), ps[u][:, 0:D], ACT.Copy).then_inc(xnT_rd, 1)
                done(act, qkv_ps, t)
                free(act, exp_done, t)
                free(act, oh_ready, t)
                nc.scalar.activation(lg[:, u], ps[4 + u][:, 0:E0], ACT.Copy).then_inc(lg_rd, 1)
                nc.scalar.activation(row(qkv[:, bass.ds(t, 1), :]), ps[2 + u][:, :], ACT.Copy).then_inc(qkv_rd, 1)

            def back_(t, u):
                done(act, top_ready, t)
                nc.scalar.activation(junk[:, u], lg[:, u], ACT.Exp, bias=negm[:, u], accum_out=zsum[:, bass.ds(t, 1)])
                nc.scalar.activation(row(e8[:, bass.ds(t, 1), :]), mx[:, u], ACT.Exp, bias=negm[:, u]).then_inc(exp_done, 1)

            pipelined(front, back_, act)
            done(act, ss_ready, NT - 1)
            nc.scalar.activation(flat(ss), flat(ss), ACT.Sqrt).then_inc(nrm_sq, 1)
            stage_end(act, 1)

            with act.Fori(0, NB) as b:
                for tt in range(TPB):
                    t, u = TPB * b + tt, tt % 2
                    done(act, yT_ps, t)
                    free(act, s0_ps, t)
                    nc.scalar.activation(flat(yT[:, u]), ps[2 + u][:, 0:D], ACT.Copy).then_inc(yT_rd, 1)
                    done(act, s0_ps, t)
                    nc.scalar.activation(row(s_sb[:, bass.ds(t, 1), :]), ps[4 + u][:, 0:D], ACT.Copy).then_inc(s0_rd, 1)
            stage_end(act, 2)

            with act.Fori(0, PAIRS // 4) as i:
                for u in range(4):
                    j, v = 4 * i + u, u % 2
                    done(act, xgT_ps, j, 1, 4)
                    free(act, gu_ps, j)
                    nc.scalar.activation(flat(xgT[:, u]), ps[v][:, 0:D], ACT.Copy).then_inc(xgT_rd, 1)
                    done(act, gu_ps, j, 1, 4)
                    free(act, hm_ready, j)
                    nc.scalar.activation(sg0[:, u], ps[2 + v][0:F0, 0:P], ACT.Silu).then_inc(sg_ready, 1)
            stage_end(act, 3)

            with act.Fori(0, NT // 2) as i:
                for u in range(2):
                    t = 2 * i + u
                    done(act, mix_done, t)
                    free(act, x1_done, t)
                    nc.scalar.activation(g0[:, u], mix[:, u], ACT.Silu).then_inc(g_ready, 1)
            act.wait_ge(var_ready, 2)
            nc.scalar.activation(tmpa, var, ACT.Sqrt).then_inc(std_ready, 1)
            act.wait_ge(var_ready, 3)
            nc.scalar.activation(tmpb, tmpb, ACT.Sqrt).then_inc(std_ready, 1)
            stage_end(act, 4)

            with act.Fori(0, NT // 2) as i:
                for u in range(2):
                    t = 2 * i + u
                    free(act, tr5_ps, t)
                    nc.scalar.activation(xn2[:, u], row(x_sb[:, bass.ds(t, 1), :]), ACT.Identity,
                                         bias=nmr[:, bass.ds(t, 1)], scale=rstd[:, bass.ds(t, 1)])
                    act.drain()
                    nc.scalar.activation(hh2[:, u], xn2[:, u], ACT.Copy, scale=rms[:, bass.ds(t, 1)])
                    nc.scalar.activation(row(s_sb[:, bass.ds(t, 1), :]), xn2[:, u], ACT.Copy).then_inc(xn2_ready, 1)
                    done(act, tr5_ps, t)
                    tr5_out.free(act, t, u)
                    free(act, lg5_ps, t)
                    nc.scalar.activation(tr5[:, u].rearrange("p a b c -> p (a b c)"), ps[u][:, :], ACT.Copy).then_inc(tr5_rd, 1)
                    done(act, lg5_ps, t)
                    free(act, rt5_done, t)
                    nc.scalar.activation(lg5[:, u], ps[2 + u][:, 0:E1 + 1], ACT.Copy).then_inc(lg5_rd, 1)
                    done(act, top5_ready, t)
                    nc.scalar.activation(ex5[:, u], lg5[:, u, 0:E1], ACT.Exp, bias=negm5[:, u], accum_out=z5[:, u, 0:1])
                    nc.scalar.activation(z5[:, u, 1:2], lg5[:, u, E1:E1 + 1], ACT.Exp, scale=-1.0).then_inc(exp5_done, 1)
            stage_end(act, 5)

            with act.Fori(0, NB) as b:
                with act.Fori(0, NG) as g:
                    n = NG * b + g

                    def swap(hh):
                        h = n * GH + hh
                        for s in range(2):
                            k = 2 * h + s
                            act.wait_ge(cos_rd, k + 3)
                            act.wait_ge(rope_done, k + 1)
                            nc.scalar.activation(qk_s[0:64, s], ps[s][64:P, :], ACT.Copy)
                            nc.scalar.activation(qk_s[64:P, s], ps[s][0:64, :], ACT.Copy).then_inc(swap_rd, 1)

                    swap(0)
                    for q in range(TPB):
                        act.wait_ge(v_ps, n * TPB + q + 2)
                        nc.scalar.activation(vv[:, q], ps[2][:, :], ACT.Copy).then_inc(v_rd, 1)
                    for hh in range(GH):
                        h = n * GH + hh
                        act.wait_ge(sm_done, h + 2)
                        act.wait_ge(pt_ps, 2 * h + 2)
                        for q in range(TPB):
                            last = nc.scalar.activation(pp[:, q, P - WIN:2 * P], sm[:, q], ACT.Exp, bias=mn[:, q:q + 1], scale=-1.0,
                                                        accum_out=rs[:, q:q + 1])
                        act.drain().then_inc(pe_done, 1)
                        if hh + 1 < GH:
                            swap(hh + 1)
                        for half in range(2):
                            act.wait_ge(pt_ps, 2 * h + half + 3)
                            act.wait_ge(ot_ps, h + 1)
                            nc.scalar.activation(pT[:, half].rearrange("p a b c -> p (a b c)"), ps[5 + half][:, :], ACT.Copy)\
                                .then_inc(pt_rd, 1)
            stage_end(act, 6)

            with act.Fori(0, NT // 2) as i:
                for u in range(2):
                    t = 2 * i + u
                    with act.Fori(0, EA // 2) as j:
                        n = t * EA + 2 * j
                        for v in range(2):
                            done(act, gu1_ps, n + v)
                            free(act, h1_ready, n + v)
                            nc.scalar.activation(sg1[:, v], ps[v][:, 0:F1], ACT.Silu).then_inc(sg1_ready, 1)
                        for v in range(2):
                            done(act, h1T_ps, n + v)
                            free(act, dn_mm, n + v)
                            nc.scalar.activation(h1T[:, v, 0:P], ps[2 + v][:, 0:P], ACT.Copy)
                            nc.scalar.activation(h1T[0:F1 - P, v, P:2 * P], ps[2 + v][0:F1 - P, P:2 * P], ACT.Copy)
                            act.drain().then_inc(h1T_rd, 1)
                    done(act, y1_ps, t, 1, 1)
                    free(act, fin_ready, t)
                    nc.scalar.activation(g1[:, u], ps[6 + u][:, 0:D], ACT.Silu).then_inc(g1_ready, 1)

        @block.vector
        def _(dve):
            credit(dve, "dve")
            nc.vector.memset(ones[:, :], 1.0).then_inc(setup, 1)
            nc.vector.memset(zrow[:, :], 0.0).then_inc(setup, 1)
            nc.vector.memset(ones_bf[:, :], 1.0).then_inc(setup, 1)
            nc.vector.memset(coef[:, :, :], 0.0)
            dve.wait_ge(w0_mm, 1)
            for m in range(DC):
                nc.vector.tensor_copy(wqkv0[:, m, :], ps[m][:, :])
                nc.vector.tensor_copy(wo0[:, m, :], ps[2 + m][:, 0:D])
            dve.wait_ge(lora_in, 16 * 13)
            for n in range(24):
                j, m, q = n // 8, n // 4 % 2, n % 4
                dve.wait_ge(lora_mm, n + 1)
                a = (wqk_raw[:, j, m] if j < 2 else wv_sb[:, m, :])[:, q * 512:(q + 1) * 512]
                nc.vector.scalar_tensor_tensor(a, ps[4 + n % 4][:, :], 1.0 / RANK, a, ALU.mult, ALU.add).then_inc(lora_add, 1)
            for h in range(0, H1, 2):
                n = 24 + h // 2
                dve.wait_ge(lora_mm, n + 1)
                a = flat(wo_sb[:, h:h + 2, :])
                nc.vector.scalar_tensor_tensor(a, ps[4 + n % 4][:, :], 1.0 / RANK, a, ALU.mult, ALU.add).then_inc(lora_add, 1)
            dve.wait_ge(consts_in, 80)
            nc.vector.tensor_copy(iota_bf[:, :], iota[:, :])
            nc.vector.tensor_tensor(tri_bf[:, :], tri[:, :], ident[:, :], ALU.subtract)
            dve.wait_ge(x_in, 48)

            def statistics(times):
                if times == 1:
                    with dve.Fori(0, NT) as t:
                        nc.vector.bn_stats(row(stat6[:, bass.ds(t, 1), :]), row(x_sb[:, bass.ds(t, 1), :]))
                dve.drain()
                nc.vector.tensor_tensor(tmpa, stat6[:, :, 1], stat6[:, :, 4], ALU.subtract)
                nc.vector.tensor_tensor(nmr, stat6[:, :, 1], stat6[:, :, 4], ALU.add)
                nc.vector.tensor_tensor(var, stat6[:, :, 2], stat6[:, :, 5], ALU.add)
                dve.drain()
                nc.vector.tensor_tensor(tmpa, tmpa, tmpa, ALU.mult)
                nc.vector.tensor_scalar(var, var, 1.0 / D, LN_EPS, ALU.mult, ALU.add)
                dve.drain()
                nc.vector.scalar_tensor_tensor(var, tmpa, 0.25, var, ALU.mult, ALU.add).then_inc(var_ready, 1)
                dve.wait_ge(std_ready, times if times == 1 else 2)
                nc.vector.reciprocal(rstd, tmpa)
                dve.drain()
                nc.vector.scalar_tensor_tensor(nmr, nmr, -0.5, rstd, ALU.mult, ALU.mult)

            statistics(1)
            nc.vector.memset(base, 0.0)
            stage_end(dve, 0)

            def back_(t, u):
                done(dve, lg_rd, t)
                free(dve, exp_done, t)
                rest(dve, "dve")
                nc.vector.max(mx[:, u], lg[:, u])
                dve.drain()
                nc.vector.max_index(mi[:, u], mx[:, u], lg[:, u])
                nc.vector.tensor_scalar(negm[:, u], mx[:, u, 0:1], -1.0, None, ALU.mult).then_inc(top_ready, 1)
                dve.drain()
                nc.vector.tensor_copy(idf[:, u], mi[:, u])
                dve.drain()
                free(dve, pos_ps, t)
                nc.vector.tensor_tensor(ohe[:, u], iota_bf[:, 0:E0].unsqueeze(1).to_broadcast([P, K0, E0]),
                                        idf[:, u].unsqueeze(2).to_broadcast([P, K0, E0]), ALU.is_equal).then_inc(ohe_ready, 1)
                done(dve, sq_ready, t)
                nc.vector.tensor_reduce(row(ss[:, bass.ds(t, 1), :]), sq[:, u].rearrange("p (g d) -> p g d", d=HD0), AX.X, ALU.add)\
                    .then_inc(ss_ready, 1)
                done(dve, pos_ps, t)
                nc.vector.tensor_tensor(posb, ps[4 + u][:, E0:2 * E0], base, ALU.add)
                dve.drain()
                nc.vector.tensor_tensor(base, ps[4 + u][:, 2 * E0:3 * E0], base, ALU.add).then_inc(pos_rd, 1)
                nc.vector.tensor_tensor(prod, ohe[:, u], posb.unsqueeze(1).to_broadcast([P, K0, E0]), ALU.mult)
                dve.drain()
                nc.vector.tensor_reduce(row(pos8[:, bass.ds(t, 1), :]), prod, AX.X, ALU.add)
                dve.drain()
                pos = row(pos8[:, bass.ds(t, 1), :])
                nc.vector.tensor_scalar(badf, pos, float(CAP), float(FULL), ALU.is_ge, ALU.mult)
                nc.vector.scalar_tensor_tensor(dstf, idf[:, u], float(CAP), pos, ALU.mult, ALU.add)
                dve.drain()
                nc.vector.tensor_tensor(dsti, dstf, badf, ALU.add)
                nc.vector.tensor_tensor(row(dest[:, bass.ds(t, 1), :]), dstf, badf, ALU.add)
                dve.drain()
                nc.vector.tensor_scalar(loi, dsti, P - 1, None, ALU.bitwise_and)
                nc.vector.tensor_scalar(hii, dsti, 7, None, ALU.arith_shift_right)
                dve.drain()
                free(dve, tab_mm, t)
                nc.vector.tensor_tensor(ohlo[:, u], iota_bf[:, :].unsqueeze(1).to_broadcast([P, K0, P]),
                                        loi.unsqueeze(2).to_broadcast([P, K0, P]), ALU.is_equal)
                nc.vector.tensor_tensor(ohhi, iota_bf[:, 0:PAIRS].unsqueeze(1).to_broadcast([P, K0, PAIRS]),
                                        hii.unsqueeze(2).to_broadcast([P, K0, PAIRS]), ALU.is_equal)
                dve.drain()
                nc.vector.tensor_scalar(tab_rhs[:, u, :, 0:PAIRS], ohhi, pid[:, 0:1], None, ALU.mult)
                nc.vector.tensor_scalar(tab_rhs[:, u, :, PAIRS:2 * PAIRS], ohhi, tile_id[:, bass.ds(t, 1)], None, ALU.mult)
                dve.drain().then_inc(oh_ready, 1)

            pipelined(lambda t, u: None, back_, dve)
            dve.wait_ge(zero_bank, 1)
            nc.vector.tensor_copy(tabf[:, 0], ps[6][:, 0:PAIRS])
            dve.drain()
            nc.vector.scalar_tensor_tensor(idx0[:, :], ps[6][:, PAIRS:2 * PAIRS], float(P), tabf[:, 0], ALU.mult, ALU.add)
            done(dve, exp_done, NT - 1)
            nc.vector.reciprocal(rz[:, :], zsum[:, :])
            dve.drain()
            nc.vector.tensor_tensor(e8[:, :, :], e8[:, :, :], rz[:, :].unsqueeze(2).to_broadcast([P, NT, K0]), ALU.mult)
            dve.drain()
            nc.vector.tensor_reduce(zsum[:, :], e8[:, :, :], AX.X, ALU.add)
            dve.drain()
            nc.vector.tensor_scalar(zsum[:, :], zsum[:, :], 1e-20, None, ALU.add)
            dve.drain()
            nc.vector.reciprocal(rz[:, :], zsum[:, :])
            nc.vector.tensor_scalar(w8[:, :, :], pos8[:, :, :], float(CAP), None, ALU.is_lt)
            dve.drain()
            nc.vector.tensor_tensor(e8[:, :, :], e8[:, :, :], rz[:, :].unsqueeze(2).to_broadcast([P, NT, K0]), ALU.mult)
            dve.drain()
            nc.vector.tensor_tensor(w8[:, :, :], w8[:, :, :], e8[:, :, :], ALU.mult)
            dve.wait_ge(nrm_sq, 1)
            nc.vector.reciprocal(flat(ss), flat(ss)).then_inc(nrm_rt, 1)
            stage_end(dve, 1)

            with dve.Fori(0, NB) as b:
                for tt in range(TPB):
                    t, u = TPB * b + tt, tt % 2
                    done(dve, kvn_ready, t)
                    done(dve, cum_ps, t)
                    free(dve, yT_ps, t)
                    v4 = lambda a: a.rearrange("p (h c k) -> p h c k", h=H0, c=2)
                    q4, c4, a4, b4, y4 = v4(qn[:, u]), v4(ps[u][:, 0:D]), v4(pa), v4(pb), v4(yy[:, u])
                    nc.vector.tensor_tensor(pa, qn[:, u], ps[u][:, 0:D], ALU.mult)
                    nc.vector.tensor_tensor(b4[:, :, 0], q4[:, :, 1], c4[:, :, 0], ALU.mult)
                    nc.vector.tensor_tensor(b4[:, :, 1], q4[:, :, 0], c4[:, :, 1], ALU.mult).then_inc(prod_done, 1)
                    dve.drain()
                    nc.vector.tensor_tensor(y4[:, :, 0], a4[:, :, 0], a4[:, :, 1], ALU.subtract)
                    nc.vector.tensor_tensor(y4[:, :, 1], b4[:, :, 0], b4[:, :, 1], ALU.add)
                    dve.drain()
                    nc.vector.tensor_copy(y4[:, :, :, 0], a4[:, :, :, 0]).then_inc(y_ready, 1)
            stage_end(dve, 2)

            with dve.Fori(0, PAIRS // 4) as i:
                for u in range(4):
                    j, v = 4 * i + u, u % 2
                    done(dve, sg_ready, j, 1, 4)
                    free(dve, y0_ps, j)
                    nc.vector.tensor_tensor(hm0[:, u], ps[2 + v][0:F0, P:2 * P], sg0[:, u], ALU.mult).then_inc(hm_ready, 1)
                    done(dve, y0_ps, j, 1, 4)
                    y0_out.free(dve, j, u)
                    nc.vector.tensor_copy(y0[:, u], ps[4 + v][:, 0:D]).then_inc(y0_rd, 1)
            nc.vector.memset(yg, 0.0).then_inc(zeroed, 1)
            stage_end(dve, 3)

            with dve.Fori(0, NT // 2) as i:
                for u in range(2):
                    t = 2 * i + u
                    dve.wait_ge(yg_in[u], 16 * K0 * (i + 1))
                    free(dve, g_ready, t)
                    nc.vector.tensor_scalar(mix[:, u], yg[:, u, 0], w8[:, bass.ds(t, 1), 0:1].rearrange("p a b -> p (a b)"), None, ALU.mult)
                    for k in range(1, K0):
                        dve.drain()
                        last = nc.vector.scalar_tensor_tensor(mix[:, u], yg[:, u, k],
                                                              w8[:, bass.ds(t, 1), k:k + 1].rearrange("p a b -> p (a b)"), mix[:, u],
                                                              ALU.mult, ALU.add)
                    last.then_inc(mix_done, 1)
                    done(dve, g_ready, t)
                    nc.vector.tensor_tensor(g0[:, u], g0[:, u], row(s_sb[:, bass.ds(t, 1), :]), ALU.mult)
                    dve.drain()
                    nc.vector.tensor_tensor(row(x_sb[:, bass.ds(t, 1), :]), row(x_sb[:, bass.ds(t, 1), :]), g0[:, u], ALU.add)
                    dve.drain()
                    nc.vector.bn_stats(row(stat6[:, bass.ds(t, 1), :]), row(x_sb[:, bass.ds(t, 1), :])).then_inc(x1_done, 1)
            statistics(2)
            nc.vector.tensor_scalar(tmpb, var, LN_EPS, None, ALU.subtract)
            nc.vector.reciprocal(rms, var)
            dve.drain()
            nc.vector.tensor_tensor(tmpb, tmpb, rms, ALU.mult)
            dve.drain()
            nc.vector.tensor_scalar(tmpb, tmpb, RMS_EPS, None, ALU.add)
            dve.drain().then_inc(var_ready, 1)
            dve.wait_ge(std_ready, 3)
            nc.vector.reciprocal(rms, tmpb)
            stage_end(dve, 4)

            with dve.Fori(0, NT // 2) as i:
                for u in range(2):
                    t = 2 * i + u
                    done(dve, lg5_rd, t)
                    free(dve, exp5_done, t)
                    rest(dve, "dve")
                    nc.vector.max(mx5[:, u], lg5[:, u, 0:E1])
                    dve.drain()
                    nc.vector.max_index(mi5[:, u], mx5[:, u], lg5[:, u, 0:E1])
                    nc.vector.tensor_scalar(negm5[:, u], mx5[:, u, 0:1], -1.0, None, ALU.mult).then_inc(top5_ready, 1)
                    dve.drain()
                    nc.vector.tensor_copy(idf5[:, u], mi5[:, u])
                    dve.drain()
                    nc.vector.tensor_tensor(oh5, iota[:, 0:E1].unsqueeze(1).to_broadcast([P, K1, E1]),
                                            idf5[:, u, 0:K1].unsqueeze(2).to_broadcast([P, K1, E1]), ALU.is_equal)
                    dve.drain()
                    nc.vector.tensor_reduce(mk5, oh5.rearrange("p k e -> p e k"), AX.X, ALU.add)
                    done(dve, exp5_done, t)
                    nc.vector.tensor_scalar(z5[:, u, 1:2], z5[:, u, 1:2], 1.0, None, ALU.add)
                    dve.drain()
                    nc.vector.reciprocal(sc5[:, u], z5[:, u])
                    dve.drain()
                    nc.vector.scalar_tensor_tensor(row(coef[:, bass.ds(t, 1), 0:E1]), ex5[:, u], sc5[:, u, 0:1], mk5, ALU.mult, ALU.mult)
                    nc.vector.tensor_scalar(row(coef[:, bass.ds(t, 1), E1:EA]), ones[:, 0:NS], sc5[:, u, 1:2], None, ALU.mult).then_inc(rt5_done, 1)
            stage_end(dve, 5)

            nc.vector.memset(kr[:, :, 0:WIN], 0.0)
            nc.vector.memset(pp[:, :, 0:P - WIN], 0.0)
            dve.wait_ge(tabs_in, 64)
            with dve.Fori(0, NB) as b:
                with dve.Fori(0, NG) as g:
                    n = NG * b + g

                    def rope(hh):
                        h = n * GH + hh
                        for s in range(2):
                            k = 2 * h + s
                            dve.wait_ge(proj_mm, k + 3)
                            nc.vector.tensor_tensor(qk_c[:, s], ps[s][:, :], cos, ALU.mult).then_inc(cos_rd, 1)
                        for s in range(2):
                            k = 2 * h + s
                            dve.wait_ge(sin_done, k + 3)
                            dst = qr[:, hh % 2] if s == 0 else kr[:, hh % 2, WIN:WIN + SEQ]
                            nc.vector.tensor_tensor(dst, qk_c[:, s], qk_s[:, s], ALU.add).then_inc(rope_done, 1)

                    rope(0)
                    for hh in range(GH):
                        h = n * GH + hh
                        dve.wait_ge(sc_ps, h + 2)
                        dve.wait_ge(pe_done, h + 1)
                        rest(dve, "dve")
                        for q in range(TPB):
                            mask = mask0 if q == 0 else mask1
                            nc.vector.tensor_tensor_reduce(out=sm[:, q], in0=ps[3 + q // 2][:, (q % 2) * KW:(q % 2 + 1) * KW], in1=mask,
                                                           scale=-SCALE, scalar=3e38, op0=ALU.add, op1=ALU.min,
                                                           accum_out=mn[:, q:q + 1])
                        dve.drain().then_inc(sm_done, 1)
                        if hh + 1 < GH:
                            rope(hh + 1)
                        dve.wait_ge(pe_done, h + 2)
                        dve.wait_ge(pn_done, h + 1)
                        nc.vector.reciprocal(ri, rs).then_inc(rs_done, 1)
                        dve.wait_ge(ot_ps, h + 2)
                        nc.vector.tensor_copy(oT[:, hh], ps[7][:, :]).then_inc(ot_rd, 1)
                    for half in range(2):
                        dve.wait_ge(op_ps, 2 * n + half + 2)
                        a = s_sb[:, bass.ds(b * TPB + 2 * half, 2), :]
                        nc.vector.tensor_tensor(a, ps[2][:, :].rearrange("p (a d) -> p a d", a=2), a, ALU.add).then_inc(op_rd, 1)
                        dve.drain()
            stage_end(dve, 6)

            with dve.Fori(0, NT // 2) as i:
                for u in range(2):
                    t = 2 * i + u
                    with dve.Fori(0, EA // 2) as j:
                        n = t * EA + 2 * j
                        for v in range(2):
                            done(dve, sg1_ready, n + v)
                            free(dve, h1T_ps, n + v)
                            nc.vector.scalar_tensor_tensor(h1[:, v], sg1[:, v],
                                                           coef[:, bass.ds(t, 1), bass.ds(2 * j + v, 1)].rearrange("p a b -> p (a b)"),
                                                           ps[v][:, F1:2 * F1], ALU.mult, ALU.mult).then_inc(h1_ready, 1)
                    done(dve, g1_ready, t)
                    out_done.free(dve, t, u)
                    nc.vector.tensor_tensor(g1[:, u], g1[:, u], row(s_sb[:, bass.ds(t, 1), :]), ALU.mult)
                    dve.drain()
                    nc.vector.tensor_tensor(fin[:, u], row(x_sb[:, bass.ds(t, 1), :]), g1[:, u], ALU.add).then_inc(fin_ready, 1)

        @block.gpsimd
        def _(pool):
            credit(pool, "pool")
            stage_end(pool, 0)
            with pool.Fori(0, NT // 2) as i:
                for u in range(2):
                    t = 2 * i + u
                    done(pool, qkv_rd, t)
                    free(pool, ss_ready, t)
                    a = row(qkv[:, bass.ds(t, 1), :])
                    rest(pool, "pool")
                    nc.gpsimd.tensor_tensor(sq[:, u], a, a, ALU.mult).then_inc(sq_ready, 1)
            stage_end(pool, 1)

            pool.wait_ge(nrm_rt, 1)
            with pool.Fori(0, NB) as b:
                for tt in range(TPB):
                    t, u = TPB * b + tt, tt % 2
                    free(pool, cum_ps, t)
                    if tt == 0:
                        pool.wait_ge(cum_ps, t + 2)
                    free(pool, prod_done, t)
                    rest(pool, "pool")
                    for src, dst, off in ((qkv[:, bass.ds(t, 1), 0:D], qn[:, u], 0), (qkv[:, bass.ds(t, 1), D:2 * D], kvn[:, tt], H0)):
                        nc.gpsimd.tensor_tensor(dst.rearrange("p (h k) -> p h k", h=H0), row(src).rearrange("p (h k) -> p h k", h=H0),
                                                row(ss[:, bass.ds(t, 1), off:off + H0]).unsqueeze(2).to_broadcast([P, H0, HD0]), ALU.mult)
                    pool.drain().then_inc(kvn_ready, 1)
            stage_end(pool, 2)

            with pool.Fori(0, PAIRS // 4) as i:
                for u in range(4):
                    j = 4 * i + u
                    free(pool, xgT_ps, j)
                    rest(pool, "pool")
                    nc.gpsimd.tensor_copy(ic3[:, u], idx0[:, bass.ds(j, 1)]).then_inc(ic_ready, 1)
                    done(pool, ic_ready, j, 1, 4)
                    rest(pool, "pool")
                    pool.indirect_dma_start(xg[:, u], None, xn_d, bass.IndirectOffsetOnAxis(ap=ic3[:, u], axis=0)).then_inc(xg_in[u], 16)
            stage_end(pool, 3)

            pool.wait_ge(zeroed, 1)
            with pool.Fori(0, NT // 2) as i:
                for u in range(2):
                    t = 2 * i + u
                    free(pool, mix_done, t)
                    rest(pool, "pool")
                    nc.gpsimd.tensor_copy(ic4[:, u * K0:(u + 1) * K0].rearrange("p a b -> p (a b)"),
                                          row(dest[:, bass.ds(t, 1), :])).then_inc(ic4_ready, 1)
                    done(pool, ic4_ready, t)
                    rest(pool, "pool")
                    for k in range(K0):
                        pool.indirect_dma_start(yg[:, u, k], None, y0_d, bass.IndirectOffsetOnAxis(ap=ic4[:, u * K0 + k], axis=0),
                                                bounds_check=SLOTS - 1, oob_is_err=False).then_inc(yg_in[u], 16)
            stage_end(pool, 4)
            stage_end(pool, 5)

            pool.wait_ge(tabs_in, 64)
            with pool.Fori(0, NB) as b:
                with pool.Fori(0, NG) as g:
                    n = NG * b + g

                    def sine(hh):
                        h = n * GH + hh
                        for s in range(2):
                            pool.wait_ge(swap_rd, 2 * h + s + 3)
                            rest(pool, "pool")
                            nc.gpsimd.tensor_tensor(qk_s[:, s], qk_s[:, s], sin, ALU.mult).then_inc(sin_done, 1)

                    sine(0)
                    for hh in range(GH):
                        h = n * GH + hh
                        if hh + 1 < GH:
                            sine(hh + 1)
                        pool.wait_ge(rs_done, h + 2)
                        rest(pool, "pool")
                        a = pp[:, :, P - WIN:2 * P]
                        nc.gpsimd.tensor_tensor(a, a, ri.unsqueeze(2).to_broadcast([P, TPB, KW]), ALU.mult).then_inc(pn_done, 1)
            stage_end(pool, 6)


DEBUG = ()


def kernel(**inputs):
    import concourse.bacc as bacc
    from concourse.bass_utils import run_bass_kernel_spmd

    a = {k: np.ascontiguousarray(v) for k, v in inputs.items()}
    E, I2, I = E1, 2 * F1, F1
    gu = a["L1_ffn_shared_gate_up_w"]
    shared = gu.reshape(2, NS, F1, D).transpose(1, 0, 2, 3).reshape(NS, 2 * F1, D)
    w13 = np.concatenate([a["L1_ffn_w13"], shared], 0)
    w2 = np.concatenate([a["L1_ffn_w2"].transpose(0, 2, 1), a["L1_ffn_shared_down_w"].T.reshape(NS, F1, D)], 0)
    laid = {
        "x": a["L0_attn_x"].reshape(T, D),
        "wq0": a["L0_attn_W_q"], "wkv0": a["L0_attn_W_kv"], "wo0T": a["L0_attn_W_o"].T,
        "rtT": a["L0_ffn_router_w"].T, "w_gate": a["L0_ffn_w_gate"], "w_up": a["L0_ffn_w_up"], "w_down": a["L0_ffn_w_down"],
        "norm_w": a["L1_attn_norm_w"].reshape(DC, P).T,
        "wqT": a["L1_attn_wq"].T, "wkT": a["L1_attn_wk"].T, "wvT": a["L1_attn_wv"].T, "woT": a["L1_attn_wo"].T,
        "qA": a["L1_attn_qA"], "kA": a["L1_attn_kA"], "vA": a["L1_attn_vA"], "oA": a["L1_attn_oA"],
        "qBT": a["L1_attn_qB"].T, "kBT": a["L1_attn_kB"].T, "vBT": a["L1_attn_vB"].T, "oBT": a["L1_attn_oB"].T,
        "gtT": np.concatenate([a["L1_ffn_gate_w"], a["L1_ffn_sgate_w"]], 0).T,
        "w13T": w13.transpose(2, 0, 1), "w2T": w2,
    }
    laid.update(constants())
    laid = {k: np.ascontiguousarray(v) for k, v in laid.items()}
    nc = bacc.Bacc("TRN2", target_bir_lowering=False, num_devices=1)
    io = {k: nc.dram_tensor(f"in_{k}", v.shape, F32, kind="ExternalInput").ap() for k, v in laid.items()}
    io["out"] = nc.dram_tensor("out", (T, D), F32, kind="ExternalOutput").ap()
    build(nc, io, DEBUG)
    r = run_bass_kernel_spmd(nc, [{f"in_{k}": v for k, v in laid.items()}], core_ids=[0])
    return r.results[0]["out"].reshape(NB, SEQ, D)
```

```python
from contextlib import ExitStack

import concourse.bass as bass
import numpy as np
from concourse import mybir

F32 = mybir.dt.float32
BF16 = mybir.dt.bfloat16
U32 = mybir.dt.uint32
I32 = mybir.dt.int32
ALU = mybir.AluOpType
ACT = mybir.ActivationFunctionType
AX = mybir.AxisListType

P = 128
T = 2048
NB, SEQ, D = 4, 512, 256
NT = T // P
TPB = SEQ // P
DC = D // P
LN_EPS = 1e-5

H0, HD0 = 16, 16
E0, K0, CAP, F0 = 64, 8, 64, 96
PAIRS = E0 // 2
SLOTS = E0 * CAP
FULL = 8192

H1, DH, RANK, WIN = 16, 128, 16, 64
GH = 4
NG = H1 // GH
SCALE = DH ** -0.5
RMS_EPS = 1e-6
E1, K1, F1, FS = 16, 4, 176, 704
NS = FS // F1
EA = E1 + NS
XT = T * K1 // P + E1
XSLOTS = XT * P
KW = P + WIN


def constants():
    s = np.arange(P)
    c = {}
    c["ident"] = np.eye(P)
    c["tri"] = (s[:, None] <= s[None, :])
    c["tri_strict"] = (s[:, None] < s[None, :])
    c["iota"] = np.tile(s[None, :], (P, 1))
    c["pid"] = s[:, None]
    c["tile_id"] = np.tile(np.arange(NT)[None, :], (P, 1))
    n = np.arange(HD0)
    f = np.zeros((HD0, HD0))
    f[:, 0] = 0.25
    f[:, 8] = 0.25 * (-1.0) ** n
    for k in range(1, 8):
        f[:, k] = np.sqrt(2 / HD0) * np.cos(2 * np.pi * k * n / HD0)
        f[:, 8 + k] = np.sqrt(2 / HD0) * np.sin(2 * np.pi * k * n / HD0)
    back = f / 4 / np.sqrt(2)
    back[:, 0], back[:, 8] = f[:, 0] / 4, f[:, 8] / 4
    c["fwd"] = np.kron(np.eye(H0), f)
    c["back"] = np.kron(np.eye(H0), back)
    theta = (1.0 / 10000.0 ** (np.arange(DH // 2, dtype=np.float32) / np.float32(DH // 2))).astype(np.float32)
    ang = (np.arange(SEQ, dtype=np.float32)[None, :] * theta[:, None]).astype(np.float64)
    c["cos"] = np.concatenate([np.cos(ang), np.cos(ang)], 0)
    c["sin"] = np.concatenate([-np.sin(ang), np.sin(ang)], 0)
    q, k = s[:, None], np.arange(KW)[None, :] - WIN
    seen = (k <= q) & (k >= q - WIN + 1)
    c["mask_first"] = np.where(seen & (k >= 0), 0.0, -1e30)
    c["mask"] = np.where(seen, 0.0, -1e30)
    return {name: np.ascontiguousarray(a, dtype=np.float32) for name, a in c.items()}


def build(nc, io, dbg):
    ctx = ExitStack()
    with ctx:
        def sb(name, shape, dt=F32):
            return ctx.enter_context(nc.sbuf_tensor(name, shape, dt))

        def sem(name):
            return ctx.enter_context(nc.semaphore(name))

        def dram(name, shape, dt=F32):
            return nc.dram_tensor(name, shape, dt, kind="ExternalOutput" if name in dbg else "Internal").ap()

        xn_d = dram("xn_d", (T, D))
        y0_d = dram("y0_d", (SLOTS, D))
        wqk_d = dram("wqk_d", (NG, P, 2, DC, 512))
        xn2_d = dram("xn2_d", (T, D))
        y1_d = dram("y1_d", (XSLOTS, D))
        hT_d = dram("hT_d", (NT, P, DC, P))
        xT_d = dram("xT_d", (NT, P, DC, P))

        ident = sb("ident", [P, P])
        tri = sb("tri", [P, P])
        ones = sb("ones", [P, P])
        zrow = sb("zrow", [1, 512])
        tri_bf = sb("tri_bf", [P, P], BF16)
        ones_bf = sb("ones_bf", [P, P], BF16)
        iota = sb("iota", [P, P])
        iota_bf = sb("iota_bf", [P, P], BF16)
        pid = sb("pid", [P, 1])
        tile_id = sb("tile_id", [P, NT])
        x_sb = sb("x_sb", [P, NT, D])
        s_sb = sb("s_sb", [P, NT, D])
        stat6 = sb("stat6", [P, NT, 6])
        st = sb("st", [P, 8, NT])
        rstd, nmr, rms, tmpa, tmpb, var = (st[:, k, :] for k in range(6))
        wqkv0 = sb("wqkv0", [P, DC, 2 * D])
        wo0 = sb("wo0", [P, DC, D])
        rtT = sb("rtT", [P, DC, E0])
        gtT = sb("gtT", [P, DC, E1 + 1])
        norm_w = sb("norm_w", [P, DC])
        wv_sb = sb("wv_sb", [P, DC, H1 * DH])
        wo_sb = sb("wo_sb", [P, H1, D])
        dest = sb("dest", [P, NT, K0], U32)
        w8 = sb("w8", [P, NT, K0])
        e8 = sb("e8", [P, NT, K0])
        pos8 = sb("pos8", [P, NT, K0])
        zsum = sb("zsum", [P, NT])
        rz = sb("rz", [P, NT])
        idx0 = sb("idx0", [P, PAIRS], U32)
        dest1 = sb("dest1", [P, NT, K1], U32)
        w4 = sb("w4", [P, NT, K1])
        gate1 = sb("gate1", [P, NT])
        idx1 = sb("idx1", [P, XT], U32)
        etab = sb("etab", [1, XT], I32)
        ARENA = 98 * 256
        arena = sb("arena", [P, ARENA])

        class Region:
            def __init__(self):
                self.at = 0

            def take(self, parts, *shape, dt=F32):
                n = int(np.prod(shape))
                words = n if dt in (F32, U32, I32) else (n + 1) // 2
                a = arena[0:parts, self.at:self.at + words]
                self.at += words
                assert self.at <= ARENA, self.at
                if dt is not F32:
                    a = a.bitcast(dt)
                if len(shape) == 2:
                    a = a.rearrange("p (a b) -> p a b", a=shape[0])
                if len(shape) == 3:
                    a = a.rearrange("p (a b c) -> p a b c", a=shape[0], b=shape[1])
                if len(shape) == 4:
                    a = a.rearrange("p (a b c d) -> p a b c d", a=shape[0], b=shape[1], c=shape[2])
                return a

        ps = [ctx.enter_context(nc.psum_tensor(f"ps{k}", [P, 512], F32)) for k in range(8)]

        turn = {e: sem(f"turn_{e}") for e in ("pe", "act", "dve", "pool", "sp")}
        stage = sem("stage")
        STAGES = [0]

        def rest(eng, name):
            eng.sem_inc(turn[name], 1)

        def stage_end(eng, k):
            eng.drain().then_inc(stage, 1)
            eng.wait_ge(stage, 5 * (k + 1))

        CR = 2

        def done(eng, s, t, per=1, cr=CR):
            eng.wait_ge(s, (t + 1 + cr) * per)

        def free(eng, s, t, per=1, cr=CR):
            eng.wait_ge(s, (t + 1) * per)

        AHEAD = 4

        def upto(eng, s, k):
            eng.wait_ge(s, k + 1 + AHEAD)

        names = {}

        def loop_sem(name, by, per=1, cr=CR):
            s = sem(name)
            names.setdefault(by, []).append((s, per * cr))
            return s

        class Landed:

            def __init__(self, name, n=1, buffers=2):
                self.s = [loop_sem(f"{name}{u}", "sp", 16 * n, 1) for u in range(buffers)]
                self.n, self.buffers = n, buffers

            def done(self, eng, t, u):
                eng.wait_ge(self.s[u], 16 * self.n // self.buffers * (t - u) + 32 * self.n)

            def free(self, eng, t, u):
                eng.wait_ge(self.s[u], 16 * self.n // self.buffers * (t - u) + 16 * self.n)

        consts_in, w0_in, lora_in, w0_mm, w0_cp = (sem(n) for n in ("consts_in", "w0_in", "lora_in", "w0_mm", "w0_cp"))
        lora_mm, lora_add, lora_scaled, wqk_out = (sem(n) for n in ("lora_mm", "lora_add", "lora_scaled", "wqk_out"))
        x_in, setup, setup2 = sem("x_in"), sem("setup"), sem("setup2")
        var_ready, std_ready, rstd_ready = sem("var_ready"), sem("std_ready"), sem("rstd_ready")
        xn_ready = loop_sem("xn_ready", "act")
        xn_stored = Landed("xn_stored")
        xnT_ps = loop_sem("xnT_ps", "pe")
        xnT_rd = loop_sem("xnT_rd", "act")
        qkv_ps = loop_sem("qkv_ps", "pe")
        qkv_rd = loop_sem("qkv_rd", "act")
        lg_rd = loop_sem("lg_rd", "act")
        sq_ready = loop_sem("sq_ready", "pool")
        ss_ready = loop_sem("ss_ready", "dve")
        top_ready = loop_sem("top_ready", "dve")
        ohe_ready = loop_sem("ohe_ready", "dve")
        pos_ps = loop_sem("pos_ps", "pe")
        pos_rd = loop_sem("pos_rd", "dve")
        exp_done = loop_sem("exp_done", "act")
        oh_ready = loop_sem("oh_ready", "dve")
        tab_mm = loop_sem("tab_mm", "pe")
        zero_bank, table_rd, nrm_sq, nrm_rt = sem("zero_bank"), sem("table_rd"), sem("nrm_sq"), sem("nrm_rt")
        kvn_ready = loop_sem("kvn_ready", "pool")
        cum_ps = loop_sem("cum_ps", "pe")
        prod_done = loop_sem("prod_done", "dve")
        y_ready = loop_sem("y_ready", "dve")
        yT_ps = loop_sem("yT_ps", "pe")
        yT_rd = loop_sem("yT_rd", "act")
        s0_ps = loop_sem("s0_ps", "pe")
        s0_rd = loop_sem("s0_rd", "act")
        ic_ready = loop_sem("ic_ready", "pool", 1, 4)
        xg_in = [sem(f"xg_in{u}") for u in range(4)]
        we_in = Landed("we_in", 3, 4)
        xgT_ps = loop_sem("xgT_ps", "pe", 1, 4)
        xgT_rd = loop_sem("xgT_rd", "act", 1, 4)
        gu_ps = loop_sem("gu_ps", "pe", 1, 4)
        sg_ready = loop_sem("sg_ready", "act", 1, 4)
        hm_ready = loop_sem("hm_ready", "dve", 1, 4)
        y0_ps = loop_sem("y0_ps", "pe", 1, 4)
        y0_rd = loop_sem("y0_rd", "dve", 1, 4)
        y0_out = Landed("y0_out", 1, 4)
        ic4_ready = loop_sem("ic4_ready", "pool")
        yg_in = [sem(f"yg_in{u}") for u in range(2)]
        zeroed = sem("zeroed")
        mix_done = loop_sem("mix_done", "dve")
        g_ready = loop_sem("g_ready", "act")
        x1_done = loop_sem("x1_done", "dve")
        xn2_ready = loop_sem("xn2_ready", "act")
        xn2_kept = loop_sem("xn2_kept", "dve")
        xn2_out = Landed("xn2_out")
        tr5_ps = loop_sem("tr5_ps", "pe")
        tr5_rd = loop_sem("tr5_rd", "act")
        tr5_out = Landed("tr5_out", 2)
        lg5_ps = loop_sem("lg5_ps", "pe")
        lg5_rd = loop_sem("lg5_rd", "dve")
        chosen, counted, ranked, exp5_in, exp5_done, table_in, table_mm = (
            sem(n) for n in ("chosen", "counted", "ranked", "exp5_in", "exp5_done", "table_in", "table_mm"))
        tabs_in = sem("tabs_in")
        h_in = Landed("h_in", 2)
        proj_mm = loop_sem("proj_mm", "pe", 1, AHEAD)
        swap_rd = loop_sem("swap_rd", "act", 1, AHEAD)
        cos_rd = loop_sem("cos_rd", "dve", 1, AHEAD)
        sin_done = loop_sem("sin_done", "pool", 1, AHEAD)
        rope_done = loop_sem("rope_done", "dve", 1, AHEAD)
        v_ps = loop_sem("v_ps", "pe", 1, AHEAD)
        v_rd = loop_sem("v_rd", "act", 1, AHEAD)
        sc_ps = loop_sem("sc_ps", "pe", 1, AHEAD)
        sm_done = loop_sem("sm_done", "dve", 1, AHEAD)
        pe_done = loop_sem("pe_done", "act", 1, AHEAD)
        pn_done = loop_sem("pn_done", "pool", 1, AHEAD)
        rs_done = loop_sem("rs_done", "dve", 1, AHEAD)
        pt_ps = loop_sem("pt_ps", "pe", 1, AHEAD)
        pt_rd = loop_sem("pt_rd", "dve", 1, AHEAD)
        ot_ps = loop_sem("ot_ps", "pe", 1, AHEAD)
        ot_rd = loop_sem("ot_rd", "dve", 1, AHEAD)
        op_ps = loop_sem("op_ps", "pe", 1, AHEAD)
        op_rd = loop_sem("op_rd", "dve", 1, AHEAD)
        w13_in = sem("w13_in")
        ic7_ready = loop_sem("ic7_ready", "pool", 1, AHEAD)
        xs_in = [sem(f"xs_in{u}") for u in range(4)]
        xsT_ps = loop_sem("xsT_ps", "pe", 1, AHEAD)
        xsT_rd = loop_sem("xsT_rd", "act", 1, AHEAD)
        gu1_ps = loop_sem("gu1_ps", "pe", 1, AHEAD)
        sg1_ready = loop_sem("sg1_ready", "act", 1, AHEAD)
        h1_ready = loop_sem("h1_ready", "dve", 1, AHEAD)
        h1T_ps = loop_sem("h1T_ps", "pe", 1, AHEAD)
        h1T_rd = loop_sem("h1T_rd", "act", 1, AHEAD)
        y1_ps = loop_sem("y1_ps", "pe", 1, AHEAD)
        y1_rd = loop_sem("y1_rd", "dve", 1, AHEAD)
        y1_out = Landed("y1_out", 1, 4)
        y1_kept = sem("y1_kept")
        xT_in = Landed("xT_in", 1, 4)
        xT_used = loop_sem("xT_used", "pe", 1, AHEAD)
        gus_ps = loop_sem("gus_ps", "pe", 1, AHEAD)
        sgs_ready = loop_sem("sgs_ready", "act", 1, AHEAD)
        hs_ready = loop_sem("hs_ready", "dve", 1, AHEAD)
        hsT_ps = loop_sem("hsT_ps", "pe", 1, AHEAD)
        hsT_rd = loop_sem("hsT_rd", "act", 1, AHEAD)
        ys_ps = loop_sem("ys_ps", "pe", 1, AHEAD)
        ic8_ready = loop_sem("ic8_ready", "pool")
        yr_in = [sem(f"yr_in{u}") for u in range(2)]
        sum_done = loop_sem("sum_done", "dve")
        g1_ready = loop_sem("g1_ready", "act")
        fin_ready = loop_sem("fin_ready", "dve")
        out_done = Landed("out_done")

        RW = Region()
        w0_raw = RW.take(P, 3, DC, D)
        fwd = RW.take(P, DC, D)
        back = RW.take(P, DC, D)
        wqk_raw = RW.take(P, 2, DC, H1 * DH)
        lora_a = RW.take(RANK, 3, D)
        lora_b = RW.take(RANK, 3, H1 * DH)
        lora_oa = RW.take(RANK, H1 * DH)
        lora_ob = RW.take(RANK, D)

        R1 = Region()
        qkv = R1.take(P, NT, 2 * D)
        ss = R1.take(P, NT, 2 * H0)
        xn = R1.take(P, 2, D)
        xnT = R1.take(P, 2, DC, P)
        lg = R1.take(P, 2, E0)
        mx = R1.take(P, 2, 8)
        mi = R1.take(P, 2, 8, dt=U32)
        idf = R1.take(P, 2, 8)
        negm = R1.take(P, 2, 1)
        junk = R1.take(P, 2, E0)
        sq = R1.take(P, 2, 2 * D)
        ohe = R1.take(P, 2, K0, E0, dt=BF16)
        posb = R1.take(P, E0)
        base = R1.take(P, E0)
        prod = R1.take(P, K0, E0)
        dstf = R1.take(P, K0)
        badf = R1.take(P, K0)
        dsti = R1.take(P, K0, dt=I32)
        loi = R1.take(P, K0, dt=I32)
        hii = R1.take(P, K0, dt=I32)
        ohlo = R1.take(P, 2, K0, P, dt=BF16)
        ohhi = R1.take(P, K0, PAIRS, dt=BF16)
        tab_rhs = R1.take(P, 2, K0, 2 * PAIRS, dt=BF16)
        tabf = R1.take(P, 2, PAIRS)
        kvn = R1.take(P, TPB, D)
        qn = R1.take(P, 2, D)
        pa = R1.take(P, D)
        pb = R1.take(P, D)
        yy = R1.take(P, 2, D)
        yT = R1.take(P, 2, DC, P)

        R3 = Region()
        ic3 = R3.take(P, 4, 1, dt=U32)
        xg = R3.take(P, 4, D)
        xgT = R3.take(P, 4, DC, P)
        wgu_e = R3.take(P, 4, 2 * 2 * DC, F0)
        wd_e = R3.take(F0, 4, 2, D)
        sg0 = R3.take(F0, 4, P)
        hm0 = R3.take(F0, 4, P)
        y0 = R3.take(P, 4, D)
        ic4 = R3.take(P, 2 * K0, 1, dt=U32)
        yg = R3.take(P, 2, K0, D)
        mix = R3.take(P, 2, D)
        g0 = R3.take(P, 2, D)

        R5 = Region()
        xn2 = R5.take(P, 2, D)
        hh2 = R5.take(P, 2, D)
        tr5 = R5.take(P, 2, 2, DC, P)
        lg5 = R5.take(P, 2, E1 + 1)
        mx5 = R5.take(P, 2, 8)
        mi5 = R5.take(P, 2, 8, dt=U32)
        lgA = R5.take(P, NT, E1 + 1)
        mxA = R5.take(P, NT, K1)
        idA = R5.take(P, NT, K1)
        exA = R5.take(P, NT, E1)
        zA = R5.take(P, NT)
        sgA = R5.take(P, NT)
        ohA = R5.take(P, NT, K1, E1, dt=BF16)
        mkA = R5.take(P, NT, E1, dt=BF16)
        cnt = [R5.take(P, NT, E1) for _ in range(3)]
        rank = R5.take(P, NT, E1)
        ntl_i = R5.take(P, E1, dt=I32)
        ntl = [R5.take(P, E1) for _ in range(3)]
        prodA = R5.take(P, NT, K1, E1)
        dstA = R5.take(P, NT * K1)
        tileA = R5.take(P, NT * K1)
        dstI = R5.take(P, NT * K1, dt=I32)
        loA = R5.take(P, NT * K1, dt=I32)
        hiA = R5.take(P, NT * K1, dt=I32)
        ohloA = R5.take(P, NT * K1, P, dt=BF16)
        ohhiA = R5.take(P, NT * K1, XT, dt=BF16)
        tab5 = R5.take(P, NT * K1, 2 * XT, dt=BF16)
        tab5f = R5.take(P, XT)
        etmp = R5.take(1, XT, E1)
        etf = R5.take(1, XT)

        R6 = Region()
        cos = R6.take(P, SEQ)
        sin = R6.take(P, SEQ)
        mask0 = R6.take(P, KW)
        mask1 = R6.take(P, KW)
        wqk = [R6.take(P, 2, DC, 512) for _ in range(2)]
        hT = [R6.take(P, TPB, DC, P) for _ in range(2)]
        qk_c = R6.take(P, 2, SEQ)
        qk_s = R6.take(P, 2, SEQ)
        qr = R6.take(P, 2, SEQ)
        kr = R6.take(P, 2, WIN + SEQ)
        vv = [R6.take(P, TPB, GH * DH) for _ in range(2)]
        sm = R6.take(P, TPB, KW)
        mn = R6.take(P, TPB)
        pp = [R6.take(P, TPB, 2 * P) for _ in range(2)]
        rs = R6.take(P, TPB)
        ri = R6.take(P, TPB)
        pT = R6.take(P, 2, 2, 2, P)
        oT = [R6.take(P, GH, SEQ) for _ in range(2)]

        R7 = Region()
        w13 = R7.take(P, DC, EA, 2 * F1)
        w2a = R7.take(P, EA, D)
        w2b = R7.take(F1 - P, EA, D)
        wv_flat = wv_sb[:, :, :].rearrange("p c n -> p (c n)")
        wo_flat = wo_sb[:, :, :].rearrange("p h n -> p (h n)")
        xs = wv_flat[:, 0:4 * D].rearrange("p (u d) -> p u d", u=4)
        y1s = wv_flat[:, 4 * D:8 * D].rearrange("p (u d) -> p u d", u=4)
        yr = wv_flat[:, 8 * D:16 * D].rearrange("p (u k d) -> p u k d", u=2, k=K1)
        xsT = wo_flat[:, 0:4 * D].rearrange("p (u c n) -> p u c n", u=4, c=DC)
        mix1 = wo_flat[:, 4 * D:6 * D].rearrange("p (u d) -> p u d", u=2)
        h1T = wo_flat[:, 8 * D:10 * D].rearrange("p (u n) -> p u n", u=2)
        g1 = wo_flat[:, 10 * D:12 * D].rearrange("p (u d) -> p u d", u=2)
        fin = wo_flat[:, 6 * D:8 * D].rearrange("p (u d) -> p u d", u=2)
        xT = wo_flat[:, 12 * D:16 * D].rearrange("p (u c n) -> p u c n", u=4, c=DC)
        ic7 = sb("ic7", [P, 4], U32)
        ic8 = sb("ic8", [P, 2, K1], U32)
        sg1 = sb("sg1", [P, 2, F1])
        h1 = sb("h1", [P, 2, F1])

        block = ctx.enter_context(nc.Block())

        NPAIR = NB * NG // 2

        def by_pairs(eng, body):
            with eng.Fori(0, NPAIR - 1) as i:
                body(i, False)
            body(NPAIR - 1, True)

        def over_tiles(eng, body):
            body(0, 0, first=True)
            with eng.Fori(0, NT // 2 - 1) as i:
                body(2 * i + 1, 1)
                body(2 * i + 2, 0)
            body(NT - 1, 1, last=True)

        def flat(a):
            return a.rearrange("p a b -> p (a b)")

        def row(a):
            return a.rearrange("p a b -> p (a b)")

        def credit(eng, name):
            for s, n in names.get(name, []):
                eng.sem_inc(s, n)

        def pipelined(front, back, eng):
            front(0, 0)
            with eng.Fori(0, NT // 2 - 1) as i:
                front(2 * i + 1, 1)
                back(2 * i, 0)
                front(2 * i + 2, 0)
                back(2 * i + 1, 1)
            front(NT - 1, 1)
            back(NT - 2, 0)
            back(NT - 1, 1)

        @block.sync
        def _(sp):
            credit(sp, "sp")
            for t, name in ((ident, "ident"), (tri, "tri"), (iota, "iota"), (pid, "pid"), (tile_id, "tile_id")):
                sp.dma_start(t[:, :], io[name]).then_inc(consts_in, 16)
            for k, name in enumerate(("wq0", "wkv0", "wo0T")):
                sp.dma_start(w0_raw[:, k], io[name].rearrange("(c p) n -> p c n", p=P)).then_inc(w0_in, 16)
            sp.dma_start(fwd, io["fwd"].rearrange("(c p) n -> p c n", p=P)).then_inc(w0_in, 16)
            sp.dma_start(back, io["back"].rearrange("(c p) n -> p c n", p=P)).then_inc(w0_in, 16)
            sp.dma_start(x_sb[:, :, :], io["x"].rearrange("(n p) d -> p n d", p=P)).then_inc(x_in, 16)
            sp.dma_start(rtT[:, :, :], io["rtT"].rearrange("(c p) n -> p c n", p=P)).then_inc(x_in, 16)
            sp.dma_start(gtT[:, :, :], io["gtT"].rearrange("(c p) n -> p c n", p=P)).then_inc(x_in, 16)
            sp.dma_start(norm_w[:, :], io["norm_w"]).then_inc(lora_in, 16)
            for j, (wn, an, bn) in enumerate((("wqT", "qA", "qBT"), ("wkT", "kA", "kBT"), ("wvT", "vA", "vBT"))):
                dst = wqk_raw[:, j] if j < 2 else wv_sb[:, :, :]
                sp.dma_start(dst, io[wn].rearrange("(c p) n -> p c n", p=P)).then_inc(lora_in, 16)
                sp.dma_start(lora_a[:, j], io[an]).then_inc(lora_in, 16)
                sp.dma_start(lora_b[:, j], io[bn]).then_inc(lora_in, 16)
            sp.dma_start(wo_sb[:, :, :], io["woT"].rearrange("(h p) n -> p h n", p=P)).then_inc(lora_in, 16)
            sp.dma_start(lora_oa, io["oA"]).then_inc(lora_in, 16)
            sp.dma_start(lora_ob, io["oBT"]).then_inc(lora_in, 16)
            sp.wait_ge(lora_scaled, 24)
            for g in range(NG):
                sp.dma_start(wqk_d[g], wqk_raw[:, :, :, g * 512:(g + 1) * 512]).then_inc(wqk_out, 16)
            sp.wait_ge(wqk_out, 16 * NG)
            stage_end(sp, 0)

            with sp.Fori(0, NT // 2) as i:
                for u in range(2):
                    t = 2 * i + u
                    done(sp, xn_ready, t)
                    sp.dma_start(xn_d[bass.ds(t * P, P), :], xn[:, u]).then_inc(xn_stored.s[u], 16)
            for u in range(2):
                xn_stored.done(sp, NT - 2 + u, u)
            stage_end(sp, 1)
            stage_end(sp, 2)

            with sp.Fori(0, PAIRS // 4) as i:
                for u in range(4):
                    j = 4 * i + u
                    free(sp, y0_ps, j)
                    for g, name in ((0, "w_gate"), (1, "w_up")):
                        sp.dma_start(wgu_e[:, u, 4 * g:4 * g + 4, :],
                                     io[name][bass.ds(2 * j, 2)].rearrange("e (c p) f -> p (e c) f", p=P)).then_inc(we_in.s[u], 16)
                    sp.dma_start(wd_e[:, u], io["w_down"][bass.ds(2 * j, 2)].rearrange("e f d -> f e d")).then_inc(we_in.s[u], 16)
                for u in range(4):
                    j = 4 * i + u
                    done(sp, y0_rd, j, 1, 4)
                    sp.dma_start(y0_d[bass.ds(j * P, P), :], y0[:, u]).then_inc(y0_out.s[u], 16)
            for u in range(4):
                y0_out.done(sp, PAIRS - 4 + u, u)
            stage_end(sp, 3)
            stage_end(sp, 4)

            with sp.Fori(0, NT // 2) as i:
                for u in range(2):
                    t = 2 * i + u
                    done(sp, xn2_ready, t)
                    sp.dma_start(xn2_d[bass.ds(t * P, P), :], xn2[:, u]).then_inc(xn2_out.s[u], 16)
                    done(sp, tr5_rd, t)
                    sp.dma_start(hT_d[bass.ds(t, 1)].rearrange("a p c n -> p (a c) n"), tr5[:, u, 0]).then_inc(tr5_out.s[u], 16)
                    sp.dma_start(xT_d[bass.ds(t, 1)].rearrange("a p c n -> p (a c) n"), tr5[:, u, 1]).then_inc(tr5_out.s[u], 16)
            for u in range(2):
                xn2_out.done(sp, NT - 2 + u, u)
                tr5_out.done(sp, NT - 2 + u, u)
            stage_end(sp, 5)

            for dst, name in ((cos, "cos"), (sin, "sin"), (mask0, "mask_first"), (mask1, "mask")):
                sp.dma_start(dst, io[name]).then_inc(tabs_in, 16)

            def load_group(n, g, b, gg):
                sp.dma_start(wqk[gg], wqk_d[bass.ds(g, 1)].rearrange("a p s c n -> p (a s) c n")).then_inc(h_in.s[gg], 16)
                sp.dma_start(hT[gg], hT_d[bass.ds(b * TPB, TPB)].rearrange("n p c t -> p n c t")).then_inc(h_in.s[gg], 16)

            for gg in range(2):
                load_group(gg, gg, 0, gg)
            with sp.Fori(1, NPAIR) as i:
                for gg in range(2):
                    upto(sp, proj_mm, 2 * GH * (2 * i + gg - 1) - 1)
                    load_group(2 * i + gg, 2 * (i % 2) + gg, i // 2, gg)
            stage_end(sp, 6)

            sp.dma_start(w13, io["w13T"].rearrange("(c p) e f -> p c e f", p=P)).then_inc(w13_in, 16)
            sp.dma_start(w2a, io["w2T"][:, 0:P, :].rearrange("e f d -> f e d")).then_inc(w13_in, 16)
            sp.dma_start(w2b, io["w2T"][:, P:F1, :].rearrange("e f d -> f e d")).then_inc(w13_in, 16)
            def load_xT(t, u):
                upto(sp, xT_used, t - 4)
                sp.dma_start(xT[:, u], xT_d[bass.ds(t, 1)].rearrange("a p c n -> p (a c) n")).then_inc(xT_in.s[u], 16)

            for t in range(3):
                load_xT(t, t)
            with sp.Fori(0, XT // 4) as i:
                for u in range(4):
                    j = 4 * i + u
                    upto(sp, y1_rd, j)
                    sp.dma_start(y1_d[bass.ds(j * P, P), :], y1s[:, u]).then_inc(y1_out.s[u], 16)
            for u in range(4):
                y1_out.done(sp, XT - 4 + u, u)
            sp.sem_inc(y1_kept, 1)

            def store_out(t, u):
                done(sp, fin_ready, t)
                sp.dma_start(io["out"][bass.ds(t * P, P), :], fin[:, u]).then_inc(out_done.s[u], 16)

            with sp.Fori(0, NT // 4 - 1) as i:
                for k in range(4):
                    load_xT(4 * i + k + 3, (k + 3) % 4)
                    store_out(4 * i + k, k % 2)
            for k in range(4):
                if k == 0:
                    load_xT(NT - 1, 3)
                store_out(NT - 4 + k, k % 2)
            for u in range(2):
                out_done.done(sp, NT - 2 + u, u)

        @block.tensor
        def _(pe):
            credit(pe, "pe")
            pe.wait_ge(consts_in, 80)
            pe.wait_ge(w0_in, 80)
            pe.wait_ge(setup, 3)
            for m in range(DC):
                for k, at in ((0, 0), (1, D)):
                    for c in range(DC):
                        pe.matmul(ps[m][:, at:at + D], w0_raw[:, k, c, m * P:(m + 1) * P], fwd[:, c],
                                  start=(c == 0), stop=(c == DC - 1))
                for c in range(DC):
                    last = pe.matmul(ps[2 + m][:, 0:D], back[:, c, m * P:(m + 1) * P], w0_raw[:, 2, c],
                                     start=(c == 0), stop=(c == DC - 1))
            last.then_inc(w0_mm, 1)
            pe.wait_ge(lora_in, 16 * 13)
            n = 0
            for j in range(3):
                for m in range(DC):
                    for q in range(4):
                        if n >= 4:
                            pe.wait_ge(lora_add, n - 3)
                        pe.matmul(ps[4 + n % 4][:, :], lora_a[:, j, m * P:(m + 1) * P], lora_b[:, j, q * 512:(q + 1) * 512],
                                  start=True, stop=True).then_inc(lora_mm, 1)
                        n += 1
            for h in range(0, H1, 2):
                pe.wait_ge(lora_add, n - 3)
                for k in range(2):
                    last = pe.matmul(ps[4 + n % 4][:, k * D:(k + 1) * D], lora_oa[:, (h + k) * P:(h + k + 1) * P], lora_ob,
                                     start=True, stop=True)
                last.then_inc(lora_mm, 1)
                n += 1
            stage_end(pe, 0)

            pe.matmul(ps[6][:, 0:2 * PAIRS], zrow[:, 0:P], zrow[:, 0:2 * PAIRS], start=True, stop=False, skip_group_check=True)

            def front(t, u):
                done(pe, xn_ready, t)
                free(pe, xnT_rd, t)
                for c in range(DC):
                    last = pe.transpose(ps[u][:, c * P:(c + 1) * P], xn[:, u, c * P:(c + 1) * P], ident[:, :])
                last.then_inc(xnT_ps, 1)
                done(pe, xnT_rd, t)
                free(pe, pos_rd, t)
                for c in range(DC):
                    pe.matmul(ps[4 + u][:, 0:E0], xnT[:, u, c], rtT[:, c, :], start=(c == 0), stop=(c == DC - 1))
                for c in range(DC):
                    last = pe.matmul(ps[2 + u][:, :], xnT[:, u, c], wqkv0[:, c, :], start=(c == 0), stop=(c == DC - 1))
                last.then_inc(qkv_ps, 1)

            def back_(t, u):
                done(pe, ohe_ready, t)
                done(pe, lg_rd, t)
                for k in range(K0):
                    pe.matmul(ps[4 + u][:, E0:2 * E0], tri_bf[:, :], ohe[:, u, k], start=(k == 0), stop=(k == K0 - 1))
                for k in range(K0):
                    last = pe.matmul(ps[4 + u][:, 2 * E0:3 * E0], ones_bf[:, :], ohe[:, u, k], start=(k == 0), stop=(k == K0 - 1))
                last.then_inc(pos_ps, 1)
                done(pe, oh_ready, t)
                for k in range(K0):
                    last = pe.matmul(ps[6][:, 0:2 * PAIRS], ohlo[:, u, k], tab_rhs[:, u, k], start=False, stop=False,
                                     skip_group_check=True)
                last.then_inc(tab_mm, 1)

            pipelined(front, back_, pe)
            pe.matmul(ps[6][:, 0:2 * PAIRS], zrow[:, 0:P], zrow[:, 0:2 * PAIRS], start=False, stop=True,
                      skip_group_check=True).then_inc(zero_bank, 1)
            stage_end(pe, 1)

            with pe.Fori(0, NB) as b:
                for tt in range(TPB):
                    t, u = TPB * b + tt, tt % 2
                    done(pe, kvn_ready, t)
                    free(pe, prod_done, t)
                    pe.matmul(ps[u][:, 0:D], tri[:, :], kvn[:, tt], start=True, stop=(tt == 0))
                    for j in range(tt):
                        last = pe.matmul(ps[u][:, 0:D], ones[:, :], kvn[:, j], start=False, stop=(j == tt - 1))
                    pe.drain().then_inc(cum_ps, 1)
                    done(pe, y_ready, t)
                    free(pe, yT_rd, t)
                    for c in range(DC):
                        last = pe.transpose(ps[2 + u][:, c * P:(c + 1) * P], yy[:, u, c * P:(c + 1) * P], ident[:, :])
                    last.then_inc(yT_ps, 1)
                    done(pe, yT_rd, t)
                    free(pe, s0_rd, t)
                    for c in range(DC):
                        last = pe.matmul(ps[4 + u][:, 0:D], yT[:, u, c], wo0[:, c, :], start=(c == 0), stop=(c == DC - 1))
                    last.then_inc(s0_ps, 1)
            stage_end(pe, 2)

            with pe.Fori(0, PAIRS // 4) as i:
                for u in range(4):
                    j, v = 4 * i + u, u % 2
                    pe.wait_ge(xg_in[u], 16 * (i + 1))
                    if u >= 2:
                        done(pe, xgT_rd, j - 2, 1, 4)
                    else:
                        pe.wait_ge(xgT_rd, j + 3)
                    for c in range(DC):
                        last = pe.transpose(ps[v][:, c * P:(c + 1) * P], xg[:, u, c * P:(c + 1) * P], ident[:, :])
                    last.then_inc(xgT_ps, 1)
                    we_in.done(pe, j, u)
                    done(pe, xgT_rd, j, 1, 4)
                    pe.wait_ge(hm_ready, j + 3)
                    for g in range(2):
                        for e in range(2):
                            at = (2 * g + e) * CAP
                            for c in range(DC):
                                last = pe.matmul(ps[2 + v][0:F0, at:at + CAP], wgu_e[:, u, 4 * g + 2 * e + c],
                                                 xgT[:, u, c, e * CAP:(e + 1) * CAP], start=(c == 0), stop=(c == DC - 1))
                    last.then_inc(gu_ps, 1)
                    done(pe, hm_ready, j, 1, 4)
                    pe.wait_ge(y0_rd, j + 3)
                    for e in range(2):
                        last = pe.matmul(ps[4 + v][e * CAP:(e + 1) * CAP, 0:D], hm0[:, u, e * CAP:(e + 1) * CAP],
                                         wd_e[:, u, e], start=True, stop=True)
                    last.then_inc(y0_ps, 1)
            stage_end(pe, 3)
            stage_end(pe, 4)

            def front5(t, u):
                done(pe, xn2_ready, t)
                free(pe, tr5_rd, t)
                for k, a in ((0, hh2), (1, xn2)):
                    for c in range(DC):
                        last = pe.transpose(ps[u][:, (2 * k + c) * P:(2 * k + c + 1) * P], a[:, u, c * P:(c + 1) * P], ident[:, :])
                last.then_inc(tr5_ps, 1)

            def back5(t, u):
                done(pe, tr5_rd, t)
                free(pe, lg5_rd, t)
                for c in range(DC):
                    last = pe.matmul(ps[2 + u][:, 0:E1 + 1], tr5[:, u, 1, c], gtT[:, c, :], start=(c == 0), stop=(c == DC - 1))
                last.then_inc(lg5_ps, 1)

            pipelined(front5, back5, pe)
            pe.wait_ge(chosen, 1)
            pe.matmul(ps[4][:, 0:NT * E1], tri_bf[:, :], flat(mkA), start=True, stop=True)
            pe.matmul(ps[5][:, 0:NT * E1], ones_bf[:, :], flat(mkA), start=True, stop=True).then_inc(counted, 1)
            pe.wait_ge(table_in, 1)
            for n in range(NT * K1):
                last = pe.matmul(ps[6][:, 0:2 * XT], ohloA[:, n], tab5[:, n], start=(n == 0), stop=(n == NT * K1 - 1))
            last.then_inc(table_mm, 1)
            stage_end(pe, 5)


            def project(h, gg, hh):
                for s in range(2):
                    upto(pe, swap_rd, 2 * h + s - 2)
                    for c in range(DC):
                        last = pe.matmul(ps[s][:, :], wqk[gg][:, s, c, hh * DH:(hh + 1) * DH], hT[gg][:, :, c, :],
                                         start=(c == 0), stop=(c == DC - 1))
                    last.then_inc(proj_mm, 1)

            def values(n, g, gg, q):
                if q == 0:
                    h_in.done(pe, n, gg)
                    upto(pe, op_rd, 2 * n - 4)
                upto(pe, v_rd, n * TPB + q - 1)
                for c in range(DC):
                    last = pe.matmul(ps[2][:, :], hT[gg][:, q, c, :], wv_sb[:, c, bass.ds(g * 512, 512)],
                                     start=(c == 0), stop=(c == DC - 1))
                last.then_inc(v_ps, 1)

            def scores(h, u):
                upto(pe, rope_done, 2 * h + 1)
                upto(pe, sm_done, h - 1)
                for q in range(TPB):
                    last = pe.matmul(ps[3 + q // 2][:, (q % 2) * KW:(q % 2 + 1) * KW], qr[:, u, q * P:(q + 1) * P],
                                     kr[:, u, q * P:q * P + KW], start=True, stop=True)
                last.then_inc(sc_ps, 1)

            def turn_probs(h, hh):
                upto(pe, pn_done, h)
                for half in range(2):
                    k = 2 * h + half
                    upto(pe, pt_rd, k - 2)
                    for q in range(2):
                        for c in range(2):
                            last = pe.transpose(ps[5 + half][:, (2 * q + c) * P:(2 * q + c + 1) * P],
                                                pp[hh % 2][:, 2 * half + q, c * P:(c + 1) * P], ident[:, :])
                    last.then_inc(pt_ps, 1)

            def attend(h, n, gg, hh):
                upto(pe, ot_rd, h - 1)
                if hh == 0:
                    upto(pe, op_rd, 2 * n - 1)
                for q in range(TPB):
                    if q % 2 == 0:
                        upto(pe, pt_rd, 2 * h + q // 2)
                    last = pe.matmul(ps[7][:, q * P:(q + 1) * P], vv[gg][:, q, hh * DH:(hh + 1) * DH], pT[:, q // 2, q % 2, 1],
                                     start=True, stop=(q == 0))
                    if q:
                        last = pe.matmul(ps[7][:, q * P:(q + 1) * P], vv[gg][:, q - 1, hh * DH:(hh + 1) * DH],
                                         pT[:, q // 2, q % 2, 0], start=False, stop=True)
                last.then_inc(ot_ps, 1)

            def output(n, g, gg, valued):
                upto(pe, ot_rd, n * GH + GH - 1)
                upto(pe, v_rd, (n + valued) * TPB + TPB - 1)
                for half in range(2):
                    for q in range(2):
                        for hh in range(GH):
                            last = pe.matmul(ps[2 if half == 0 else 7][:, q * D:(q + 1) * D],
                                             oT[gg][:, hh, (2 * half + q) * P:(2 * half + q + 1) * P],
                                             wo_sb[:, bass.ds(g * GH + hh, 1), :].rearrange("p a d -> p (a d)"),
                                             start=(hh == 0), stop=(hh == GH - 1))
                    last.then_inc(op_ps, 1)

            h_in.done(pe, 0, 0)
            project(0, 0, 0)
            for q in range(TPB):
                values(0, 0, 0, q)
            project(1, 0, 1)
            upto(pe, v_rd, TPB - 1)
            scores(0, 0)

            def pair(i, last_pair):
                for k in range(2 * GH):
                    h, n, gg, hh = 2 * GH * i + k, 2 * i + k // GH, k // GH, k % GH
                    if not (last_pair and k >= 2 * GH - 2):
                        project(h + 2, (k + 2) // GH % 2, (k + 2) % GH)
                    if not (last_pair and k == 2 * GH - 1):
                        scores(h + 1, (k + 1) % 2)
                    turn_probs(h, hh)
                    if gg == 0:
                        values(n + 1, 2 * (i % 2) + 1, 1, hh)
                    elif not last_pair:
                        values(n + 1, 2 * ((i + 1) % 2), 0, hh)
                    attend(h, n, gg, hh)
                    if hh == GH - 1:
                        output(n, 2 * (i % 2) + gg, gg, 0 if last_pair and gg else 1)

            by_pairs(pe, pair)
            stage_end(pe, 6)

            pe.wait_ge(w13_in, 48)

            def expert_of(j):
                return pe.value_load(etab[0:1, bass.ds(j, 1)], min_val=0, max_val=E1 - 1)

            def rows_in(i, j, u):
                pe.wait_ge(xs_in[u], 16 * (i + 1))
                upto(pe, xsT_rd, j - 2)
                for c in range(DC):
                    last = pe.transpose(ps[u % 2][:, c * P:(c + 1) * P], xs[:, u, c * P:(c + 1) * P], ident[:, :])
                last.then_inc(xsT_ps, 1)

            def up_proj(e, lhs, bank):
                for c in range(DC):
                    last = pe.matmul(ps[bank][:, 0:2 * F1], lhs[:, c], w13[:, c, bass.ds(e, 1), :].rearrange("p a f -> p (a f)"),
                                     start=(c == 0), stop=(c == DC - 1))
                return last

            def turn_h(u):
                pe.transpose(ps[4 + u][:, 0:P], h1[:, u, 0:P], ident[:, :])
                return pe.transpose(ps[4 + u][0:F1 - P, P:2 * P], h1[:, u, P:F1], ident[:, :])

            def down_proj(e, u, bank, start, stop):
                pe.matmul(ps[bank][:, 0:D], h1T[:, u, 0:P], w2a[:, bass.ds(e, 1), :].rearrange("p a d -> p (a d)"),
                          start=start, stop=False)
                return pe.matmul(ps[bank][:, 0:D], h1T[0:F1 - P, u, P:2 * P],
                                 w2b[:, bass.ds(e, 1), :].rearrange("p a d -> p (a d)"), start=False, stop=stop)

            def routed_up(e, j, u):
                upto(pe, xsT_rd, j)
                upto(pe, h1_ready, j - 2)
                up_proj(e, xsT[:, u], 2 + u % 2).then_inc(gu1_ps, 1)

            def routed(i, k, last_tiles):
                j = 4 * i + k
                if not (last_tiles and k == 3):
                    e = expert_of(j + 1)
                if not (last_tiles and k >= 2):
                    rows_in(i + (k + 2) // 4, j + 2, (k + 2) % 4)
                upto(pe, h1_ready, j)
                upto(pe, h1T_rd, j - 2)
                turn_h(k % 2).then_inc(h1T_ps, 1)
                if not (last_tiles and k == 3):
                    routed_up(e, j + 1, (k + 1) % 4)
                e = expert_of(j)
                upto(pe, h1T_rd, j)
                upto(pe, y1_rd, j - 2)
                down_proj(e, k % 2, 6 + k % 2, True, True).then_inc(y1_ps, 1)

            rows_in(0, 0, 0)
            rows_in(0, 1, 1)
            routed_up(expert_of(0), 0, 0)
            with pe.Fori(0, XT // 4 - 1) as i:
                for k in range(4):
                    routed(i, k, False)
            for k in range(4):
                routed(XT // 4 - 1, k, True)

            def shared_up(t, q, u):
                n = NS * t + q
                if q == 0:
                    xT_in.done(pe, t, u)
                upto(pe, hs_ready, n - 4)
                up_proj(E1 + q, xT[:, u], q).then_inc(gus_ps, 1)

            def shared(t, u, last_tile):
                for q in range(NS):
                    n = NS * t + q
                    upto(pe, hs_ready, n)
                    upto(pe, hsT_rd, n - 2)
                    turn_h(q % 2).then_inc(hsT_ps, 1)
                    if q == NS - 1:
                        pe.sem_inc(xT_used, 1)
                    if not (last_tile and q >= NS - 2):
                        shared_up(t + (q + 2) // NS, (q + 2) % NS, (u + (q + 2) // NS) % 4)
                    if q == 0:
                        free(pe, sum_done, t)
                    upto(pe, hsT_rd, n)
                    down_proj(E1 + q, q % 2, 6 + u % 2, q == 0, q == NS - 1).then_inc(ys_ps, 1)

            upto(pe, h1T_rd, XT - 1)
            shared_up(0, 0, 0)
            shared_up(0, 1, 0)
            upto(pe, y1_rd, XT - 1)
            with pe.Fori(0, NT // 4 - 1) as i:
                for k in range(4):
                    shared(4 * i + k, k, False)
            for k in range(4):
                shared(NT - 4 + k, k, k == 3)

        @block.scalar
        def _(act):
            credit(act, "act")
            for n in range(24):
                j, m, q = n // 8, n // 4 % 2, n % 4
                act.wait_ge(lora_add, n + 1)
                a = (wqk_raw[:, j, m] if j < 2 else wv_sb[:, m, :])[:, q * 512:(q + 1) * 512]
                nc.scalar.activation(a, a, ACT.Copy, scale=norm_w[:, m:m + 1]).then_inc(lora_scaled, 1)
            act.wait_ge(var_ready, 1)
            nc.scalar.activation(tmpa, var, ACT.Sqrt).then_inc(std_ready, 1)
            stage_end(act, 0)

            def front(t, u):
                free(act, xnT_ps, t)
                xn_stored.free(act, t, u)
                nc.scalar.activation(xn[:, u], row(x_sb[:, bass.ds(t, 1), :]), ACT.Identity,
                                     bias=nmr[:, bass.ds(t, 1)], scale=rstd[:, bass.ds(t, 1)]).then_inc(xn_ready, 1)
                done(act, xnT_ps, t)
                free(act, qkv_ps, t)
                nc.scalar.activation(flat(xnT[:, u]), ps[u][:, 0:D], ACT.Copy).then_inc(xnT_rd, 1)
                done(act, qkv_ps, t)
                free(act, exp_done, t)
                free(act, oh_ready, t)
                nc.scalar.activation(lg[:, u], ps[4 + u][:, 0:E0], ACT.Copy).then_inc(lg_rd, 1)
                nc.scalar.activation(row(qkv[:, bass.ds(t, 1), :]), ps[2 + u][:, :], ACT.Copy).then_inc(qkv_rd, 1)

            def back_(t, u):
                done(act, top_ready, t)
                nc.scalar.activation(junk[:, u], lg[:, u], ACT.Exp, bias=negm[:, u], accum_out=zsum[:, bass.ds(t, 1)])
                nc.scalar.activation(row(e8[:, bass.ds(t, 1), :]), mx[:, u], ACT.Exp, bias=negm[:, u]).then_inc(exp_done, 1)

            pipelined(front, back_, act)
            done(act, ss_ready, NT - 1)
            nc.scalar.activation(flat(ss), flat(ss), ACT.Sqrt).then_inc(nrm_sq, 1)
            stage_end(act, 1)

            with act.Fori(0, NB) as b:
                for tt in range(TPB):
                    t, u = TPB * b + tt, tt % 2
                    done(act, yT_ps, t)
                    free(act, s0_ps, t)
                    nc.scalar.activation(flat(yT[:, u]), ps[2 + u][:, 0:D], ACT.Copy).then_inc(yT_rd, 1)
                    done(act, s0_ps, t)
                    nc.scalar.activation(row(s_sb[:, bass.ds(t, 1), :]), ps[4 + u][:, 0:D], ACT.Copy).then_inc(s0_rd, 1)
            stage_end(act, 2)

            with act.Fori(0, PAIRS // 4) as i:
                for u in range(4):
                    j, v = 4 * i + u, u % 2
                    done(act, xgT_ps, j, 1, 4)
                    free(act, gu_ps, j)
                    nc.scalar.activation(flat(xgT[:, u]), ps[v][:, 0:D], ACT.Copy).then_inc(xgT_rd, 1)
                    done(act, gu_ps, j, 1, 4)
                    free(act, hm_ready, j)
                    nc.scalar.activation(sg0[:, u], ps[2 + v][0:F0, 0:P], ACT.Silu).then_inc(sg_ready, 1)
            stage_end(act, 3)

            with act.Fori(0, NT // 2) as i:
                for u in range(2):
                    t = 2 * i + u
                    done(act, mix_done, t)
                    free(act, x1_done, t)
                    nc.scalar.activation(g0[:, u], mix[:, u], ACT.Silu).then_inc(g_ready, 1)
            act.wait_ge(var_ready, 2)
            nc.scalar.activation(tmpa, var, ACT.Sqrt).then_inc(std_ready, 1)
            act.wait_ge(var_ready, 3)
            nc.scalar.activation(tmpb, tmpb, ACT.Sqrt).then_inc(std_ready, 1)
            stage_end(act, 4)

            def front(t, u):
                free(act, tr5_ps, t)
                free(act, xn2_kept, t)
                xn2_out.free(act, t, u)
                nc.scalar.activation(xn2[:, u], row(x_sb[:, bass.ds(t, 1), :]), ACT.Identity,
                                     bias=nmr[:, bass.ds(t, 1)], scale=rstd[:, bass.ds(t, 1)])
                act.drain()
                nc.scalar.activation(hh2[:, u], xn2[:, u], ACT.Copy, scale=rms[:, bass.ds(t, 1)]).then_inc(xn2_ready, 1)

            def back_(t, u):
                done(act, tr5_ps, t)
                tr5_out.free(act, t, u)
                free(act, lg5_ps, t)
                nc.scalar.activation(tr5[:, u].rearrange("p a b c -> p (a b c)"), ps[u][:, :], ACT.Copy).then_inc(tr5_rd, 1)

            pipelined(front, back_, act)
            act.wait_ge(exp5_in, 1)
            nc.scalar.activation(flat(exA), flat(exA), ACT.Exp)
            nc.scalar.activation(flat(w4[:, :, :]), flat(w4[:, :, :]), ACT.Exp)
            nc.scalar.activation(sgA, lgA[:, :, E1], ACT.Exp, scale=-1.0)
            act.drain().then_inc(exp5_done, 1)
            stage_end(act, 5)

            def swap(h):
                for s in range(2):
                    k = 2 * h + s
                    upto(act, cos_rd, k)
                    upto(act, rope_done, k - 2)
                    nc.scalar.activation(qk_s[0:64, s], ps[s][64:P, :], ACT.Copy)
                    nc.scalar.activation(qk_s[64:P, s], ps[s][0:64, :], ACT.Copy).then_inc(swap_rd, 1)

            def value_out(n, gg, q):
                upto(act, v_ps, n * TPB + q)
                nc.scalar.activation(vv[gg][:, q], ps[2][:, :], ACT.Copy).then_inc(v_rd, 1)

            def exponentials(h, u):
                upto(act, sm_done, h)
                upto(act, pt_ps, 2 * h - 3)
                upto(act, rs_done, h - 1)
                for q in range(TPB):
                    nc.scalar.activation(pp[u][:, q, P - WIN:2 * P], sm[:, q], ACT.Exp, bias=mn[:, q:q + 1], scale=-1.0,
                                         accum_out=rs[:, q:q + 1])
                act.drain().then_inc(pe_done, 1)

            swap(0)
            for q in range(TPB):
                value_out(0, 0, q)
            swap(1)
            exponentials(0, 0)

            def pair(i, last_pair):
                for k in range(2 * GH):
                    h, n, gg, hh = 2 * GH * i + k, 2 * i + k // GH, k // GH, k % GH
                    if not (last_pair and k >= 2 * GH - 2):
                        swap(h + 2)
                    if not (last_pair and k == 2 * GH - 1):
                        exponentials(h + 1, (k + 1) % 2)
                    if not (last_pair and gg):
                        value_out(n + 1, 1 - gg, hh)

            by_pairs(act, pair)
            stage_end(act, 6)

            def evacuate(dst, src):
                nc.scalar.activation(dst, src, ACT.Copy)

            def rows_out(j, u):
                upto(act, xsT_ps, j)
                upto(act, gu1_ps, j - 4)
                nc.scalar.activation(flat(xsT[:, u]), ps[u % 2][:, 0:D], ACT.Copy).then_inc(xsT_rd, 1)

            def gate_out(s_in, s_free, s_out, j, u):
                upto(act, s_in, j)
                upto(act, s_free, j - 2)
                nc.scalar.activation(sg1[:, u], ps[2 + u][:, 0:F1], ACT.Silu).then_inc(s_out, 1)

            def h_out(s_in, s_free, s_out, j, u):
                upto(act, s_in, j)
                upto(act, s_free, j - 2)
                nc.scalar.activation(h1T[:, u, 0:P], ps[4 + u][:, 0:P], ACT.Copy)
                nc.scalar.activation(h1T[0:F1 - P, u, P:2 * P], ps[4 + u][0:F1 - P, P:2 * P], ACT.Copy)
                act.drain().then_inc(s_out, 1)

            def routed(i, k, last_tiles):
                j = 4 * i + k
                if not (last_tiles and k >= 2):
                    rows_out(j + 2, (k + 2) % 4)
                h_out(h1T_ps, y1_ps, h1T_rd, j, k % 2)
                if not (last_tiles and k == 3):
                    gate_out(gu1_ps, h1_ready, sg1_ready, j + 1, (k + 1) % 2)

            rows_out(0, 0)
            rows_out(1, 1)
            gate_out(gu1_ps, h1_ready, sg1_ready, 0, 0)
            with act.Fori(0, XT // 4 - 1) as i:
                for k in range(4):
                    routed(i, k, False)
            for k in range(4):
                routed(XT // 4 - 1, k, True)

            def shared_gate(n, q):
                upto(act, gus_ps, n)
                upto(act, hs_ready, n - 2)
                nc.scalar.activation(sg1[:, q % 2], ps[q][:, 0:F1], ACT.Silu).then_inc(sgs_ready, 1)

            def out_gate(t, u):
                done(act, sum_done, t)
                free(act, fin_ready, t)
                nc.scalar.activation(g1[:, u], mix1[:, u], ACT.Silu).then_inc(g1_ready, 1)

            def shared(t, u, first=False, last=False):
                for q in range(NS):
                    n = NS * t + q
                    h_out(hsT_ps, ys_ps, hsT_rd, n, q % 2)
                    if not (last and q >= NS - 2):
                        shared_gate(n + 2, (q + 2) % NS)
                    if q == 2 and not first:
                        out_gate(t - 1, 1 - u)

            upto(act, h1_ready, XT - 1)
            shared_gate(0, 0)
            shared_gate(1, 1)
            upto(act, y1_ps, XT - 1)
            over_tiles(act, shared)
            out_gate(NT - 1, 1)

        @block.vector
        def _(dve):
            credit(dve, "dve")
            nc.vector.memset(ones[:, :], 1.0).then_inc(setup, 1)
            nc.vector.memset(zrow[:, :], 0.0).then_inc(setup, 1)
            nc.vector.memset(ones_bf[:, :], 1.0).then_inc(setup, 1)
            dve.wait_ge(w0_mm, 1)
            for m in range(DC):
                nc.vector.tensor_copy(wqkv0[:, m, :], ps[m][:, :])
                nc.vector.tensor_copy(wo0[:, m, :], ps[2 + m][:, 0:D])
            dve.wait_ge(lora_in, 16 * 13)
            for n in range(24):
                j, m, q = n // 8, n // 4 % 2, n % 4
                dve.wait_ge(lora_mm, n + 1)
                a = (wqk_raw[:, j, m] if j < 2 else wv_sb[:, m, :])[:, q * 512:(q + 1) * 512]
                nc.vector.scalar_tensor_tensor(a, ps[4 + n % 4][:, :], 1.0 / RANK, a, ALU.mult, ALU.add).then_inc(lora_add, 1)
            for h in range(0, H1, 2):
                n = 24 + h // 2
                dve.wait_ge(lora_mm, n + 1)
                a = flat(wo_sb[:, h:h + 2, :])
                nc.vector.scalar_tensor_tensor(a, ps[4 + n % 4][:, :], 1.0 / RANK, a, ALU.mult, ALU.add).then_inc(lora_add, 1)
            dve.wait_ge(consts_in, 80)
            nc.vector.tensor_copy(iota_bf[:, :], iota[:, :])
            nc.vector.tensor_tensor(tri_bf[:, :], tri[:, :], ident[:, :], ALU.subtract)
            dve.wait_ge(x_in, 48)

            def statistics(times):
                if times == 1:
                    with dve.Fori(0, NT) as t:
                        nc.vector.bn_stats(row(stat6[:, bass.ds(t, 1), :]), row(x_sb[:, bass.ds(t, 1), :]))
                dve.drain()
                nc.vector.tensor_tensor(tmpa, stat6[:, :, 1], stat6[:, :, 4], ALU.subtract)
                nc.vector.tensor_tensor(nmr, stat6[:, :, 1], stat6[:, :, 4], ALU.add)
                nc.vector.tensor_tensor(var, stat6[:, :, 2], stat6[:, :, 5], ALU.add)
                dve.drain()
                nc.vector.tensor_tensor(tmpa, tmpa, tmpa, ALU.mult)
                nc.vector.tensor_scalar(var, var, 1.0 / D, LN_EPS, ALU.mult, ALU.add)
                dve.drain()
                nc.vector.scalar_tensor_tensor(var, tmpa, 0.25, var, ALU.mult, ALU.add).then_inc(var_ready, 1)
                dve.wait_ge(std_ready, times if times == 1 else 2)
                nc.vector.reciprocal(rstd, tmpa)
                dve.drain()
                nc.vector.scalar_tensor_tensor(nmr, nmr, -0.5, rstd, ALU.mult, ALU.mult)

            statistics(1)
            nc.vector.memset(base, 0.0)
            stage_end(dve, 0)

            def back_(t, u):
                done(dve, lg_rd, t)
                free(dve, exp_done, t)
                rest(dve, "dve")
                nc.vector.max(mx[:, u], lg[:, u])
                dve.drain()
                nc.vector.max_index(mi[:, u], mx[:, u], lg[:, u])
                nc.vector.tensor_scalar(negm[:, u], mx[:, u, 0:1], -1.0, None, ALU.mult).then_inc(top_ready, 1)
                dve.drain()
                nc.vector.tensor_copy(idf[:, u], mi[:, u])
                dve.drain()
                free(dve, pos_ps, t)
                nc.vector.tensor_tensor(ohe[:, u], iota_bf[:, 0:E0].unsqueeze(1).to_broadcast([P, K0, E0]),
                                        idf[:, u].unsqueeze(2).to_broadcast([P, K0, E0]), ALU.is_equal).then_inc(ohe_ready, 1)
                done(dve, sq_ready, t)
                nc.vector.tensor_reduce(row(ss[:, bass.ds(t, 1), :]), sq[:, u].rearrange("p (g d) -> p g d", d=HD0), AX.X, ALU.add)\
                    .then_inc(ss_ready, 1)
                done(dve, pos_ps, t)
                nc.vector.tensor_tensor(posb, ps[4 + u][:, E0:2 * E0], base, ALU.add)
                dve.drain()
                nc.vector.tensor_tensor(base, ps[4 + u][:, 2 * E0:3 * E0], base, ALU.add).then_inc(pos_rd, 1)
                nc.vector.tensor_tensor(prod, ohe[:, u], posb.unsqueeze(1).to_broadcast([P, K0, E0]), ALU.mult)
                dve.drain()
                nc.vector.tensor_reduce(row(pos8[:, bass.ds(t, 1), :]), prod, AX.X, ALU.add)
                dve.drain()
                pos = row(pos8[:, bass.ds(t, 1), :])
                nc.vector.tensor_scalar(badf, pos, float(CAP), float(FULL), ALU.is_ge, ALU.mult)
                nc.vector.scalar_tensor_tensor(dstf, idf[:, u], float(CAP), pos, ALU.mult, ALU.add)
                dve.drain()
                nc.vector.tensor_tensor(dsti, dstf, badf, ALU.add)
                nc.vector.tensor_tensor(row(dest[:, bass.ds(t, 1), :]), dstf, badf, ALU.add)
                dve.drain()
                nc.vector.tensor_scalar(loi, dsti, P - 1, None, ALU.bitwise_and)
                nc.vector.tensor_scalar(hii, dsti, 7, None, ALU.arith_shift_right)
                dve.drain()
                free(dve, tab_mm, t)
                nc.vector.tensor_tensor(ohlo[:, u], iota_bf[:, :].unsqueeze(1).to_broadcast([P, K0, P]),
                                        loi.unsqueeze(2).to_broadcast([P, K0, P]), ALU.is_equal)
                nc.vector.tensor_tensor(ohhi, iota_bf[:, 0:PAIRS].unsqueeze(1).to_broadcast([P, K0, PAIRS]),
                                        hii.unsqueeze(2).to_broadcast([P, K0, PAIRS]), ALU.is_equal)
                dve.drain()
                nc.vector.tensor_scalar(tab_rhs[:, u, :, 0:PAIRS], ohhi, pid[:, 0:1], None, ALU.mult)
                nc.vector.tensor_scalar(tab_rhs[:, u, :, PAIRS:2 * PAIRS], ohhi, tile_id[:, bass.ds(t, 1)], None, ALU.mult)
                dve.drain().then_inc(oh_ready, 1)

            pipelined(lambda t, u: None, back_, dve)
            dve.wait_ge(zero_bank, 1)
            nc.vector.tensor_copy(tabf[:, 0], ps[6][:, 0:PAIRS])
            dve.drain()
            nc.vector.scalar_tensor_tensor(idx0[:, :], ps[6][:, PAIRS:2 * PAIRS], float(P), tabf[:, 0], ALU.mult, ALU.add)
            done(dve, exp_done, NT - 1)
            nc.vector.reciprocal(rz[:, :], zsum[:, :])
            dve.drain()
            nc.vector.tensor_tensor(e8[:, :, :], e8[:, :, :], rz[:, :].unsqueeze(2).to_broadcast([P, NT, K0]), ALU.mult)
            dve.drain()
            nc.vector.tensor_reduce(zsum[:, :], e8[:, :, :], AX.X, ALU.add)
            dve.drain()
            nc.vector.tensor_scalar(zsum[:, :], zsum[:, :], 1e-20, None, ALU.add)
            dve.drain()
            nc.vector.reciprocal(rz[:, :], zsum[:, :])
            nc.vector.tensor_scalar(w8[:, :, :], pos8[:, :, :], float(CAP), None, ALU.is_lt)
            dve.drain()
            nc.vector.tensor_tensor(e8[:, :, :], e8[:, :, :], rz[:, :].unsqueeze(2).to_broadcast([P, NT, K0]), ALU.mult)
            dve.drain()
            nc.vector.tensor_tensor(w8[:, :, :], w8[:, :, :], e8[:, :, :], ALU.mult)
            dve.wait_ge(nrm_sq, 1)
            nc.vector.reciprocal(flat(ss), flat(ss)).then_inc(nrm_rt, 1)
            stage_end(dve, 1)

            with dve.Fori(0, NB) as b:
                for tt in range(TPB):
                    t, u = TPB * b + tt, tt % 2
                    done(dve, kvn_ready, t)
                    done(dve, cum_ps, t)
                    free(dve, yT_ps, t)
                    v4 = lambda a: a.rearrange("p (h c k) -> p h c k", h=H0, c=2)
                    q4, c4, a4, b4, y4 = v4(qn[:, u]), v4(ps[u][:, 0:D]), v4(pa), v4(pb), v4(yy[:, u])
                    nc.vector.tensor_tensor(pa, qn[:, u], ps[u][:, 0:D], ALU.mult)
                    nc.vector.tensor_tensor(b4[:, :, 0], q4[:, :, 1], c4[:, :, 0], ALU.mult)
                    nc.vector.tensor_tensor(b4[:, :, 1], q4[:, :, 0], c4[:, :, 1], ALU.mult).then_inc(prod_done, 1)
                    dve.drain()
                    nc.vector.tensor_tensor(y4[:, :, 0], a4[:, :, 0], a4[:, :, 1], ALU.subtract)
                    nc.vector.tensor_tensor(y4[:, :, 1], b4[:, :, 0], b4[:, :, 1], ALU.add)
                    dve.drain()
                    nc.vector.tensor_copy(y4[:, :, :, 0], a4[:, :, :, 0]).then_inc(y_ready, 1)
            stage_end(dve, 2)

            with dve.Fori(0, PAIRS // 4) as i:
                for u in range(4):
                    j, v = 4 * i + u, u % 2
                    done(dve, sg_ready, j, 1, 4)
                    free(dve, y0_ps, j)
                    nc.vector.tensor_tensor(hm0[:, u], ps[2 + v][0:F0, P:2 * P], sg0[:, u], ALU.mult).then_inc(hm_ready, 1)
                    done(dve, y0_ps, j, 1, 4)
                    y0_out.free(dve, j, u)
                    nc.vector.tensor_copy(y0[:, u], ps[4 + v][:, 0:D]).then_inc(y0_rd, 1)
            nc.vector.memset(yg, 0.0).then_inc(zeroed, 1)
            stage_end(dve, 3)

            with dve.Fori(0, NT // 2) as i:
                for u in range(2):
                    t = 2 * i + u
                    dve.wait_ge(yg_in[u], 16 * K0 * (i + 1))
                    free(dve, g_ready, t)
                    nc.vector.tensor_scalar(mix[:, u], yg[:, u, 0], w8[:, bass.ds(t, 1), 0:1].rearrange("p a b -> p (a b)"), None, ALU.mult)
                    for k in range(1, K0):
                        dve.drain()
                        last = nc.vector.scalar_tensor_tensor(mix[:, u], yg[:, u, k],
                                                              w8[:, bass.ds(t, 1), k:k + 1].rearrange("p a b -> p (a b)"), mix[:, u],
                                                              ALU.mult, ALU.add)
                    last.then_inc(mix_done, 1)
                    done(dve, g_ready, t)
                    nc.vector.tensor_tensor(g0[:, u], g0[:, u], row(s_sb[:, bass.ds(t, 1), :]), ALU.mult)
                    dve.drain()
                    nc.vector.tensor_tensor(row(x_sb[:, bass.ds(t, 1), :]), row(x_sb[:, bass.ds(t, 1), :]), g0[:, u], ALU.add)
                    dve.drain()
                    nc.vector.bn_stats(row(stat6[:, bass.ds(t, 1), :]), row(x_sb[:, bass.ds(t, 1), :])).then_inc(x1_done, 1)
            statistics(2)
            nc.vector.tensor_scalar(tmpb, var, LN_EPS, None, ALU.subtract)
            nc.vector.reciprocal(rms, var)
            dve.drain()
            nc.vector.tensor_tensor(tmpb, tmpb, rms, ALU.mult)
            dve.drain()
            nc.vector.tensor_scalar(tmpb, tmpb, RMS_EPS, None, ALU.add)
            dve.drain().then_inc(var_ready, 1)
            dve.wait_ge(std_ready, 3)
            nc.vector.reciprocal(rms, tmpb)
            stage_end(dve, 4)

            def front5(t, u):
                done(dve, xn2_ready, t)
                nc.vector.tensor_copy(row(s_sb[:, bass.ds(t, 1), :]), xn2[:, u]).then_inc(xn2_kept, 1)

            def back5(t, u):
                done(dve, lg5_ps, t)
                nc.vector.tensor_copy(lg5[:, u], ps[2 + u][:, 0:E1 + 1]).then_inc(lg5_rd, 1)
                dve.drain()
                nc.vector.max(mx5[:, u], lg5[:, u, 0:E1])
                nc.vector.tensor_copy(row(lgA[:, bass.ds(t, 1), :]), lg5[:, u])
                dve.drain()
                nc.vector.max_index(mi5[:, u], mx5[:, u], lg5[:, u, 0:E1])
                nc.vector.tensor_copy(row(mxA[:, bass.ds(t, 1), :]), mx5[:, u, 0:K1])
                dve.drain()
                nc.vector.tensor_copy(row(idA[:, bass.ds(t, 1), :]), mi5[:, u, 0:K1])

            pipelined(front5, back5, dve)
            dve.drain()
            nc.vector.tensor_tensor(exA, lgA[:, :, 0:E1], mxA[:, :, 0:1].to_broadcast([P, NT, E1]), ALU.subtract)
            nc.vector.tensor_tensor(w4[:, :, :], mxA, mxA[:, :, 0:1].to_broadcast([P, NT, K1]), ALU.subtract)
            dve.drain().then_inc(exp5_in, 1)
            for n in range(0, NT, 4):
                nc.vector.tensor_tensor(ohA[:, n:n + 4].rearrange("p n k e -> p (n k) e"),
                                        iota_bf[:, 0:E1].unsqueeze(1).to_broadcast([P, 4 * K1, E1]),
                                        flat(idA[:, n:n + 4]).unsqueeze(2).to_broadcast([P, 4 * K1, E1]), ALU.is_equal)
            dve.drain()
            nc.vector.tensor_tensor(mkA, ohA[:, :, 0], ohA[:, :, 1], ALU.add)
            nc.vector.tensor_tensor(rank, ohA[:, :, 2], ohA[:, :, 3], ALU.add)
            dve.drain()
            nc.vector.tensor_tensor(mkA, mkA, rank, ALU.add)
            dve.drain().then_inc(chosen, 1)
            dve.wait_ge(counted, 1)
            nc.vector.tensor_copy(flat(rank), ps[4][:, 0:NT * E1])
            nc.vector.tensor_copy(flat(cnt[0]), ps[5][:, 0:NT * E1])

            def running(a, b, n, at):
                step = 1
                while step < n:
                    dve.drain()
                    nc.vector.tensor_tensor(at(b, step, n), at(a, step, n), at(a, 0, n - step), ALU.add)
                    nc.vector.tensor_copy(at(b, 0, step), at(a, 0, step))
                    a, b, step = b, a, 2 * step
                dve.drain()
                return a

            nc.vector.tensor_copy(flat(cnt[2]), ps[5][:, 0:NT * E1])
            upto_tile = running(cnt[2], cnt[1], NT, lambda a, lo, hi: a[:, lo:hi])
            nc.vector.tensor_scalar(ntl_i, upto_tile[:, NT - 1], float(P - 1), None, ALU.add)
            dve.drain()
            nc.vector.tensor_scalar(ntl_i, ntl_i, 7, None, ALU.arith_shift_right)
            dve.drain()
            nc.vector.tensor_copy(ntl[0], ntl_i)
            nc.vector.tensor_copy(ntl[2], ntl_i)
            upto_expert = running(ntl[2], ntl[1], E1, lambda a, lo, hi: a[:, lo:hi])
            nc.vector.tensor_tensor(ntl[0], upto_expert, ntl[0], ALU.subtract)
            nc.vector.tensor_tensor(rank, rank, upto_tile, ALU.add)
            nc.vector.tensor_tensor(etmp, iota[0:1, 0:XT].unsqueeze(2).to_broadcast([1, XT, E1]),
                                    upto_expert[0:1].unsqueeze(1).to_broadcast([1, XT, E1]), ALU.is_ge)
            dve.drain()
            nc.vector.tensor_reduce(etf, etmp, AX.X, ALU.add)
            nc.vector.tensor_tensor(rank, rank, cnt[0], ALU.subtract)
            nc.vector.tensor_scalar(ntl[0], ntl[0], float(P), None, ALU.mult)
            dve.drain()
            nc.vector.tensor_scalar(etab[:, :], etf, float(E1 - 1), None, ALU.min)
            nc.vector.tensor_tensor(rank, rank, ntl[0].unsqueeze(1).to_broadcast([P, NT, E1]), ALU.add)
            dve.drain()
            for k in range(K1):
                nc.vector.tensor_tensor(prodA[:, :, k], ohA[:, :, k], rank, ALU.mult)
            dve.drain()
            nc.vector.tensor_reduce(dstA, prodA.rearrange("p n k e -> p (n k) e"), AX.X, ALU.add)
            dve.drain()
            nc.vector.tensor_copy(flat(dest1[:, :, :]), dstA)
            nc.vector.tensor_copy(dstI, dstA)
            nc.vector.tensor_copy(tileA.rearrange("p (n k) -> p n k", k=K1), tile_id[:, :].unsqueeze(2).to_broadcast([P, NT, K1]))
            dve.drain()
            nc.vector.tensor_scalar(loA, dstI, P - 1, None, ALU.bitwise_and)
            nc.vector.tensor_scalar(hiA, dstI, 7, None, ALU.arith_shift_right)
            dve.drain()
            nc.vector.tensor_tensor(ohloA, iota_bf[:, :].unsqueeze(1).to_broadcast([P, NT * K1, P]),
                                    loA.unsqueeze(2).to_broadcast([P, NT * K1, P]), ALU.is_equal)
            nc.vector.tensor_tensor(ohhiA, iota_bf[:, 0:XT].unsqueeze(1).to_broadcast([P, NT * K1, XT]),
                                    hiA.unsqueeze(2).to_broadcast([P, NT * K1, XT]), ALU.is_equal)
            dve.drain()
            nc.vector.tensor_scalar(tab5[:, :, 0:XT], ohhiA, pid[:, 0:1], None, ALU.mult)
            nc.vector.tensor_tensor(tab5[:, :, XT:2 * XT], ohhiA, tileA.unsqueeze(2).to_broadcast([P, NT * K1, XT]), ALU.mult)
            dve.drain().then_inc(table_in, 1)
            dve.wait_ge(exp5_done, 1)
            nc.vector.tensor_reduce(zA, exA, AX.X, ALU.add)
            nc.vector.tensor_scalar(sgA, sgA, 1.0, None, ALU.add)
            dve.drain()
            nc.vector.reciprocal(zA, zA)
            nc.vector.reciprocal(gate1[:, :], sgA)
            dve.drain()
            nc.vector.tensor_tensor(w4[:, :, :], w4[:, :, :], zA.unsqueeze(2).to_broadcast([P, NT, K1]), ALU.mult)
            dve.wait_ge(table_mm, 1)
            nc.vector.tensor_copy(tab5f, ps[6][:, 0:XT])
            dve.drain()
            nc.vector.scalar_tensor_tensor(idx1[:, :], ps[6][:, XT:2 * XT], float(P), tab5f, ALU.mult, ALU.add)
            stage_end(dve, 5)

            nc.vector.memset(kr[:, :, 0:WIN], 0.0)
            for u in range(2):
                nc.vector.memset(pp[u][:, :, 0:P - WIN], 0.0)
            dve.wait_ge(tabs_in, 64)

            def cosine(h, s):
                upto(dve, proj_mm, 2 * h + s)
                upto(dve, rope_done, 2 * h + s - 2)
                nc.vector.tensor_tensor(qk_c[:, s], ps[s][:, :], cos, ALU.mult).then_inc(cos_rd, 1)

            def turned(h, u, s):
                upto(dve, sin_done, 2 * h + s)
                upto(dve, sc_ps, h - 2)
                dst = qr[:, u] if s == 0 else kr[:, u, WIN:WIN + SEQ]
                nc.vector.tensor_tensor(dst, qk_c[:, s], qk_s[:, s], ALU.add).then_inc(rope_done, 1)

            def masked(h):
                upto(dve, sc_ps, h)
                upto(dve, pe_done, h - 1)
                rest(dve, "dve")
                for q in range(TPB):
                    mask = mask0 if q == 0 else mask1
                    nc.vector.tensor_tensor_reduce(out=sm[:, q], in0=ps[3 + q // 2][:, (q % 2) * KW:(q % 2 + 1) * KW], in1=mask,
                                                   scale=-SCALE, scalar=3e38, op0=ALU.add, op1=ALU.min,
                                                   accum_out=mn[:, q:q + 1])
                dve.drain().then_inc(sm_done, 1)

            def inverse(h):
                upto(dve, pe_done, h)
                upto(dve, pn_done, h - 1)
                nc.vector.reciprocal(ri, rs).then_inc(rs_done, 1)

            def probs_out(h, half):
                upto(dve, pt_ps, 2 * h + half)
                upto(dve, ot_ps, h - 1)
                nc.vector.tensor_copy(pT[:, half].rearrange("p a b c -> p (a b c)"), ps[5 + half][:, :]).then_inc(pt_rd, 1)

            for h in range(2):
                cosine(h, 0)
                cosine(h, 1)
                turned(h, h, 0)
                turned(h, h, 1)
            masked(0)
            inverse(0)

            def pair(i, last_pair):
                for k in range(2 * GH):
                    h, n, gg, hh = 2 * GH * i + k, 2 * i + k // GH, k // GH, k % GH
                    ahead = not (last_pair and k >= 2 * GH - 2)
                    if ahead:
                        cosine(h + 2, 0)
                        cosine(h + 2, 1)
                    if not (last_pair and k == 2 * GH - 1):
                        masked(h + 1)
                    probs_out(h, 0)
                    probs_out(h, 1)
                    if ahead:
                        turned(h + 2, k % 2, 0)
                        turned(h + 2, k % 2, 1)
                    if not (last_pair and k == 2 * GH - 1):
                        inverse(h + 1)
                    upto(dve, ot_ps, h)
                    nc.vector.tensor_copy(oT[gg][:, hh], ps[7][:, :]).then_inc(ot_rd, 1)
                    if hh == GH - 1:
                        for half in range(2):
                            upto(dve, op_ps, 2 * n + half)
                            a = s_sb[:, bass.ds(i // 2 * TPB + 2 * half, 2), :]
                            nc.vector.tensor_tensor(a, ps[2 if half == 0 else 7][:, :].rearrange("p (a d) -> p a d", a=2), a, ALU.add)\
                                .then_inc(op_rd, 1)
                            dve.drain()

            by_pairs(dve, pair)
            stage_end(dve, 6)

            def product(s_in, s_free, s_out, j, u):
                upto(dve, s_in, j)
                upto(dve, s_free, j - 2)
                nc.vector.tensor_tensor(h1[:, u], sg1[:, u], ps[2 + u][:, F1:2 * F1], ALU.mult).then_inc(s_out, 1)

            def routed(i, k, last_tiles):
                j = 4 * i + k
                if not (last_tiles and k == 3):
                    product(sg1_ready, h1T_ps, h1_ready, j + 1, (k + 1) % 2)
                upto(dve, y1_ps, j)
                y1_out.free(dve, j, k)
                nc.vector.tensor_copy(y1s[:, k], ps[6 + k % 2][:, 0:D]).then_inc(y1_rd, 1)

            product(sg1_ready, h1T_ps, h1_ready, 0, 0)
            with dve.Fori(0, XT // 4 - 1) as i:
                for k in range(4):
                    routed(i, k, False)
            for k in range(4):
                routed(XT // 4 - 1, k, True)

            def shared_product(n, q):
                upto(dve, sgs_ready, n)
                upto(dve, hsT_ps, n - 2)
                nc.vector.tensor_tensor(h1[:, q % 2], sg1[:, q % 2], ps[q][:, F1:2 * F1], ALU.mult).then_inc(hs_ready, 1)

            def add_routed(t, u, k):
                dve.drain()
                return nc.vector.scalar_tensor_tensor(mix1[:, u], yr[:, u, k],
                                                      w4[:, bass.ds(t, 1), k:k + 1].rearrange("p a b -> p (a b)"), mix1[:, u],
                                                      ALU.mult, ALU.add)

            def sum_up(t, u, part):
                if part == 0:
                    upto(dve, ys_ps, NS * t + NS - 1)
                    dve.wait_ge(yr_in[u], 16 * K1 // 2 * (t - u) + 16 * K1)
                    free(dve, g1_ready, t)
                    nc.vector.tensor_scalar(mix1[:, u], ps[6 + u][:, 0:D], gate1[:, bass.ds(t, 1)], None, ALU.mult)
                    add_routed(t, u, 0)
                elif part == 1:
                    add_routed(t, u, 1)
                    add_routed(t, u, 2)
                elif part == 2:
                    add_routed(t, u, 3).then_inc(sum_done, 1)
                else:
                    done(dve, g1_ready, t)
                    out_done.free(dve, t, u)
                    nc.vector.tensor_tensor(g1[:, u], g1[:, u], row(s_sb[:, bass.ds(t, 1), :]), ALU.mult)
                    dve.drain()
                    nc.vector.tensor_tensor(fin[:, u], row(x_sb[:, bass.ds(t, 1), :]), g1[:, u], ALU.add).then_inc(fin_ready, 1)

            def shared(t, u, first=False, last=False):
                for q in range(NS):
                    if not (last and q >= NS - 2):
                        shared_product(NS * t + q + 2, (q + 2) % NS)
                    if not first:
                        sum_up(t - 1, 1 - u, q)

            upto(dve, h1T_ps, XT - 1)
            shared_product(0, 0)
            shared_product(1, 1)
            over_tiles(dve, shared)
            for part in range(4):
                sum_up(NT - 1, 1, part)

        @block.gpsimd
        def _(pool):
            credit(pool, "pool")
            stage_end(pool, 0)
            with pool.Fori(0, NT // 2) as i:
                for u in range(2):
                    t = 2 * i + u
                    done(pool, qkv_rd, t)
                    free(pool, ss_ready, t)
                    a = row(qkv[:, bass.ds(t, 1), :])
                    rest(pool, "pool")
                    nc.gpsimd.tensor_tensor(sq[:, u], a, a, ALU.mult).then_inc(sq_ready, 1)
            stage_end(pool, 1)

            pool.wait_ge(nrm_rt, 1)
            with pool.Fori(0, NB) as b:
                for tt in range(TPB):
                    t, u = TPB * b + tt, tt % 2
                    free(pool, cum_ps, t)
                    if tt == 0:
                        pool.wait_ge(cum_ps, t + 2)
                    free(pool, prod_done, t)
                    rest(pool, "pool")
                    for src, dst, off in ((qkv[:, bass.ds(t, 1), 0:D], qn[:, u], 0), (qkv[:, bass.ds(t, 1), D:2 * D], kvn[:, tt], H0)):
                        nc.gpsimd.tensor_tensor(dst.rearrange("p (h k) -> p h k", h=H0), row(src).rearrange("p (h k) -> p h k", h=H0),
                                                row(ss[:, bass.ds(t, 1), off:off + H0]).unsqueeze(2).to_broadcast([P, H0, HD0]), ALU.mult)
                    pool.drain().then_inc(kvn_ready, 1)
            stage_end(pool, 2)

            with pool.Fori(0, PAIRS // 4) as i:
                for u in range(4):
                    j = 4 * i + u
                    free(pool, xgT_ps, j)
                    rest(pool, "pool")
                    nc.gpsimd.tensor_copy(ic3[:, u], idx0[:, bass.ds(j, 1)]).then_inc(ic_ready, 1)
                    done(pool, ic_ready, j, 1, 4)
                    rest(pool, "pool")
                    pool.indirect_dma_start(xg[:, u], None, xn_d, bass.IndirectOffsetOnAxis(ap=ic3[:, u], axis=0)).then_inc(xg_in[u], 16)
            stage_end(pool, 3)

            pool.wait_ge(zeroed, 1)
            with pool.Fori(0, NT // 2) as i:
                for u in range(2):
                    t = 2 * i + u
                    free(pool, mix_done, t)
                    rest(pool, "pool")
                    nc.gpsimd.tensor_copy(ic4[:, u * K0:(u + 1) * K0].rearrange("p a b -> p (a b)"),
                                          row(dest[:, bass.ds(t, 1), :])).then_inc(ic4_ready, 1)
                    done(pool, ic4_ready, t)
                    rest(pool, "pool")
                    for k in range(K0):
                        pool.indirect_dma_start(yg[:, u, k], None, y0_d, bass.IndirectOffsetOnAxis(ap=ic4[:, u * K0 + k], axis=0),
                                                bounds_check=SLOTS - 1, oob_is_err=False).then_inc(yg_in[u], 16)
            stage_end(pool, 4)
            stage_end(pool, 5)

            pool.wait_ge(tabs_in, 64)

            def sine(h):
                for s in range(2):
                    upto(pool, swap_rd, 2 * h + s)
                    rest(pool, "pool")
                    nc.gpsimd.tensor_tensor(qk_s[:, s], qk_s[:, s], sin, ALU.mult).then_inc(sin_done, 1)

            def normalized(h, u):
                upto(pool, rs_done, h)
                rest(pool, "pool")
                a = pp[u][:, :, P - WIN:2 * P]
                nc.gpsimd.tensor_tensor(a, a, ri.unsqueeze(2).to_broadcast([P, TPB, KW]), ALU.mult).then_inc(pn_done, 1)

            sine(0)
            sine(1)
            normalized(0, 0)

            def pair(i, last_pair):
                for k in range(2 * GH):
                    h = 2 * GH * i + k
                    if not (last_pair and k >= 2 * GH - 2):
                        sine(h + 2)
                    if not (last_pair and k == 2 * GH - 1):
                        normalized(h + 1, (k + 1) % 2)

            by_pairs(pool, pair)
            stage_end(pool, 6)

            with pool.Fori(0, XT // 4) as i:
                for u in range(4):
                    j = 4 * i + u
                    upto(pool, xsT_ps, j - 4)
                    rest(pool, "pool")
                    nc.gpsimd.tensor_copy(ic7[:, u:u + 1], idx1[:, bass.ds(j, 1)]).then_inc(ic7_ready, 1)
                    upto(pool, ic7_ready, j)
                    rest(pool, "pool")
                    pool.indirect_dma_start(xs[:, u], None, xn2_d, bass.IndirectOffsetOnAxis(ap=ic7[:, u:u + 1], axis=0)).then_inc(xs_in[u], 16)
            pool.wait_ge(y1_kept, 1)

            with pool.Fori(0, NT // 2) as i:
                for u in range(2):
                    t = 2 * i + u
                    free(pool, sum_done, t)
                    rest(pool, "pool")
                    nc.gpsimd.tensor_copy(ic8[:, u], row(dest1[:, bass.ds(t, 1), :])).then_inc(ic8_ready, 1)
                    done(pool, ic8_ready, t)
                    rest(pool, "pool")
                    for k in range(K1):
                        pool.indirect_dma_start(yr[:, u, k], None, y1_d, bass.IndirectOffsetOnAxis(ap=ic8[:, u, k:k + 1], axis=0)).then_inc(yr_in[u], 16)


DEBUG = ()


def kernel(**inputs):
    import concourse.bacc as bacc
    from concourse.bass_utils import run_bass_kernel_spmd

    a = {k: np.ascontiguousarray(v) for k, v in inputs.items()}
    E, I2, I = E1, 2 * F1, F1
    gu = a["L1_ffn_shared_gate_up_w"]
    shared = gu.reshape(2, NS, F1, D).transpose(1, 0, 2, 3).reshape(NS, 2 * F1, D)
    w13 = np.concatenate([a["L1_ffn_w13"], shared], 0)
    w2 = np.concatenate([a["L1_ffn_w2"].transpose(0, 2, 1), a["L1_ffn_shared_down_w"].T.reshape(NS, F1, D)], 0)
    laid = {
        "x": a["L0_attn_x"].reshape(T, D),
        "wq0": a["L0_attn_W_q"], "wkv0": a["L0_attn_W_kv"], "wo0T": a["L0_attn_W_o"].T,
        "rtT": a["L0_ffn_router_w"].T, "w_gate": a["L0_ffn_w_gate"], "w_up": a["L0_ffn_w_up"], "w_down": a["L0_ffn_w_down"],
        "norm_w": a["L1_attn_norm_w"].reshape(DC, P).T,
        "wqT": a["L1_attn_wq"].T, "wkT": a["L1_attn_wk"].T, "wvT": a["L1_attn_wv"].T, "woT": a["L1_attn_wo"].T,
        "qA": a["L1_attn_qA"], "kA": a["L1_attn_kA"], "vA": a["L1_attn_vA"], "oA": a["L1_attn_oA"],
        "qBT": a["L1_attn_qB"].T, "kBT": a["L1_attn_kB"].T, "vBT": a["L1_attn_vB"].T, "oBT": a["L1_attn_oB"].T,
        "gtT": np.concatenate([a["L1_ffn_gate_w"], a["L1_ffn_sgate_w"]], 0).T,
        "w13T": w13.transpose(2, 0, 1), "w2T": w2,
    }
    laid.update(constants())
    laid = {k: np.ascontiguousarray(v) for k, v in laid.items()}
    nc = bacc.Bacc("TRN2", target_bir_lowering=False, num_devices=1)
    io = {k: nc.dram_tensor(f"in_{k}", v.shape, F32, kind="ExternalInput").ap() for k, v in laid.items()}
    io["out"] = nc.dram_tensor("out", (T, D), F32, kind="ExternalOutput").ap()
    build(nc, io, DEBUG)
    r = run_bass_kernel_spmd(nc, [{f"in_{k}": v for k, v in laid.items()}], core_ids=[0])
    return r.results[0]["out"].reshape(NB, SEQ, D)
```

```python
from contextlib import ExitStack

import concourse.bass as bass
import numpy as np
from concourse import mybir

F32 = mybir.dt.float32
BF16 = mybir.dt.bfloat16
F16 = mybir.dt.float16
U32 = mybir.dt.uint32
I32 = mybir.dt.int32
ALU = mybir.AluOpType
ACT = mybir.ActivationFunctionType
AX = mybir.AxisListType

P = 128
T = 2048
NB, SEQ, D = 4, 512, 256
NT = T // P
TPB = SEQ // P
DC = D // P
LN_EPS = 1e-5

H0, HD0 = 16, 16
E0, K0, CAP, F0 = 64, 8, 64, 96
PAIRS = E0 // 2
SLOTS = E0 * CAP
FULL = 8192

H1, DH, RANK, WIN = 16, 128, 16, 64
GH = 4
NG = H1 // GH
SCALE = DH ** -0.5
RMS_EPS = 1e-6
E1, K1, F1, FS = 16, 4, 176, 704
FC = -(-FS // P)
XT = T * K1 // P + E1
XSLOTS = XT * P
KW = P + WIN
UP_X, UP_W = 16.0, 256.0
DOWN = 1.0 / (UP_X * UP_W)
PARTS = ((0, 0), (0, 1), (1, 0))


def constants():
    s = np.arange(P)
    c = {}
    c["ident"] = np.eye(P)
    c["tri"] = (s[:, None] <= s[None, :])
    c["tri_strict"] = (s[:, None] < s[None, :])
    c["iota"] = np.tile(s[None, :], (P, 1))
    c["pid"] = s[:, None]
    c["tile_id"] = np.tile(np.arange(NT)[None, :], (P, 1))
    n = np.arange(HD0)
    f = np.zeros((HD0, HD0))
    f[:, 0] = 0.25
    f[:, 8] = 0.25 * (-1.0) ** n
    for k in range(1, 8):
        f[:, k] = np.sqrt(2 / HD0) * np.cos(2 * np.pi * k * n / HD0)
        f[:, 8 + k] = np.sqrt(2 / HD0) * np.sin(2 * np.pi * k * n / HD0)
    back = f / 4 / np.sqrt(2)
    back[:, 0], back[:, 8] = f[:, 0] / 4, f[:, 8] / 4
    c["fwd"] = np.kron(np.eye(H0), f)
    c["back"] = np.kron(np.eye(H0), back)
    theta = (1.0 / 10000.0 ** (np.arange(DH // 2, dtype=np.float32) / np.float32(DH // 2))).astype(np.float32)
    ang = (np.arange(SEQ, dtype=np.float32)[None, :] * theta[:, None]).astype(np.float64)
    c["cos"] = DOWN * np.concatenate([np.cos(ang), np.cos(ang)], 0)
    c["sin"] = DOWN * np.concatenate([-np.sin(ang), np.sin(ang)], 0)
    q, k = s[:, None], np.arange(KW)[None, :] - WIN
    seen = (k <= q) & (k >= q - WIN + 1)
    c["mask_first"] = np.where(seen & (k >= 0), 0.0, -1e30)
    c["mask"] = np.where(seen, 0.0, -1e30)
    return {name: np.ascontiguousarray(a, dtype=np.float32) for name, a in c.items()}


def build(nc, io, dbg):
    ctx = ExitStack()
    with ctx:
        def sb(name, shape, dt=F32):
            return ctx.enter_context(nc.sbuf_tensor(name, shape, dt))

        def sem(name):
            return ctx.enter_context(nc.semaphore(name))

        def dram(name, shape, dt=F32):
            return nc.dram_tensor(name, shape, dt, kind="ExternalOutput" if name in dbg else "Internal").ap()

        xn_d = dram("xn_d", (T, D))
        y0_d = dram("y0_d", (SLOTS, D))
        wqk_d = dram("wqk_d", (NG, P, 2, DC, 512))
        xn2_d = dram("xn2_d", (T, D))
        y1_d = dram("y1_d", (XSLOTS, D))
        hT_d = dram("hT_d", (NT, P, DC, P))
        xT_d = dram("xT_d", (NT, P, DC, P))

        ident = sb("ident", [P, P])
        tri = sb("tri", [P, P])
        ones = sb("ones", [P, P])
        tri_bf = sb("tri_bf", [P, P], BF16)
        ones_bf = sb("ones_bf", [P, P], BF16)
        iota = sb("iota", [P, P])
        iota_bf = sb("iota_bf", [P, P], BF16)
        pid = sb("pid", [P, 1])
        tile_id = sb("tile_id", [P, NT])
        x_sb = sb("x_sb", [P, NT, D])
        s_sb = sb("s_sb", [P, NT, D])
        stat6 = sb("stat6", [P, NT, 6])
        st = sb("st", [P, 8, NT])
        rstd, nmr, rms, tmpa, tmpb, var = (st[:, k, :] for k in range(6))
        wqkv0 = sb("wqkv0", [P, DC, 2 * D])
        wo0 = sb("wo0", [P, DC, D])
        rtT = sb("rtT", [P, DC, E0])
        gtT = sb("gtT", [P, DC, E1 + 1])
        norm_w = sb("norm_w", [P, DC])
        UNITS = 8
        wvo = sb("wvo", [P, (2 * UNITS + 1) * 512])
        wo_raw = wvo[:, 512:(UNITS + 1) * 512].rearrange("p (h n) -> p h n", h=H1)
        wv_raw = wvo[:, (UNITS + 1) * 512:(2 * UNITS + 1) * 512].rearrange("p (c n) -> p c n", c=DC)
        wvo16 = wvo[:, 0:2 * UNITS * 512].bitcast(F16).rearrange("p (u a n) -> p u a n", u=2 * UNITS, a=2)
        norm_up = sb("norm_up", [P, DC])
        dest = sb("dest", [P, NT, K0], U32)
        w8 = sb("w8", [P, NT, K0])
        pos8 = sb("pos8", [P, NT, K0])
        zsum = sb("zsum", [P, NT])
        rz = sb("rz", [P, NT])
        idx0 = sb("idx0", [P, PAIRS], U32)
        dest1 = sb("dest1", [P, NT, K1], U32)
        w4 = sb("w4", [P, NT, K1])
        gate1 = sb("gate1", [P, NT])
        idx1 = sb("idx1", [P, XT], U32)
        etab = sb("etab", [1, XT], I32)
        ARENA = 127 * 256
        arena = sb("arena", [P, ARENA])

        class Region:
            def __init__(self):
                self.at = 0

            def take(self, parts, *shape, dt=F32):
                n = int(np.prod(shape))
                words = n if dt in (F32, U32, I32) else (n + 1) // 2
                a = arena[0:parts, self.at:self.at + words]
                self.at += words
                assert self.at <= ARENA, self.at
                if dt is not F32:
                    a = a.bitcast(dt)
                if len(shape) == 5:
                    a = a.rearrange("p (a b c d e) -> p a b c d e", a=shape[0], b=shape[1], c=shape[2], d=shape[3])
                if len(shape) == 2:
                    a = a.rearrange("p (a b) -> p a b", a=shape[0])
                if len(shape) == 3:
                    a = a.rearrange("p (a b c) -> p a b c", a=shape[0], b=shape[1])
                if len(shape) == 4:
                    a = a.rearrange("p (a b c d) -> p a b c d", a=shape[0], b=shape[1], c=shape[2])
                return a

        ps = [ctx.enter_context(nc.psum_tensor(f"ps{k}", [P, 512], F32)) for k in range(8)]

        turn = {e: sem(f"turn_{e}") for e in ("pe", "act", "dve", "pool", "sp")}
        stage = sem("stage")
        STAGES = [0]

        def rest(eng, name):
            eng.sem_inc(turn[name], 1)

        def stage_end(eng, k):
            eng.drain().then_inc(stage, 1)
            eng.wait_ge(stage, 5 * (k + 1))

        CR = 2

        def done(eng, s, t, per=1, cr=CR):
            eng.wait_ge(s, (t + 1 + cr) * per)

        def free(eng, s, t, per=1, cr=CR):
            eng.wait_ge(s, (t + 1) * per)

        AHEAD = 4
        HC1 = NT * K1 // 2
        LORA_ORDER = (2, 0, 1)

        def upto(eng, s, k):
            eng.wait_ge(s, k + 1 + AHEAD)

        names = {}

        def loop_sem(name, by, per=1, cr=CR):
            s = sem(name)
            names.setdefault(by, []).append((s, per * cr))
            return s

        class Landed:

            def __init__(self, name, n=1, buffers=2):
                self.s = [loop_sem(f"{name}{u}", "sp", 16 * n, 1) for u in range(buffers)]
                self.n, self.buffers = n, buffers

            def done(self, eng, t, u):
                eng.wait_ge(self.s[u], 16 * self.n // self.buffers * (t - u) + 32 * self.n)

            def free(self, eng, t, u):
                eng.wait_ge(self.s[u], 16 * self.n // self.buffers * (t - u) + 16 * self.n)

        consts_in, w0_in, wvo_in, wqk_in, lora_in, w0_mm = (
            sem(n) for n in ("consts_in", "w0_in", "wvo_in", "wqk_in", "lora_in", "w0_mm"))
        lora_mm, lora_add, hi_done, lo_done, wqk_out = (sem(n) for n in ("lora_mm", "lora_add", "hi_done", "lo_done", "wqk_out"))
        x_in = sem("x_in")
        var_ready, std_ready, stats_ready = sem("var_ready"), sem("std_ready"), sem("stats_ready")
        xn_ready = loop_sem("xn_ready", "act")
        xn_stored = Landed("xn_stored")
        xnT_ps = loop_sem("xnT_ps", "pe")
        xnT_rd = loop_sem("xnT_rd", "act")
        qkv_ps = loop_sem("qkv_ps", "pe")
        qkv_rd = loop_sem("qkv_rd", "act")
        lg_rd = loop_sem("lg_rd", "dve")
        sq_ready = loop_sem("sq_ready", "pool")
        ss_ready = loop_sem("ss_ready", "dve")
        nrm_sq = sem("nrm_sq")
        chosen0, counted0, exp0_in, exp0_done, ohhi0_ready, table0_in, table0_mm = (
            sem(n) for n in ("chosen0", "counted0", "exp0_in", "exp0_done", "ohhi0_ready", "table0_in", "table0_mm"))
        qkn_ready = loop_sem("qkn_ready", "pool", 1, AHEAD)
        cum_ps = loop_sem("cum_ps", "pe", 1, AHEAD)
        cum_rd = loop_sem("cum_rd", "act", 1, AHEAD)
        y_ready = loop_sem("y_ready", "pool", 1, AHEAD)
        yT_ps = loop_sem("yT_ps", "pe", 1, AHEAD)
        yT_rd = loop_sem("yT_rd", "act", 1, AHEAD)
        s0_ps = loop_sem("s0_ps", "pe", 1, AHEAD)
        s0_rd = loop_sem("s0_rd", "act", 1, AHEAD)
        ic_ready = loop_sem("ic_ready", "pool", 1, AHEAD)
        xg_in = [sem(f"xg_in{u}") for u in range(4)]
        we_in = Landed("we_in", 3, 4)
        xgT_ps = loop_sem("xgT_ps", "pe", 1, AHEAD)
        xgT_rd = loop_sem("xgT_rd", "act", 1, AHEAD)
        gu_ps = loop_sem("gu_ps", "pe", 1, AHEAD)
        sg_ready = loop_sem("sg_ready", "act", 1, AHEAD)
        hm_ready = loop_sem("hm_ready", "dve", 1, AHEAD)
        y0_ps = loop_sem("y0_ps", "pe", 1, AHEAD)
        y0_rd = loop_sem("y0_rd", "dve", 1, AHEAD)
        y0_out = Landed("y0_out", 1, 4)
        ic4_ready = loop_sem("ic4_ready", "pool", 1, AHEAD)
        yg_in = [sem(f"yg_in{u}") for u in range(4)]
        zeroed = sem("zeroed")
        mix_begun = loop_sem("mix_begun", "act")
        mix_done = loop_sem("mix_done", "dve", 1, AHEAD)
        g_ready = loop_sem("g_ready", "act")
        x1_done = loop_sem("x1_done", "dve")
        ohhi_ready = sem("ohhi_ready")
        xn2_ready = loop_sem("xn2_ready", "act")
        xn2_kept = loop_sem("xn2_kept", "dve")
        xn2_out = Landed("xn2_out")
        tr5_ps = loop_sem("tr5_ps", "pe")
        tr5_rd = loop_sem("tr5_rd", "act")
        h_lo = loop_sem("h_lo", "dve")
        tr5_out = Landed("tr5_out", 2)
        lg5_ps = loop_sem("lg5_ps", "pe")
        lg5_rd = loop_sem("lg5_rd", "dve")
        chosen, counted, exp5_in, exp5_done, table_in, table_mm = (
            sem(n) for n in ("chosen", "counted", "exp5_in", "exp5_done", "table_in", "table_mm"))
        tabs_in = sem("tabs_in")
        h_in = Landed("h_in", 2)
        proj_mm = loop_sem("proj_mm", "pe", 1, AHEAD)
        swap_rd = loop_sem("swap_rd", "act", 1, AHEAD)
        cos_rd = loop_sem("cos_rd", "dve", 1, AHEAD)
        sin_done = loop_sem("sin_done", "pool", 1, AHEAD)
        rope_done = loop_sem("rope_done", "dve", 1, AHEAD)
        v_ps = loop_sem("v_ps", "pe", 1, AHEAD)
        v_rd = loop_sem("v_rd", "act", 1, AHEAD)
        sc_ps = loop_sem("sc_ps", "pe", 1, AHEAD)
        sm_done = loop_sem("sm_done", "dve", 1, AHEAD)
        pe_done = loop_sem("pe_done", "act", 1, AHEAD)
        pn_done = loop_sem("pn_done", "pool", 1, AHEAD)
        rs_done = loop_sem("rs_done", "dve", 1, AHEAD)
        pt_ps = loop_sem("pt_ps", "pe", 1, AHEAD)
        pt_rd = [loop_sem("pt_rd0", "act", 1, AHEAD), loop_sem("pt_rd1", "dve", 1, AHEAD)]
        ot_ps = loop_sem("ot_ps", "pe", 1, AHEAD)
        ot_rd = loop_sem("ot_rd", "dve", 1, AHEAD)
        op_ps = loop_sem("op_ps", "pe", 1, AHEAD)
        op_rd = loop_sem("op_rd", "dve", 1, AHEAD)
        w13_in, w2_in = sem("w13_in"), sem("w2_in")
        ic7_ready = loop_sem("ic7_ready", "pool", 1, AHEAD)
        xs_in = [sem(f"xs_in{u}") for u in range(4)]
        xsT_ps = loop_sem("xsT_ps", "pe", 1, AHEAD)
        xsT_rd = loop_sem("xsT_rd", "act", 1, AHEAD)
        xs_lo = loop_sem("xs_lo", "dve", 1, AHEAD)
        gu1_ps = loop_sem("gu1_ps", "pe", 1, AHEAD)
        sg1_ready = loop_sem("sg1_ready", "act", 1, AHEAD)
        h1_ready = loop_sem("h1_ready", "dve", 1, AHEAD)
        h1T_ps = loop_sem("h1T_ps", "pe", 1, AHEAD)
        h1T_rd = loop_sem("h1T_rd", "act", 1, AHEAD)
        y1_ps = loop_sem("y1_ps", "pe", 1, AHEAD)
        y1_rd = loop_sem("y1_rd", "dve", 1, AHEAD)
        y1_out = Landed("y1_out", 1, 4)
        y1_kept = sem("y1_kept")
        ffn_in = sem("ffn_in")
        xb_in = [sem(f"xb_in{u}") for u in range(2)]
        xb_used = loop_sem("xb_used", "pe", 1, AHEAD)
        gus_ps = loop_sem("gus_ps", "pe", 1, AHEAD)
        sgs_ready = loop_sem("sgs_ready", "act", 1, AHEAD)
        hs_ready = loop_sem("hs_ready", "dve", 1, AHEAD)
        ys_ps = loop_sem("ys_ps", "pe", 1, AHEAD)
        ys_rd = loop_sem("ys_rd", "dve", 1, AHEAD)
        ic8_ready = loop_sem("ic8_ready", "pool")
        yr_in = [sem(f"yr_in{u}") for u in range(2)]
        sum_done = loop_sem("sum_done", "dve")
        yr_used = loop_sem("yr_used", "dve")
        g1_ready = loop_sem("g1_ready", "act")
        fin_ready = loop_sem("fin_ready", "dve")
        out_done = Landed("out_done")

        NC0 = NT * K0
        R1 = Region()
        qkv = R1.take(P, NT, 2 * D)
        ss = R1.take(P, NT, 2 * H0)
        lgA0 = R1.take(P, NT, E0)
        mxA0 = R1.take(P, NT, K0)
        idA0 = R1.take(P, NC0)
        exA0 = lgA0
        ex8 = R1.take(P, NT, K0)
        dstA0 = R1.take(P, NC0)
        badA0 = R1.take(P, NC0)
        tileA0 = R1.take(P, NC0)
        dstI0 = R1.take(P, NC0, dt=I32)
        loA0 = R1.take(P, NC0, dt=I32)
        hiA0 = R1.take(P, NC0, dt=I32)
        tabf = R1.take(P, PAIRS)
        at_ohe = R1.at
        ohe = R1.take(P, NT, K0, E0, dt=BF16)
        at_prod = R1.at
        prod = R1.take(P, NT, K0, E0)
        at_ohhi = R1.at
        ohhi = R1.take(P, NC0, PAIRS, dt=BF16)
        at_s2 = R1.at
        cs = R1.take(P, 2, D)
        pa = R1.take(P, D)
        pb = R1.take(P, D)
        yy = R1.take(P, 2, D)
        yT = R1.take(P, 2, DC, P)
        at_w = R1.at
        wgu_e = R1.take(P, 4, 2 * 2 * DC, F0)
        wd_e = R1.take(F0, 4, 2, D)
        R1.at = at_ohe
        tab_rhs = R1.take(P, NC0, 2 * PAIRS, dt=BF16)
        R1.at = at_prod
        ohlo = R1.take(P, NC0, P, dt=BF16)
        R1.at = at_prod
        assert R1.at <= at_ohhi
        R1.at = at_ohhi
        mk0 = R1.take(P, NT, E0, dt=BF16)
        R1.at = at_prod
        ohs = [R1.take(P, NT, K0 // 2, E0, dt=BF16), R1.take(P, NT, K0 // 4, E0, dt=BF16)]
        R1.at = at_s2
        xn = R1.take(P, 2, D)
        xnT = R1.take(P, 2, DC, P)
        sq = R1.take(P, 2, 2 * D)
        assert R1.at <= at_w
        R1.at = at_ohe
        lg = R1.take(P, 2, E0)
        mx = R1.take(P, 2, 8)
        mi = R1.take(P, 2, 8, dt=U32)
        w0_raw = R1.take(P, 3, DC, D)
        fwd = R1.take(P, DC, D)
        back = R1.take(P, DC, D)

        R3 = Region()
        wqk_parts = R3.take(P, 2, DC, UNITS // DC, 512)
        R3.at = 0
        wqk16 = R3.take(P, 2 * UNITS, 2, 512, dt=F16)
        R3.at = 512
        wqk_raw = R3.take(P, 2, DC, H1 * DH)
        lora_a = R3.take(2 * 32 + RANK, D)
        lora_b = R3.take(2 * 32 + RANK, H1 * DH)
        lora_oa = R3.take(RANK, H1 * DH)
        lora_ob = R3.take(RANK, D)
        at_end_w = R3.at
        ic3 = R3.take(P, 4, 1, dt=U32)
        xg = R3.take(P, 4, D)
        xgT = R3.take(P, 4, DC, P)
        sg0 = R3.take(F0, 4, P)
        hm0 = R3.take(F0, 4, P)
        y0 = R3.take(P, 4, D)
        assert R3.at <= at_w

        R5 = Region()
        R5.at = at_end_w
        ic4 = R5.take(P, 4 * K0, 1, dt=U32)
        mix = R5.take(P, 2, D)
        xn2 = R5.take(P, 2, D)
        at_hh2 = R5.at
        hh2 = R5.take(P, 2, D)
        R5.at = at_hh2
        xnT5 = R5.take(P, 2, DC, P)
        at_tr5 = R5.at
        tr5 = R5.take(P, 2, 2, 2, P)
        R5.at = at_tr5
        tr16 = R5.take(P, 2, 2, 2 * D, dt=F16)
        lg5 = R5.take(P, 2, E1 + 1)
        mx5 = R5.take(P, 2, 8)
        mi5 = R5.take(P, 2, 8, dt=U32)
        lgA = R5.take(P, NT, E1 + 1)
        mxA = R5.take(P, NT, K1)
        idA = R5.take(P, NT, K1)
        at_yg = R5.at
        yg = R5.take(P, 4, K0, D)
        assert R3.at <= at_yg + K0 * D and R5.at <= at_w
        end_of_4 = R5.at
        R5.at = 0
        exA = R5.take(P, NT, E1)
        zA = R5.take(P, NT)
        sgA = R5.take(P, NT)
        ohA = R5.take(P, NT, K1, E1, dt=BF16)
        mkA = R5.take(P, NT, E1, dt=BF16)
        cnt = [R5.take(P, NT, E1) for _ in range(3)]
        rank = R5.take(P, NT, E1)
        ntl_i = R5.take(P, E1, dt=I32)
        ntl = [R5.take(P, E1) for _ in range(3)]
        prodA = R5.take(P, NT, K1, E1)
        dstA = R5.take(P, NT * K1)
        tileA = R5.take(P, NT * K1)
        dstI = R5.take(P, NT * K1, dt=I32)
        loA = R5.take(P, NT * K1, dt=I32)
        hiA = R5.take(P, NT * K1, dt=I32)
        ohhiA = R5.take(P, NT * K1, XT, dt=BF16)
        tab5 = R5.take(P, NT * K1, 2 * XT, dt=BF16)
        tab5f = R5.take(P, XT)
        etmp = R5.take(1, XT, E1)
        etf = R5.take(1, XT)
        assert R5.at <= at_end_w
        R5.at = at_yg
        ohloA = R5.take(P, NT * K1, P, dt=BF16)

        R6 = Region()
        qk_c = R6.take(P, 2, SEQ)
        qk_s = R6.take(P, 2, SEQ)
        qr = R6.take(P, 2, SEQ)
        kr = R6.take(P, 2, WIN + SEQ)
        vv = [R6.take(P, TPB, GH * DH) for _ in range(2)]
        sm = R6.take(P, TPB, KW)
        mn = R6.take(P, TPB)
        pp = [R6.take(P, TPB, 2 * P) for _ in range(2)]
        rs = R6.take(P, TPB)
        ri = R6.take(P, TPB)
        pT = R6.take(P, 2, 2 * KW)
        oT = [R6.take(P, 2, GH, SEQ, dt=F16) for _ in range(2)]
        R6_gap = R6.at
        R6.at = max(R6.at, end_of_4)
        R6_tail = R6.at
        cos = R6.take(P, SEQ)
        sin = R6.take(P, SEQ)
        mask0 = R6.take(P, KW)
        mask1 = R6.take(P, KW)
        at_group = R6.at
        wqk_f = [R6.take(P, 2, DC, 512) for _ in range(2)]
        hT_f = [R6.take(P, TPB, DC, P) for _ in range(2)]
        R6.at = at_group
        wqk = [R6.take(P, 2 * DC, 2, 512, dt=F16) for _ in range(2)]
        hT = [R6.take(P, TPB, 2, DC, P, dt=F16) for _ in range(2)]

        R7 = Region()
        GU = DC * 2 * F1
        w13 = R7.take(P, E1, 2, GU, dt=F16)
        R7.at = 2 * GU
        w13_raw = R7.take(P, E1, DC, 2 * F1)
        w2a = R7.take(P, E1, D)
        R7.at = max(R7.at, R6_gap)
        SGU = 2 * DC
        at_sgw = R7.at
        sgw16 = R7.take(P, SGU, 2, FS, dt=F16)
        R7.at = at_sgw + FS
        sgw = R7.take(P, SGU, FS)
        sdw = R7.take(P, FC, D)
        at_xb = R7.at
        xb = R7.take(P, 2, TPB, 2, P)
        R7.at = at_xb
        xb16 = R7.take(P, 2, TPB, 2, DC * P, dt=F16)
        assert R7.at <= R6_tail
        hsT = R7.take(P, FC, SEQ)
        w2b = R7.take(F1 - P, E1, D)
        sgs = R7.take(P, 2, SEQ)
        sg1 = R7.take(P, 2, F1)
        wv_flat, wo_flat = wvo[:, 0:UNITS * 512], wvo[:, UNITS * 512:(2 * UNITS + 1) * 512]
        xs = wv_flat[:, 0:4 * D].rearrange("p (u d) -> p u d", u=4)
        y1s = wv_flat[:, 4 * D:8 * D].rearrange("p (u d) -> p u d", u=4)
        yr = wv_flat[:, 8 * D:16 * D].rearrange("p (u k d) -> p u k d", u=2, k=K1)
        xsT = wo_flat[:, 0:4 * D].bitcast(F16).rearrange("p (u a n) -> p u a n", u=4, a=2)
        mix1 = wo_flat[:, 4 * D:6 * D].rearrange("p (u d) -> p u d", u=2)
        h1T = wo_flat[:, 8 * D:10 * D].rearrange("p (u n) -> p u n", u=2)
        g1 = wo_flat[:, 10 * D:12 * D].rearrange("p (u d) -> p u d", u=2)
        fin = wo_flat[:, 6 * D:8 * D].rearrange("p (u d) -> p u d", u=2)
        ic7 = sb("ic7", [P, 4], U32)
        ic8 = sb("ic8", [P, 2, K1], U32)
        h1 = wo_flat[:, 12 * D:12 * D + 2 * F1].rearrange("p (u n) -> p u n", u=2)
        sh0 = wo_flat[:, 12 * D + 2 * F1:16 * D + 2 * F1].rearrange("p (n d) -> p n d", n=TPB)

        block = ctx.enter_context(nc.Block())

        NPAIR = NB * NG // 2

        def by_pairs(eng, body):
            with eng.Fori(0, NPAIR - 1) as i:
                body(i, False)
            body(NPAIR - 1, True)

        def unit(n):
            if n < 2 * UNITS:
                return wvo[:, 512 * (n + 1):512 * (n + 2)], wvo16[:, n]
            n -= 2 * UNITS
            return arena[:, 512 * (n + 1):512 * (n + 2)], wqk16[:, n]

        def unit_scale(n):
            return UP_W if n < UNITS else norm_up[:, n // 4 % 2:n // 4 % 2 + 1]

        SUM_AFTER = ((None, None, 0, 1), (2, 3, 4, 5))

        SPLIT_AFTER = [range(0), range(0), range(0), range(0, 2), range(2, 4), range(4, E1)]
        assert len(SPLIT_AFTER) == FC

        GT = 4

        def by_groups(begin, finish, low_rank, between, follow_a, follow_b):
            for t in range(NT):
                begin(t)
                if t >= GT:
                    follow_a(t - GT, t % 2)
                    follow_b(t - GT, t % 2)
                finish(t, t % 2)
                low_rank(t)
                if t % GT == GT - 1:
                    between(t // GT)
            rest_of = range(NT - GT, NT)
            for t in rest_of:
                follow_a(t, t % 2)
                if t > rest_of[0]:
                    follow_b(t - 1, (t - 1) % 2)
            follow_b(NT - 1, 1)

        def over_tiles(eng, body):
            body(0, 0, first=True)
            with eng.Fori(0, NT // 2 - 1) as i:
                body(2 * i + 1, 1)
                body(2 * i + 2, 0)
            body(NT - 1, 1, last=True)

        def flat(a):
            return a.rearrange("p a b -> p (a b)")

        def row(a):
            return a.rearrange("p a b -> p (a b)")

        def credit(eng, name):
            for s, n in names.get(name, []):
                eng.sem_inc(s, n)

        def pipelined(front, back, eng):
            front(0, 0)
            with eng.Fori(0, NT // 2 - 1) as i:
                front(2 * i + 1, 1)
                back(2 * i, 0)
                front(2 * i + 2, 0)
                back(2 * i + 1, 1)
            front(NT - 1, 1)
            back(NT - 2, 0)
            back(NT - 1, 1)

        @block.sync
        def _(sp):
            credit(sp, "sp")
            sp.dma_start(x_sb[:, :, :], io["x"].rearrange("(n p) d -> p n d", p=P)).then_inc(x_in, 16)
            for k, name in enumerate(("wq0", "wkv0", "wo0T")):
                sp.dma_start(w0_raw[:, k], io[name].rearrange("(c p) n -> p c n", p=P)).then_inc(w0_in, 16)
            sp.dma_start(fwd, io["fwd"].rearrange("(c p) n -> p c n", p=P)).then_inc(w0_in, 16)
            sp.dma_start(back, io["back"].rearrange("(c p) n -> p c n", p=P)).then_inc(w0_in, 16)
            for t, name in ((ident, "ident"), (tri, "tri"), (iota, "iota"), (pid, "pid"), (tile_id, "tile_id"), (norm_w, "norm_w")):
                sp.dma_start(t[:, :], io[name]).then_inc(consts_in, 16)
            sp.dma_start(rtT[:, :, :], io["rtT"].rearrange("(c p) n -> p c n", p=P)).then_inc(consts_in, 16)
            sp.dma_start(gtT[:, :, :], io["gtT"].rearrange("(c p) n -> p c n", p=P)).then_inc(consts_in, 16)
            sp.dma_start(wv_raw, io["wvT"].rearrange("(c p) n -> p c n", p=P)).then_inc(wvo_in, 16)
            sp.dma_start(wo_raw, io["woT"].rearrange("(h p) n -> p h n", p=P)).then_inc(wvo_in, 16)
            stage_end(sp, 0)

            with sp.Fori(0, NT // 2) as i:
                for u in range(2):
                    t = 2 * i + u
                    done(sp, xn_ready, t)
                    sp.dma_start(xn_d[bass.ds(t * P, P), :], xn[:, u]).then_inc(xn_stored.s[u], 16)
            for u in range(2):
                xn_stored.done(sp, NT - 2 + u, u)
            stage_end(sp, 1)

            def load_experts(j, u):
                upto(sp, y0_ps, j - 4)
                for g, name in ((0, "w_gate"), (1, "w_up")):
                    sp.dma_start(wgu_e[:, u, 4 * g:4 * g + 4, :],
                                 io[name][bass.ds(2 * j, 2)].rearrange("e (c p) f -> p (e c) f", p=P)).then_inc(we_in.s[u], 16)
                sp.dma_start(wd_e[:, u], io["w_down"][bass.ds(2 * j, 2)].rearrange("e f d -> f e d")).then_inc(we_in.s[u], 16)

            def store_outputs(j, u):
                upto(sp, y0_rd, j)
                sp.dma_start(y0_d[bass.ds(j * P, P), :], y0[:, u]).then_inc(y0_out.s[u], 16)

            for j in range(3):
                load_experts(j, j)
            stage_end(sp, 2)
            with sp.Fori(0, PAIRS // 4 - 1) as i:
                for k in range(4):
                    load_experts(4 * i + k + 3, (k + 3) % 4)
                    store_outputs(4 * i + k, k)
            for k in range(4):
                if k == 0:
                    load_experts(PAIRS - 1, 3)
                    sp.dma_start(lora_oa, io["oA"]).then_inc(lora_in, 16)
                    sp.dma_start(lora_ob, io["oBT"]).then_inc(lora_in, 16)
                    for j, (an, bn) in ((2, ("vA", "vBT")), (0, ("qA", "qBT")), (1, ("kA", "kBT"))):
                        sp.dma_start(lora_a[32 * j:32 * j + RANK, :], io[an]).then_inc(lora_in, 16)
                        sp.dma_start(lora_b[32 * j:32 * j + RANK, :], io[bn]).then_inc(lora_in, 16)
                    for j, wn in enumerate(("wqT", "wkT")):
                        sp.dma_start(wqk_raw[:, j], io[wn].rearrange("(c p) n -> p c n", p=P)).then_inc(wqk_in, 16)
                store_outputs(PAIRS - 4 + k, k)
            for u in range(4):
                y0_out.done(sp, PAIRS - 4 + u, u)
            stage_end(sp, 3)

            for dst, name in ((cos, "cos"), (sin, "sin"), (mask0, "mask_first"), (mask1, "mask")):
                sp.dma_start(dst, io[name]).then_inc(tabs_in, 16)
            with sp.Fori(0, NT // 2) as i:
                for u in range(2):
                    t = 2 * i + u
                    done(sp, xn2_ready, t)
                    sp.dma_start(xn2_d[bass.ds(t * P, P), :], xn2[:, u]).then_inc(xn2_out.s[u], 16)
                    done(sp, tr5_rd, t)
                    done(sp, h_lo, t)
                    sp.dma_start(hT_d[bass.ds(t, 1)].rearrange("a p c n -> p (a c) n"), tr5[:, u, :, 0]).then_inc(tr5_out.s[u], 16)
                    sp.dma_start(xT_d[bass.ds(t, 1)].rearrange("a p c n -> p (a c) n"), tr5[:, u, :, 1]).then_inc(tr5_out.s[u], 16)
            for u in range(2):
                xn2_out.done(sp, NT - 2 + u, u)
                tr5_out.done(sp, NT - 2 + u, u)

            def load_group(n, g, b, gg):
                sp.dma_start(wqk_f[gg], wqk_d[bass.ds(g, 1)].rearrange("a p s c n -> p (a s) c n")).then_inc(h_in.s[gg], 16)
                sp.dma_start(hT_f[gg], hT_d[bass.ds(b * TPB, TPB)].rearrange("n p c t -> p n c t")).then_inc(h_in.s[gg], 16)

            sp.wait_ge(wqk_out, 16 * 8)
            for gg in range(2):
                load_group(gg, gg, 0, gg)
            stage_end(sp, 4)

            def load_batch(b):
                sp.dma_start(xb[:, b % 2], xT_d[b * TPB:(b + 1) * TPB].rearrange("n p c t -> p n c t")).then_inc(xb_in[b % 2], 16)

            load_batch(0)
            load_batch(1)
            sp.dma_start(sgw.rearrange("p (c g) f -> p c (g f)", c=DC), io["sguT"].rearrange("(c p) f -> p c f", p=P)).then_inc(ffn_in, 16)
            sp.dma_start(sdw[:, 0:FC - 1], io["sdT"][0:(FC - 1) * P, :].rearrange("(c p) d -> p c d", p=P)).then_inc(ffn_in, 16)
            sp.dma_start(sdw[0:FS - (FC - 1) * P, FC - 1], io["sdT"][(FC - 1) * P:FS, :]).then_inc(ffn_in, 16)

            with sp.Fori(1, NPAIR) as i:
                for gg in range(2):
                    upto(sp, proj_mm, 2 * GH * (2 * i + gg - 1) - 1)
                    load_group(2 * i + gg, 2 * (i % 2) + gg, i // 2, gg)
            stage_end(sp, 5)

            for half, landed in ((slice(0, E1 // 2), ffn_in), (slice(E1 // 2, E1), w13_in)):
                for c in range(DC):
                    sp.dma_start(w13_raw[:, half, c], io["w13T"][c * P:(c + 1) * P, half]).then_inc(landed, 16)
            sp.dma_start(w2a, io["w2T"][:, 0:P, :].rearrange("e f d -> f e d")).then_inc(w2_in, 16)
            sp.dma_start(w2b, io["w2T"][:, P:F1, :].rearrange("e f d -> f e d")).then_inc(w2_in, 16)
            upto(sp, xb_used, 0)
            load_batch(2)
            with sp.Fori(0, XT // 4) as i:
                for u in range(4):
                    j = 4 * i + u
                    upto(sp, y1_rd, j)
                    sp.dma_start(y1_d[bass.ds(j * P, P), :], y1s[:, u]).then_inc(y1_out.s[u], 16)
            for u in range(4):
                y1_out.done(sp, XT - 4 + u, u)
            sp.sem_inc(y1_kept, 1)

            def store_out(t, u):
                done(sp, fin_ready, t)
                sp.dma_start(io["out"][bass.ds(t * P, P), :], fin[:, u]).then_inc(out_done.s[u], 16)

            for t in range(TPB):
                store_out(t, t % 2)
            upto(sp, xb_used, 1)
            load_batch(3)
            with sp.Fori(TPB // 2, NT // 2) as i:
                for u in range(2):
                    store_out(2 * i + u, u)
            for u in range(2):
                out_done.done(sp, NT - 2 + u, u)

        @block.tensor
        def _(pe):
            credit(pe, "pe")
            pe.wait_ge(consts_in, 16 * 8)
            pe.wait_ge(w0_in, 80)
            for m in range(DC):
                for k, at in ((0, 0), (1, D)):
                    for c in range(DC):
                        pe.matmul(ps[m][:, at:at + D], w0_raw[:, k, c, m * P:(m + 1) * P], fwd[:, c],
                                  start=(c == 0), stop=(c == DC - 1))
                for c in range(DC):
                    last = pe.matmul(ps[2 + m][:, 0:D], back[:, c, m * P:(m + 1) * P], w0_raw[:, 2, c],
                                     start=(c == 0), stop=(c == DC - 1))
            last.then_inc(w0_mm, 1)
            stage_end(pe, 0)

            def front(t, u):
                done(pe, xn_ready, t)
                free(pe, xnT_rd, t)
                for c in range(DC):
                    last = pe.transpose(ps[u][:, c * P:(c + 1) * P], xn[:, u, c * P:(c + 1) * P], ident[:, :])
                last.then_inc(xnT_ps, 1)

            def back_(t, u):
                done(pe, xnT_rd, t)
                free(pe, lg_rd, t)
                for c in range(DC):
                    pe.matmul(ps[4 + u][:, 0:E0], xnT[:, u, c], rtT[:, c, :], start=(c == 0), stop=(c == DC - 1))
                free(pe, qkv_rd, t)
                for c in range(DC):
                    last = pe.matmul(ps[2 + u][:, :], xnT[:, u, c], wqkv0[:, c, :], start=(c == 0), stop=(c == DC - 1))
                last.then_inc(qkv_ps, 1)

            pipelined(front, back_, pe)
            stage_end(pe, 1)

            def running_sum(b, tt):
                t = TPB * b + tt
                upto(pe, qkn_ready, t)
                upto(pe, cum_rd, t - 2)
                out = ps[tt % 2][:, 0:D]
                for j in range(tt):
                    pe.matmul(out, ones[:, :], row(qkv[:, bass.ds(TPB * b + j, 1), D:2 * D]), start=(j == 0), stop=False)
                pe.matmul(out, tri[:, :], row(qkv[:, bass.ds(t, 1), D:2 * D]), start=(tt == 0), stop=True).then_inc(cum_ps, 1)

            def spectral(b, last_batch):
                for tt in range(TPB):
                    t, u = TPB * b + tt, tt % 2
                    upto(pe, y_ready, t)
                    upto(pe, yT_rd, t - 2)
                    for c in range(DC):
                        last = pe.transpose(ps[2 + u][:, c * P:(c + 1) * P], yy[:, u, c * P:(c + 1) * P], ident[:, :])
                    last.then_inc(yT_ps, 1)
                    if not (last_batch and tt >= TPB - 2):
                        running_sum(b + (tt + 2) // TPB, (tt + 2) % TPB)
                    upto(pe, yT_rd, t)
                    upto(pe, s0_rd, t - 2)
                    for c in range(DC):
                        last = pe.matmul(ps[4 + u][:, 0:D], yT[:, u, c], wo0[:, c, :], start=(c == 0), stop=(c == DC - 1))
                    last.then_inc(s0_ps, 1)

            running_sum(0, 0)
            running_sum(0, 1)
            spectral(0, False)
            pe.wait_ge(chosen0, 1)
            HALF = NT // 2
            for half in range(2):
                counts = ps[6 + half]
                pe.matmul(counts[:, :], tri_bf[:, :], flat(mk0[:, half * HALF:(half + 1) * HALF]), start=True, stop=False,
                          skip_group_check=True)
                for n in range(half * HALF + HALF - 1):
                    to = max(n + 1 - half * HALF, 0)
                    last = pe.matmul(counts[:, to * E0:HALF * E0], ones_bf[:, :], mk0[:, n:n + 1].to_broadcast([P, HALF - to, E0]),
                                     start=False, stop=(n == half * HALF + HALF - 2), skip_group_check=True)
            last.then_inc(counted0, 1)
            with pe.Fori(1, NB - 1) as b:
                spectral(b, False)
            spectral(NB - 1, True)
            pe.wait_ge(table0_in, 2)
            for n in range(NC0):
                last = pe.matmul(ps[6][:, 0:2 * PAIRS], ohlo[:, n], tab_rhs[:, n], start=(n == 0), stop=(n == NC0 - 1))
            last.then_inc(table0_mm, 1)
            stage_end(pe, 2)

            def expert_rows(i, j, u):
                pe.wait_ge(xg_in[u], 16 * (i + 1))
                upto(pe, xgT_rd, j - 2)
                for c in range(DC):
                    last = pe.transpose(ps[u % 2][:, c * P:(c + 1) * P], xg[:, u, c * P:(c + 1) * P], ident[:, :])
                last.then_inc(xgT_ps, 1)

            def expert_up(j, u):
                we_in.done(pe, j, u)
                upto(pe, xgT_rd, j)
                upto(pe, hm_ready, j - 2)
                for g in range(2):
                    for e in range(2):
                        at = (2 * g + e) * CAP
                        for c in range(DC):
                            last = pe.matmul(ps[2 + u % 2][0:F0, at:at + CAP], wgu_e[:, u, 4 * g + 2 * e + c],
                                             xgT[:, u, c, e * CAP:(e + 1) * CAP], start=(c == 0), stop=(c == DC - 1))
                last.then_inc(gu_ps, 1)

            def experts(i, k, last_pairs):
                j = 4 * i + k
                if not (last_pairs and k >= 2):
                    expert_rows(i + (k + 2) // 4, j + 2, (k + 2) % 4)
                if not (last_pairs and k == 3):
                    expert_up(j + 1, (k + 1) % 4)
                upto(pe, hm_ready, j)
                upto(pe, y0_rd, j - 2)
                for e in range(2):
                    last = pe.matmul(ps[4 + k % 2][e * CAP:(e + 1) * CAP, 0:D], hm0[:, k, e * CAP:(e + 1) * CAP],
                                     wd_e[:, k, e], start=True, stop=True)
                last.then_inc(y0_ps, 1)

            expert_rows(0, 0, 0)
            expert_rows(0, 1, 1)
            expert_up(0, 0)
            with pe.Fori(0, PAIRS // 4 - 1) as i:
                for k in range(4):
                    experts(i, k, False)
            for k in range(4):
                experts(PAIRS // 4 - 1, k, True)
            stage_end(pe, 3)

            def follow_a(t, u):
                done(pe, xn2_ready, t)
                free(pe, tr5_rd, t)
                free(pe, h_lo, t)
                for k, a in ((0, hh2), (1, xn2)):
                    for c in range(DC):
                        last = pe.transpose(ps[u][:, (2 * k + c) * P:(2 * k + c + 1) * P], a[:, u, c * P:(c + 1) * P], ident[:, :])
                last.then_inc(tr5_ps, 1)

            def follow_b(t, u):
                done(pe, tr5_rd, t)
                free(pe, lg5_rd, t)
                for c in range(DC):
                    last = pe.matmul(ps[2 + u][:, 0:E1 + 1], xnT5[:, u, c], gtT[:, c, :], start=(c == 0), stop=(c == DC - 1))
                last.then_inc(lg5_ps, 1)

            def low_rank(t):
                if t == 0:
                    pe.wait_ge(lora_in, 16 * 8)
                for n in (2 * t, 2 * t + 1):
                    if n >= 4:
                        pe.wait_ge(lora_add, n - 3)
                    if n < 8:
                        for k in range(2):
                            last = pe.matmul(ps[4 + n % 4][:, k * D:(k + 1) * D], lora_oa[:, (2 * n + k) * P:(2 * n + k + 1) * P],
                                             lora_ob, start=True, stop=True)
                        last.then_inc(lora_mm, 1)
                    else:
                        j, m, q = LORA_ORDER[n // 8 - 1], n // 4 % 2, n % 4
                        rows = slice(32 * j, 32 * j + RANK)
                        pe.matmul(ps[4 + n % 4][:, :], lora_a[rows, m * P:(m + 1) * P], lora_b[rows, q * 512:(q + 1) * 512],
                                  start=True, stop=True).then_inc(lora_mm, 1)

            by_groups(lambda t: None, lambda t, u: None, low_rank, lambda g: None, follow_a, follow_b)
            pe.wait_ge(chosen, 1)
            pe.matmul(ps[4][:, 0:NT * E1], tri_bf[:, :], flat(mkA), start=True, stop=True)
            pe.matmul(ps[5][:, 0:NT * E1], ones_bf[:, :], flat(mkA), start=True, stop=True).then_inc(counted, 1)
            pe.wait_ge(table_in, 3)
            for n in range(NT * K1):
                last = pe.matmul(ps[6][:, 0:2 * XT], ohloA[:, n], tab5[:, n], start=(n == 0), stop=(n == NT * K1 - 1))
            last.then_inc(table_mm, 1)
            stage_end(pe, 4)


            def project(h, gg, hh):
                for s in range(2):
                    upto(pe, swap_rd, 2 * h + s - 2)
                    for c in range(DC):
                        for w, x in PARTS:
                            last = pe.matmul(ps[s][:, :], wqk[gg][:, s * DC + c, w, hh * DH:(hh + 1) * DH], hT[gg][:, :, x, c, :],
                                             start=(c == 0 and w == x), stop=(c == DC - 1 and w == 1))
                    last.then_inc(proj_mm, 1)

            def values(n, g, gg, q):
                if q == 0:
                    h_in.done(pe, n, gg)
                    upto(pe, op_rd, 2 * n - 4)
                upto(pe, v_rd, n * TPB + q - 1)
                for c in range(DC):
                    for x, w in PARTS:
                        last = pe.matmul(ps[2][:, :], hT[gg][:, q, x, c, :],
                                         wvo16[:, bass.ds(UNITS + c * NG + g, 1), w, :].rearrange("p a n -> p (a n)"),
                                         start=(c == 0 and w == x), stop=(c == DC - 1 and x == 1))
                last.then_inc(v_ps, 1)

            def scores(h, u):
                upto(pe, rope_done, 2 * h + 1)
                upto(pe, sm_done, h - 1)
                for q in range(TPB):
                    last = pe.matmul(ps[3 + q // 2][:, (q % 2) * KW:(q % 2 + 1) * KW], qr[:, u, q * P:(q + 1) * P],
                                     kr[:, u, q * P:q * P + KW], start=True, stop=True)
                last.then_inc(sc_ps, 1)

            def turn_probs(h, hh):
                upto(pe, pn_done, h)
                for half in range(2):
                    upto(pe, pt_rd[half], h - 1)
                    for q in range(2):
                        tile, at = 2 * half + q, q * KW
                        last = pe.transpose(ps[5 + half][:, at + WIN:at + KW], pp[hh % 2][:, tile, P:2 * P], ident[:, :])
                        if tile:
                            last = pe.transpose(ps[5 + half][:, at:at + WIN], pp[hh % 2][0:WIN, tile, 0:P], ident[0:WIN, 0:WIN])
                    last.then_inc(pt_ps, 1)

            def attend(h, n, gg, hh):
                upto(pe, ot_rd, h - 1)
                if hh == 0:
                    upto(pe, op_rd, 2 * n - 1)
                for q in range(TPB):
                    if q % 2 == 0:
                        upto(pe, pt_rd[q // 2], h)
                    at = q % 2 * KW
                    last = pe.matmul(ps[7][:, q * P:(q + 1) * P], vv[gg][:, q, hh * DH:(hh + 1) * DH], pT[:, q // 2, at + WIN:at + KW],
                                     start=True, stop=(q == 0), skip_group_check=True)
                    if q:
                        last = pe.matmul(ps[7][:, q * P:q * P + WIN], vv[gg][:, q - 1, hh * DH:(hh + 1) * DH],
                                         pT[:, q // 2, at:at + WIN], start=False, stop=True, skip_group_check=True)
                last.then_inc(ot_ps, 1)

            def output(n, g, gg, valued):
                upto(pe, ot_rd, n * GH + GH - 2)
                upto(pe, v_rd, (n + valued) * TPB + TPB - 1)
                for half in range(2):
                    for q in range(2):
                        for hh in range(GH):
                            if half == 0 and q == 0 and hh == GH - 1:
                                upto(pe, ot_rd, n * GH + GH - 1)
                            for x, w in PARTS:
                                last = pe.matmul(ps[2 if half == 0 else 7][:, q * D:(q + 1) * D],
                                                 oT[gg][:, x, hh, (2 * half + q) * P:(2 * half + q + 1) * P],
                                                 wvo16[:, bass.ds(2 * g + hh // 2, 1), w, hh % 2 * D:(hh % 2 + 1) * D].rearrange("p a d -> p (a d)"),
                                                 start=(hh == 0 and w == x), stop=(hh == GH - 1 and x == 1))
                    last.then_inc(op_ps, 1)

            h_in.done(pe, 0, 0)
            project(0, 0, 0)
            for q in range(TPB):
                values(0, 0, 0, q)
            project(1, 0, 1)
            upto(pe, v_rd, TPB - 1)
            scores(0, 0)

            def pair(i, last_pair):
                for k in range(2 * GH):
                    h, n, gg, hh = 2 * GH * i + k, 2 * i + k // GH, k // GH, k % GH
                    if not (last_pair and k >= 2 * GH - 2):
                        project(h + 2, (k + 2) // GH % 2, (k + 2) % GH)
                    if not (last_pair and k == 2 * GH - 1):
                        scores(h + 1, (k + 1) % 2)
                    turn_probs(h, hh)
                    if gg == 0:
                        values(n + 1, 2 * (i % 2) + 1, 1, hh)
                    elif not last_pair:
                        values(n + 1, 2 * ((i + 1) % 2), 0, hh)
                    attend(h, n, gg, hh)
                    if hh == GH - 1:
                        output(n, 2 * (i % 2) + gg, gg, 0 if last_pair and gg else 1)

            by_pairs(pe, pair)
            stage_end(pe, 5)

            def shared_up(b, c):
                n, rows = FC * b + c, min(P, FS - c * P)
                upto(pe, hs_ready, n - 2)
                for g in range(2):
                    for d in range(DC):
                        for w, x in PARTS:
                            last = pe.matmul(ps[2 * (c % 2) + g][0:rows, :], sgw16[:, 2 * d + g, w, c * P:c * P + rows],
                                             xb16[:, b % 2, :, x, d * P:(d + 1) * P],
                                             start=(d == 0 and w == x), stop=(d == DC - 1 and w == 1))
                last.then_inc(gus_ps, 1)

            def shared_down(b, k, after_routed):
                t = TPB * b + k
                upto(pe, hs_ready, FC * b + FC - 1)
                if b >= 2:
                    done(pe, sum_done, t - TPB)
                else:
                    upto(pe, ys_rd, t - TPB)
                if after_routed:
                    upto(pe, y1_rd, XT - 1)
                for c in range(FC):
                    rows = min(P, FS - c * P)
                    last = pe.matmul(ps[4 + k][:, 0:D], hsT[0:rows, c, k * P:(k + 1) * P], sdw[0:rows, c], start=(c == 0), stop=(c == FC - 1))
                last.then_inc(ys_ps, 1)

            def shared(b, after_routed):
                for c in range(1 if b > 1 else 0, FC):
                    shared_up(b, c)
                if 1 <= b < NB - 1:
                    pe.wait_ge(xb_in[(b + 1) % 2], 16 * ((b + 1) // 2 + 1))
                    shared_up(b + 1, 0)
                for k in range(TPB):
                    shared_down(b, k, after_routed)
                    if k == 0:
                        pe.sem_inc(xb_used, 1)

            pe.wait_ge(ffn_in, 48)
            pe.wait_ge(lo_done, 4 * UNITS + SGU)
            pe.wait_ge(xb_in[0], 16)
            shared(0, False)

            pe.wait_ge(w2_in, 32)
            pe.wait_ge(lo_done, 4 * UNITS + SGU + E1)

            def expert_of(j):
                return pe.value_load(etab[0:1, bass.ds(j, 1)], min_val=0, max_val=E1 - 1)

            registers = [pe.alloc_register(f"expert{u}") for u in range(2)]
            carried = [bass.RuntimeValue.of_register_unchecked(r, min_val=0, max_val=E1 - 1) for r in registers]
            for u in range(2):
                pe.reg_load(registers[u], etab[0:1, u:u + 1])
            experts = {}

            def rows_in(i, j, u):
                pe.wait_ge(xs_in[u], 16 * (i + 1))
                upto(pe, xs_lo, j - 1)
                for c in range(DC):
                    last = pe.transpose(ps[0][:, c * P:(c + 1) * P], xs[:, u, c * P:(c + 1) * P], ident[:, :])
                last.then_inc(xsT_ps, 1)

            def up_proj(e, lhs, bank):
                for c in range(DC):
                    for x, w in PARTS:
                        last = pe.matmul(ps[bank][:, 0:2 * F1], lhs[:, x, c * P:(c + 1) * P],
                                         w13[:, bass.ds(e, 1), w, c * 2 * F1:(c + 1) * 2 * F1].rearrange("p a f -> p (a f)"),
                                         start=(c == 0 and x == w), stop=(c == DC - 1 and x == 1))
                return last

            def turn_h(u):
                pe.transpose(ps[5][:, 0:P], h1[:, u, 0:P], ident[:, :])
                return pe.transpose(ps[5][0:F1 - P, P:2 * P], h1[:, u, P:F1], ident[:, :])

            def down_proj(e, u, bank, start, stop):
                pe.matmul(ps[bank][:, 0:D], h1T[:, u, 0:P], w2a[:, bass.ds(e, 1), :].rearrange("p a d -> p (a d)"),
                          start=start, stop=False)
                return pe.matmul(ps[bank][:, 0:D], h1T[0:F1 - P, u, P:2 * P],
                                 w2b[:, bass.ds(e, 1), :].rearrange("p a d -> p (a d)"), start=False, stop=stop)

            def routed_up(e, j, u):
                upto(pe, xs_lo, j)
                upto(pe, h1_ready, j - 4)
                up_proj(e, xsT[:, u], 1 + u).then_inc(gu1_ps, 1)

            def routed(i, k, last_tiles):
                j = 4 * i + k
                if k < 2:
                    experts[k] = expert_of(j) if last_tiles else carried[k]
                    ahead = experts[k + 2] = expert_of(j + 2)
                elif not last_tiles:
                    pe.reg_load(registers[k - 2], etab[0:1, bass.ds(j + 2, 1)])
                    ahead = carried[k - 2]
                upto(pe, h1_ready, j)
                upto(pe, h1T_rd, j - 1)
                turn_h(k % 2).then_inc(h1T_ps, 1)
                if not (last_tiles and k >= 1):
                    rows_in(i + (k + 3) // 4, j + 3, (k + 3) % 4)
                if not (last_tiles and k >= 2):
                    routed_up(ahead, j + 2, (k + 2) % 4)
                upto(pe, h1T_rd, j)
                upto(pe, y1_rd, j - 2)
                down_proj(experts[k], k % 2, 6 + k % 2, True, True).then_inc(y1_ps, 1)

            for j in range(3):
                rows_in(0, j, j)
            routed_up(expert_of(0), 0, 0)
            routed_up(expert_of(1), 1, 1)
            upto(pe, ys_rd, TPB - 1)
            with pe.Fori(0, XT // 4 - 1) as i:
                for k in range(4):
                    routed(i, k, False)
            for k in range(4):
                routed(XT // 4 - 1, k, True)

            pe.wait_ge(xb_in[1], 16)
            for b in range(1, NB):
                shared(b, True)

        @block.scalar
        def _(act):
            credit(act, "act")
            act.wait_ge(var_ready, 1)
            nc.scalar.activation(tmpa, var, ACT.Sqrt).then_inc(std_ready, 1)
            stage_end(act, 0)

            def normed(t, u):
                free(act, xnT_ps, t)
                xn_stored.free(act, t, u)
                nc.scalar.activation(xn[:, u], row(x_sb[:, bass.ds(t, 1), :]), ACT.Identity,
                                     bias=nmr[:, bass.ds(t, 1)], scale=rstd[:, bass.ds(t, 1)]).then_inc(xn_ready, 1)

            def turned(t, u):
                done(act, xnT_ps, t)
                free(act, qkv_ps, t)
                nc.scalar.activation(flat(xnT[:, u]), ps[u][:, 0:D], ACT.Copy).then_inc(xnT_rd, 1)

            def qkv_out(t, u):
                done(act, qkv_ps, t)
                nc.scalar.activation(row(qkv[:, bass.ds(t, 1), :]), ps[2 + u][:, :], ACT.Copy).then_inc(qkv_rd, 1)

            normed(0, 0)
            normed(1, 1)
            turned(0, 0)
            normed(2, 0)
            with act.Fori(0, NT // 2 - 2) as i:
                for u in range(2):
                    t = 2 * i + u
                    turned(t + 1, 1 - u)
                    normed(t + 3, 1 - u)
                    qkv_out(t, u)
            for t in range(NT - 4, NT):
                if t + 1 < NT:
                    turned(t + 1, (t + 1) % 2)
                if t + 3 < NT:
                    normed(t + 3, (t + 1) % 2)
                qkv_out(t, t % 2)
            done(act, ss_ready, NT - 1)
            nc.scalar.activation(flat(ss), flat(ss), ACT.Sqrt).then_inc(nrm_sq, 1)
            stage_end(act, 1)

            def sum_out(t, u):
                upto(act, cum_ps, t)
                upto(act, y_ready, t - 2)
                nc.scalar.activation(cs[:, u], ps[u][:, 0:D], ACT.Copy).then_inc(cum_rd, 1)

            def spectral(b, last_batch):
                for tt in range(TPB):
                    t, u = TPB * b + tt, tt % 2
                    upto(act, yT_ps, t)
                    upto(act, s0_ps, t - 2)
                    nc.scalar.activation(flat(yT[:, u]), ps[2 + u][:, 0:D], ACT.Copy).then_inc(yT_rd, 1)
                    if not (last_batch and tt >= TPB - 2):
                        sum_out(t + 2, u)
                    upto(act, s0_ps, t)
                    nc.scalar.activation(row(s_sb[:, bass.ds(t, 1), :]), ps[4 + u][:, 0:D], ACT.Copy).then_inc(s0_rd, 1)

            sum_out(0, 0)
            sum_out(1, 1)
            spectral(0, False)
            act.wait_ge(exp0_in, 1)
            nc.scalar.activation(flat(exA0), flat(exA0), ACT.Exp)
            nc.scalar.activation(flat(ex8), flat(ex8), ACT.Exp)
            act.drain().then_inc(exp0_done, 1)
            with act.Fori(1, NB - 1) as b:
                spectral(b, False)
            spectral(NB - 1, True)
            act.wait_ge(ohhi0_ready, 1)
            nc.scalar.activation(tab_rhs[:, :, 0:PAIRS], ohhi, ACT.Copy, scale=pid[:, 0:1]).then_inc(table0_in, 1)
            stage_end(act, 2)

            def rows_out(j, u):
                upto(act, xgT_ps, j)
                upto(act, gu_ps, j - 4)
                nc.scalar.activation(flat(xgT[:, u]), ps[u % 2][:, 0:D], ACT.Copy).then_inc(xgT_rd, 1)

            def gate_out(j, u):
                upto(act, gu_ps, j)
                upto(act, hm_ready, j - 4)
                nc.scalar.activation(sg0[:, u], ps[2 + u % 2][0:F0, 0:P], ACT.Silu).then_inc(sg_ready, 1)

            def experts(i, k, last_pairs):
                j = 4 * i + k
                if not (last_pairs and k >= 2):
                    rows_out(j + 2, (k + 2) % 4)
                if not (last_pairs and k == 3):
                    gate_out(j + 1, (k + 1) % 4)

            rows_out(0, 0)
            rows_out(1, 1)
            gate_out(0, 0)
            with act.Fori(0, PAIRS // 4 - 1) as i:
                for k in range(4):
                    experts(i, k, False)
            for k in range(4):
                experts(PAIRS // 4 - 1, k, True)
            stage_end(act, 3)

            def begin(t):
                act.wait_ge(yg_in[t % 4], 16 * K0 * (t // 4 + 1))
                free(act, x1_done, t)
                nc.scalar.activation(mix[:, t % 2], yg[:, t % 4, 0], ACT.Copy, scale=w8[:, t, 0:1]).then_inc(mix_begun, 1)

            def finish(t, u):
                upto(act, mix_done, t)
                nc.scalar.activation(mix[:, u], mix[:, u], ACT.Silu).then_inc(g_ready, 1)

            def high_parts(t):
                for n in (2 * t - 2, 2 * t - 1):
                    if n >= 0:
                        raw, parts = unit(n)
                        act.wait_ge(lora_add, n + 1)
                        if n:
                            act.wait_ge(lo_done, n)
                        nc.scalar.activation(parts[:, 0], raw, ACT.Copy, scale=unit_scale(n)).then_inc(hi_done, 1)
                if t in (13, 16):
                    act.wait_ge(lo_done, 24 if t == 13 else 32)
                    for k in range(NG):
                        act.dma_start(wqk_d[k, :, t // 16], wqk_parts[:, t // 16, :, k]).then_inc(wqk_out, 16)

            def between(g):
                at = slice(GT * g, GT * g + GT)
                act.wait_ge(var_ready, 2 * g + 2)
                nc.scalar.activation(tmpa[:, at], var[:, at], ACT.Sqrt).then_inc(std_ready, 1)
                act.wait_ge(var_ready, 2 * g + 3)
                nc.scalar.activation(tmpb[:, at], tmpb[:, at], ACT.Sqrt).then_inc(std_ready, 1)
                act.wait_ge(stats_ready, g + 1)
                if g == NT // GT - 1:
                    high_parts(NT)

            def follow_a(t, u):
                free(act, tr5_ps, t)
                free(act, lg5_ps, t)
                free(act, xn2_kept, t)
                xn2_out.free(act, t, u)
                nc.scalar.activation(xn2[:, u], row(x_sb[:, bass.ds(t, 1), :]), ACT.Identity,
                                     bias=nmr[:, bass.ds(t, 1)], scale=rstd[:, bass.ds(t, 1)])
                act.drain()
                nc.scalar.activation(hh2[:, u], xn2[:, u], ACT.Copy, scale=rms[:, bass.ds(t, 1)]).then_inc(xn2_ready, 1)

            def follow_b(t, u):
                done(act, tr5_ps, t)
                tr5_out.free(act, t, u)
                free(act, lg5_ps, t)
                nc.scalar.activation(tr16[:, u, 0], ps[u][:, 0:2 * D], ACT.Copy, scale=UP_X)
                nc.scalar.activation(flat(xnT5[:, u]), ps[u][:, D:2 * D], ACT.Copy)
                act.drain().then_inc(tr5_rd, 1)

            by_groups(begin, finish, high_parts, between, follow_a, follow_b)
            act.wait_ge(exp5_in, 1)
            nc.scalar.activation(flat(exA), flat(exA), ACT.Exp)
            nc.scalar.activation(flat(w4[:, :, :]), flat(w4[:, :, :]), ACT.Exp)
            nc.scalar.activation(sgA, lgA[:, :, E1], ACT.Exp, scale=-1.0)
            act.drain().then_inc(exp5_done, 1)
            act.wait_ge(ohhi_ready, 1)
            nc.scalar.activation(tab5[:, :, 0:XT], ohhiA, ACT.Copy, scale=pid[:, 0:1])
            for t in range(HC1 // K1, NT):
                last = nc.scalar.activation(tab5[:, K1 * t:K1 * (t + 1), XT:2 * XT], ohhiA[:, K1 * t:K1 * (t + 1)], ACT.Copy,
                                            scale=tile_id[:, t:t + 1])
            act.drain().then_inc(table_in, 1)
            stage_end(act, 4)

            def swap(h):
                for s in range(2):
                    k = 2 * h + s
                    upto(act, cos_rd, k)
                    upto(act, rope_done, k - 2)
                    nc.scalar.activation(qk_s[0:64, s], ps[s][64:P, :], ACT.Copy)
                    nc.scalar.activation(qk_s[64:P, s], ps[s][0:64, :], ACT.Copy).then_inc(swap_rd, 1)

            def probs_out(h):
                upto(act, pt_ps, 2 * h)
                upto(act, ot_ps, h - 1)
                nc.scalar.activation(pT[:, 0, WIN:2 * KW], ps[5][:, WIN:2 * KW], ACT.Copy).then_inc(pt_rd[0], 1)

            def value_out(n, gg, q):
                upto(act, v_ps, n * TPB + q)
                nc.scalar.activation(vv[gg][:, q], ps[2][:, :], ACT.Copy, scale=DOWN).then_inc(v_rd, 1)

            def exponentials(h, u):
                upto(act, sm_done, h)
                upto(act, pt_ps, 2 * h - 3)
                upto(act, rs_done, h - 1)
                for q in range(TPB):
                    nc.scalar.activation(pp[u][:, q, P - WIN:2 * P], sm[:, q], ACT.Exp, bias=mn[:, q:q + 1], scale=-1.0,
                                         accum_out=rs[:, q:q + 1])
                act.drain().then_inc(pe_done, 1)

            swap(0)
            for q in range(TPB):
                value_out(0, 0, q)
            swap(1)
            exponentials(0, 0)

            def shared_high(n):
                act.wait_ge(ffn_in, 48)
                if n:
                    act.wait_ge(lo_done, 4 * UNITS + n)
                nc.scalar.activation(sgw16[:, n, 0], sgw[:, n], ACT.Copy, scale=UP_W).then_inc(hi_done, 1)

            def pair(i, last_pair):
                for k in range(2 * GH):
                    h, n, gg, hh = 2 * GH * i + k, 2 * i + k // GH, k // GH, k % GH
                    if not (last_pair and k >= 2 * GH - 2):
                        swap(h + 2)
                    elif k == 2 * GH - 2:
                        shared_high(1)
                    probs_out(h)
                    if last_pair and k == 2 * GH - 1:
                        shared_high(3)
                    if not (last_pair and k == 2 * GH - 1):
                        exponentials(h + 1, (k + 1) % 2)
                    if last_pair and 2 * GH - 3 <= k < 2 * GH - 1:
                        shared_high(2 * (k - (2 * GH - 3)))
                    if not (last_pair and gg):
                        value_out(n + 1, 1 - gg, hh)

            by_pairs(act, pair)
            stage_end(act, 5)

            def evacuate(dst, src):
                nc.scalar.activation(dst, src, ACT.Copy)

            def shared_gate(b, c):
                n, rows = FC * b + c, min(P, FS - c * P)
                upto(act, gus_ps, n)
                upto(act, hs_ready, n - 2)
                nc.scalar.activation(sgs[0:rows, c % 2], ps[2 * (c % 2)][0:rows, :], ACT.Silu, scale=DOWN).then_inc(sgs_ready, 1)

            for c in range(FC):
                shared_gate(0, c)
                for e in SPLIT_AFTER[c]:
                    if e == 0:
                        act.wait_ge(ffn_in, 48 + 16 * DC)
                    if e == E1 // 2:
                        act.wait_ge(w13_in, 16 * DC)
                    if e >= 2:
                        act.wait_ge(lo_done, 4 * UNITS + SGU + e - 1)
                    nc.scalar.activation(w13[:, e, 0], flat(w13_raw[:, e]), ACT.Copy, scale=UP_W).then_inc(hi_done, 1)

            def rows_out(j, u):
                upto(act, xsT_ps, j)
                upto(act, gu1_ps, j - 4)
                nc.scalar.activation(xsT[:, u, 0], ps[0][:, 0:D], ACT.Copy, scale=UP_X).then_inc(xsT_rd, 1)

            def gate_out(s_in, s_free, s_out, j, u):
                upto(act, s_in, j)
                upto(act, s_free, j - 2)
                nc.scalar.activation(sg1[:, u % 2], ps[1 + u][:, 0:F1], ACT.Silu, scale=DOWN).then_inc(s_out, 1)

            def h_out(s_in, s_free, s_out, j, u):
                upto(act, s_in, j)
                upto(act, s_free, j - 2)
                nc.scalar.activation(h1T[:, u, 0:P], ps[5][:, 0:P], ACT.Copy)
                nc.scalar.activation(h1T[0:F1 - P, u, P:2 * P], ps[5][0:F1 - P, P:2 * P], ACT.Copy)
                act.drain().then_inc(s_out, 1)

            def routed(i, k, last_tiles):
                j = 4 * i + k
                h_out(h1T_ps, y1_ps, h1T_rd, j, k % 2)
                if not (last_tiles and k >= 1):
                    rows_out(j + 3, (k + 3) % 4)
                if not (last_tiles and k >= 2):
                    gate_out(gu1_ps, h1_ready, sg1_ready, j + 2, (k + 2) % 4)

            for j in range(3):
                rows_out(j, j)
            for j in range(2):
                gate_out(gu1_ps, h1_ready, sg1_ready, j, j)
            with act.Fori(0, XT // 4 - 1) as i:
                for k in range(4):
                    routed(i, k, False)
            for k in range(4):
                routed(XT // 4 - 1, k, True)

            def out_gate(t, u):
                done(act, sum_done, t)
                free(act, fin_ready, t)
                nc.scalar.activation(g1[:, u], mix1[:, u], ACT.Silu).then_inc(g1_ready, 1)

            for b in range(1, NB):
                for c in range(FC + 1):
                    if c < FC:
                        shared_gate(b, c)
                    for k in range(TPB):
                        if SUM_AFTER[b == 1][k] is not None and c == SUM_AFTER[b == 1][k] + 1:
                            out_gate(TPB * (b - 1) + k, k % 2)
                out_gate(TPB * b, 0)
                out_gate(TPB * b + 1, 1)
            out_gate(NT - 2, 0)
            out_gate(NT - 1, 1)

        @block.vector
        def _(dve):
            credit(dve, "dve")
            nc.vector.memset(ones[:, :], 1.0)
            nc.vector.memset(ones_bf[:, :], 1.0)
            dve.wait_ge(x_in, 16)

            def statistics(at, times):
                dve.drain()
                nc.vector.tensor_tensor(tmpa[:, at], stat6[:, at, 1], stat6[:, at, 4], ALU.subtract)
                nc.vector.tensor_tensor(nmr[:, at], stat6[:, at, 1], stat6[:, at, 4], ALU.add)
                nc.vector.tensor_tensor(var[:, at], stat6[:, at, 2], stat6[:, at, 5], ALU.add)
                dve.drain()
                nc.vector.tensor_tensor(tmpa[:, at], tmpa[:, at], tmpa[:, at], ALU.mult)
                nc.vector.tensor_scalar(var[:, at], var[:, at], 1.0 / D, LN_EPS, ALU.mult, ALU.add)
                dve.drain()
                nc.vector.scalar_tensor_tensor(var[:, at], tmpa[:, at], 0.25, var[:, at], ALU.mult, ALU.add).then_inc(var_ready, 1)
                dve.wait_ge(std_ready, times)
                nc.vector.reciprocal(rstd[:, at], tmpa[:, at])
                dve.drain()
                nc.vector.scalar_tensor_tensor(nmr[:, at], nmr[:, at], -0.5, rstd[:, at], ALU.mult, ALU.mult)

            with dve.Fori(0, NT) as t:
                nc.vector.bn_stats(row(stat6[:, bass.ds(t, 1), :]), row(x_sb[:, bass.ds(t, 1), :]))
            statistics(slice(0, NT), 1)
            dve.wait_ge(w0_mm, 1)
            for m in range(DC):
                nc.vector.tensor_copy(wqkv0[:, m, :], ps[m][:, :])
                nc.vector.tensor_copy(wo0[:, m, :], ps[2 + m][:, 0:D])
            dve.wait_ge(consts_in, 16 * 8)
            nc.vector.tensor_copy(iota_bf[:, :], iota[:, :])
            nc.vector.tensor_tensor(tri_bf[:, :], tri[:, :], ident[:, :], ALU.subtract)
            stage_end(dve, 0)

            def front(t, u):
                done(dve, qkv_ps, t)
                nc.vector.tensor_copy(lg[:, u], ps[4 + u][:, 0:E0]).then_inc(lg_rd, 1)
                dve.drain()
                nc.vector.max(mx[:, u], lg[:, u])
                nc.vector.tensor_copy(row(lgA0[:, bass.ds(t, 1), :]), lg[:, u])
                dve.drain()
                nc.vector.max_index(mi[:, u], mx[:, u], lg[:, u])
                nc.vector.tensor_copy(row(mxA0[:, bass.ds(t, 1), :]), mx[:, u])
                dve.drain()
                nc.vector.tensor_copy(idA0[:, bass.ds(t * K0, K0)], mi[:, u])

            def back_(t, u):
                done(dve, sq_ready, t)
                nc.vector.tensor_reduce(row(ss[:, bass.ds(t, 1), :]), sq[:, u].rearrange("p (g d) -> p g d", d=HD0), AX.X, ALU.add)\
                    .then_inc(ss_ready, 1)

            pipelined(front, back_, dve)
            dve.wait_ge(nrm_sq, 1)
            nc.vector.reciprocal(flat(ss), flat(ss))
            stage_end(dve, 1)

            oh_flat = ohe.rearrange("p n k e -> p (n k) e")
            nc.vector.tensor_tensor(oh_flat, iota_bf[:, 0:E0].unsqueeze(1).to_broadcast([P, NC0, E0]),
                                    idA0.unsqueeze(2).to_broadcast([P, NC0, E0]), ALU.is_equal)
            dve.drain()
            nc.vector.tensor_tensor(ohs[0], ohe[:, :, 0:4], ohe[:, :, 4:8], ALU.add)
            dve.drain()
            nc.vector.tensor_tensor(ohs[1], ohs[0][:, :, 0:2], ohs[0][:, :, 2:4], ALU.add)
            dve.drain()
            nc.vector.tensor_tensor(mk0, ohs[1][:, :, 0], ohs[1][:, :, 1], ALU.add)
            dve.drain().then_inc(chosen0, 1)
            nc.vector.tensor_tensor(exA0, lgA0, mxA0[:, :, 0:1].to_broadcast([P, NT, E0]), ALU.subtract)
            nc.vector.tensor_tensor(ex8, mxA0, mxA0[:, :, 0:1].to_broadcast([P, NT, K0]), ALU.subtract)
            nc.vector.tensor_copy(tileA0.rearrange("p (n k) -> p n k", k=K0), tile_id[:, :].unsqueeze(2).to_broadcast([P, NT, K0]))
            dve.drain().then_inc(exp0_in, 1)
            dve.wait_ge(counted0, 1)
            for k in range(K0):
                for half in range(2):
                    at = slice(half * NT // 2, (half + 1) * NT // 2)
                    nc.vector.tensor_tensor(prod[:, at, k], ohe[:, at, k], ps[6 + half][:, :].rearrange("p (n e) -> p n e", e=E0), ALU.mult)
            dve.drain()
            pos = flat(pos8[:, :, :])
            nc.vector.tensor_reduce(pos, prod.rearrange("p n k e -> p (n k) e"), AX.X, ALU.add)
            dve.drain()
            nc.vector.tensor_scalar(badA0, pos, float(CAP), float(FULL), ALU.is_ge, ALU.mult)
            nc.vector.scalar_tensor_tensor(dstA0, idA0, float(CAP), pos, ALU.mult, ALU.add)
            dve.drain()
            nc.vector.tensor_tensor(dstI0, dstA0, badA0, ALU.add)
            nc.vector.tensor_tensor(flat(dest[:, :, :]), dstA0, badA0, ALU.add)
            dve.drain()
            nc.vector.tensor_scalar(loA0, dstI0, P - 1, None, ALU.bitwise_and)
            nc.vector.tensor_scalar(hiA0, dstI0, 7, None, ALU.arith_shift_right)
            dve.drain()
            nc.vector.tensor_tensor(ohhi, iota_bf[:, 0:PAIRS].unsqueeze(1).to_broadcast([P, NC0, PAIRS]),
                                    hiA0.unsqueeze(2).to_broadcast([P, NC0, PAIRS]), ALU.is_equal)
            dve.drain().then_inc(ohhi0_ready, 1)
            nc.vector.tensor_tensor(ohlo, iota_bf[:, :].unsqueeze(1).to_broadcast([P, NC0, P]),
                                    loA0.unsqueeze(2).to_broadcast([P, NC0, P]), ALU.is_equal)
            nc.vector.tensor_tensor(tab_rhs[:, :, PAIRS:2 * PAIRS], ohhi, tileA0.unsqueeze(2).to_broadcast([P, NC0, PAIRS]), ALU.mult)
            dve.drain().then_inc(table0_in, 1)
            dve.wait_ge(exp0_done, 1)
            nc.vector.tensor_reduce(zsum[:, :], exA0, AX.X, ALU.add)
            dve.drain()
            nc.vector.reciprocal(rz[:, :], zsum[:, :])
            dve.drain()
            nc.vector.tensor_tensor(ex8, ex8, rz[:, :].unsqueeze(2).to_broadcast([P, NT, K0]), ALU.mult)
            dve.drain()
            nc.vector.tensor_reduce(zsum[:, :], ex8, AX.X, ALU.add)
            dve.drain()
            nc.vector.tensor_scalar(zsum[:, :], zsum[:, :], 1e-20, None, ALU.add)
            dve.drain()
            nc.vector.reciprocal(rz[:, :], zsum[:, :])
            nc.vector.tensor_scalar(w8[:, :, :], pos8[:, :, :], float(CAP), None, ALU.is_lt)
            dve.drain()
            nc.vector.tensor_tensor(ex8, ex8, rz[:, :].unsqueeze(2).to_broadcast([P, NT, K0]), ALU.mult)
            dve.drain()
            nc.vector.tensor_tensor(w8[:, :, :], w8[:, :, :], ex8, ALU.mult)
            dve.wait_ge(table0_mm, 1)
            nc.vector.tensor_copy(tabf, ps[6][:, 0:PAIRS])
            dve.drain()
            nc.vector.scalar_tensor_tensor(idx0[:, :], ps[6][:, PAIRS:2 * PAIRS], float(P), tabf, ALU.mult, ALU.add)
            stage_end(dve, 2)

            nc.vector.memset(yg[:, 1:4], 0.0).then_inc(zeroed, 1)

            def h_product(j, u):
                upto(dve, sg_ready, j)
                upto(dve, y0_ps, j - 4)
                nc.vector.tensor_tensor(hm0[:, u], ps[2 + u % 2][0:F0, P:2 * P], sg0[:, u], ALU.mult).then_inc(hm_ready, 1)

            def experts(i, k, last_pairs):
                j = 4 * i + k
                if not (last_pairs and k == 3):
                    h_product(j + 1, (k + 1) % 4)
                upto(dve, y0_ps, j)
                y0_out.free(dve, j, k)
                nc.vector.tensor_copy(y0[:, k], ps[4 + k % 2][:, 0:D]).then_inc(y0_rd, 1)

            h_product(0, 0)
            with dve.Fori(0, PAIRS // 4 - 1) as i:
                for k in range(4):
                    experts(i, k, False)
            for k in range(4):
                experts(PAIRS // 4 - 1, k, True)
            stage_end(dve, 3)

            nc.vector.memset(yg[:, 0], 0.0).then_inc(zeroed, 1)

            def begin(t):
                done(dve, mix_begun, t)
                for k in range(1, K0):
                    last = nc.vector.scalar_tensor_tensor(mix[:, t % 2], yg[:, t % 4, k], w8[:, t, k:k + 1], mix[:, t % 2],
                                                          ALU.mult, ALU.add)
                    if k < K0 - 1:
                        dve.drain()
                last.then_inc(mix_done, 1)

            def finish(t, u):
                done(dve, g_ready, t)
                nc.vector.tensor_tensor(mix[:, u], mix[:, u], row(s_sb[:, bass.ds(t, 1), :]), ALU.mult)
                dve.drain()
                nc.vector.tensor_tensor(row(x_sb[:, bass.ds(t, 1), :]), row(x_sb[:, bass.ds(t, 1), :]), mix[:, u], ALU.add)
                dve.drain()
                nc.vector.bn_stats(row(stat6[:, bass.ds(t, 1), :]), row(x_sb[:, bass.ds(t, 1), :])).then_inc(x1_done, 1)

            def low_rank(t):
                if t == 0:
                    dve.wait_ge(wvo_in, 32)
                    nc.vector.tensor_scalar(norm_up[:, :], norm_w[:, :], UP_W, None, ALU.mult)
                if t == NT // 2:
                    dve.wait_ge(wqk_in, 32)
                if t:
                    low_part(2 * t - 2)
                for n in (2 * t, 2 * t + 1):
                    dve.wait_ge(lora_mm, n + 1)
                    raw, _ = unit(n)
                    nc.vector.scalar_tensor_tensor(raw, ps[4 + n % 4][:, :], 1.0 / RANK, raw, ALU.mult, ALU.add).then_inc(lora_add, 1)
                if t:
                    low_part(2 * t - 1)

            def low_part(n):
                raw, parts = unit(n)
                dve.wait_ge(hi_done, n + 1)
                nc.vector.scalar_tensor_tensor(parts[:, 1], raw, unit_scale(n), parts[:, 0], ALU.mult, ALU.subtract).then_inc(lo_done, 1)

            def between(g):
                at = slice(GT * g, GT * g + GT)
                statistics(at, 2 * g + 2)
                nc.vector.tensor_scalar(tmpb[:, at], var[:, at], LN_EPS, None, ALU.subtract)
                nc.vector.reciprocal(rms[:, at], var[:, at])
                dve.drain()
                nc.vector.tensor_tensor(tmpb[:, at], tmpb[:, at], rms[:, at], ALU.mult)
                dve.drain()
                nc.vector.tensor_scalar(tmpb[:, at], tmpb[:, at], RMS_EPS, None, ALU.add)
                dve.drain().then_inc(var_ready, 1)
                dve.wait_ge(std_ready, 2 * g + 3)
                nc.vector.reciprocal(rms[:, at], tmpb[:, at])
                dve.drain().then_inc(stats_ready, 1)
                if g == NT // GT - 1:
                    low_part(2 * NT - 2)
                    low_part(2 * NT - 1)

            def follow_a(t, u):
                done(dve, xn2_ready, t)
                nc.vector.tensor_copy(row(s_sb[:, bass.ds(t, 1), :]), xn2[:, u]).then_inc(xn2_kept, 1)

            def follow_b(t, u):
                done(dve, tr5_rd, t)
                nc.vector.scalar_tensor_tensor(tr16[:, u, 1], ps[u][:, 0:2 * D], UP_X, tr16[:, u, 0], ALU.mult, ALU.subtract).then_inc(h_lo, 1)
                done(dve, lg5_ps, t)
                nc.vector.tensor_copy(lg5[:, u], ps[2 + u][:, 0:E1 + 1]).then_inc(lg5_rd, 1)
                dve.drain()
                nc.vector.max(mx5[:, u], lg5[:, u, 0:E1])
                nc.vector.tensor_copy(row(lgA[:, bass.ds(t, 1), :]), lg5[:, u])
                dve.drain()
                nc.vector.max_index(mi5[:, u], mx5[:, u], lg5[:, u, 0:E1])
                nc.vector.tensor_copy(row(mxA[:, bass.ds(t, 1), :]), mx5[:, u, 0:K1])
                dve.drain()
                nc.vector.tensor_copy(row(idA[:, bass.ds(t, 1), :]), mi5[:, u, 0:K1])

            by_groups(begin, finish, low_rank, between, follow_a, follow_b)
            dve.wait_ge(wqk_out, 16 * 8)
            dve.drain()
            nc.vector.tensor_tensor(exA, lgA[:, :, 0:E1], mxA[:, :, 0:1].to_broadcast([P, NT, E1]), ALU.subtract)
            nc.vector.tensor_tensor(w4[:, :, :], mxA, mxA[:, :, 0:1].to_broadcast([P, NT, K1]), ALU.subtract)
            dve.drain().then_inc(exp5_in, 1)
            for n in range(0, NT, 4):
                nc.vector.tensor_tensor(ohA[:, n:n + 4].rearrange("p n k e -> p (n k) e"),
                                        iota_bf[:, 0:E1].unsqueeze(1).to_broadcast([P, 4 * K1, E1]),
                                        flat(idA[:, n:n + 4]).unsqueeze(2).to_broadcast([P, 4 * K1, E1]), ALU.is_equal)
            dve.drain()
            nc.vector.tensor_tensor(mkA, ohA[:, :, 0], ohA[:, :, 1], ALU.add)
            nc.vector.tensor_tensor(rank, ohA[:, :, 2], ohA[:, :, 3], ALU.add)
            dve.drain()
            nc.vector.tensor_tensor(mkA, mkA, rank, ALU.add)
            dve.drain().then_inc(chosen, 1)
            dve.wait_ge(counted, 1)
            nc.vector.tensor_copy(flat(rank), ps[4][:, 0:NT * E1])
            nc.vector.tensor_copy(flat(cnt[0]), ps[5][:, 0:NT * E1])

            def running(a, b, n, at):
                step = 1
                while step < n:
                    dve.drain()
                    nc.vector.tensor_tensor(at(b, step, n), at(a, step, n), at(a, 0, n - step), ALU.add)
                    nc.vector.tensor_copy(at(b, 0, step), at(a, 0, step))
                    a, b, step = b, a, 2 * step
                dve.drain()
                return a

            nc.vector.tensor_copy(flat(cnt[2]), ps[5][:, 0:NT * E1])
            upto_tile = running(cnt[2], cnt[1], NT, lambda a, lo, hi: a[:, lo:hi])
            nc.vector.tensor_scalar(ntl_i, upto_tile[:, NT - 1], float(P - 1), None, ALU.add)
            dve.drain()
            nc.vector.tensor_scalar(ntl_i, ntl_i, 7, None, ALU.arith_shift_right)
            dve.drain()
            nc.vector.tensor_copy(ntl[0], ntl_i)
            nc.vector.tensor_copy(ntl[2], ntl_i)
            upto_expert = running(ntl[2], ntl[1], E1, lambda a, lo, hi: a[:, lo:hi])
            nc.vector.tensor_tensor(ntl[0], upto_expert, ntl[0], ALU.subtract)
            nc.vector.tensor_tensor(rank, rank, upto_tile, ALU.add)
            nc.vector.tensor_tensor(etmp, iota[0:1, 0:XT].unsqueeze(2).to_broadcast([1, XT, E1]),
                                    upto_expert[0:1].unsqueeze(1).to_broadcast([1, XT, E1]), ALU.is_ge)
            dve.drain()
            nc.vector.tensor_reduce(etf, etmp, AX.X, ALU.add)
            nc.vector.tensor_tensor(rank, rank, cnt[0], ALU.subtract)
            nc.vector.tensor_scalar(ntl[0], ntl[0], float(P), None, ALU.mult)
            dve.drain()
            nc.vector.tensor_scalar(etab[:, :], etf, float(E1 - 1), None, ALU.min)
            nc.vector.tensor_tensor(rank, rank, ntl[0].unsqueeze(1).to_broadcast([P, NT, E1]), ALU.add)
            dve.drain()
            for k in range(K1):
                nc.vector.tensor_tensor(prodA[:, :, k], ohA[:, :, k], rank, ALU.mult)
            dve.drain()
            nc.vector.tensor_reduce(dstA, prodA.rearrange("p n k e -> p (n k) e"), AX.X, ALU.add)
            dve.drain()
            nc.vector.tensor_copy(flat(dest1[:, :, :]), dstA)
            nc.vector.tensor_copy(dstI, dstA)
            nc.vector.tensor_copy(tileA.rearrange("p (n k) -> p n k", k=K1), tile_id[:, :].unsqueeze(2).to_broadcast([P, NT, K1]))
            dve.drain()
            nc.vector.tensor_scalar(loA, dstI, P - 1, None, ALU.bitwise_and)
            nc.vector.tensor_scalar(hiA, dstI, 7, None, ALU.arith_shift_right)
            dve.drain()
            nc.vector.tensor_tensor(ohhiA, iota_bf[:, 0:XT].unsqueeze(1).to_broadcast([P, NT * K1, XT]),
                                    hiA.unsqueeze(2).to_broadcast([P, NT * K1, XT]), ALU.is_equal).then_inc(ohhi_ready, 1)
            nc.vector.tensor_tensor(ohloA, iota_bf[:, :].unsqueeze(1).to_broadcast([P, NT * K1, P]),
                                    loA.unsqueeze(2).to_broadcast([P, NT * K1, P]), ALU.is_equal)
            dve.drain().then_inc(table_in, 1)
            dve.wait_ge(exp5_done, 1)
            nc.vector.tensor_reduce(zA, exA, AX.X, ALU.add)
            nc.vector.tensor_scalar(sgA, sgA, 1.0, None, ALU.add)
            dve.drain()
            nc.vector.reciprocal(zA, zA)
            nc.vector.reciprocal(gate1[:, :], sgA)
            dve.drain()
            nc.vector.tensor_tensor(w4[:, :, :], w4[:, :, :], zA.unsqueeze(2).to_broadcast([P, NT, K1]), ALU.mult)
            dve.wait_ge(table_mm, 1)
            nc.vector.tensor_copy(tab5f, ps[6][:, 0:XT])
            dve.drain()
            nc.vector.scalar_tensor_tensor(idx1[:, :], ps[6][:, XT:2 * XT], float(P), tab5f, ALU.mult, ALU.add)
            stage_end(dve, 4)

            nc.vector.memset(kr[:, :, 0:WIN], 0.0)
            for u in range(2):
                nc.vector.memset(pp[u][:, :, 0:P - WIN], 0.0)
            dve.wait_ge(tabs_in, 64)

            def cosine(h, s):
                upto(dve, proj_mm, 2 * h + s)
                upto(dve, rope_done, 2 * h + s - 2)
                nc.vector.tensor_tensor(qk_c[:, s], ps[s][:, :], cos, ALU.mult).then_inc(cos_rd, 1)

            def turned(h, u, s):
                upto(dve, sin_done, 2 * h + s)
                upto(dve, sc_ps, h - 2)
                dst = qr[:, u] if s == 0 else kr[:, u, WIN:WIN + SEQ]
                nc.vector.tensor_tensor(dst, qk_c[:, s], qk_s[:, s], ALU.add).then_inc(rope_done, 1)

            def masked(h):
                upto(dve, sc_ps, h)
                upto(dve, pe_done, h - 1)
                rest(dve, "dve")
                for q in range(TPB):
                    mask = mask0 if q == 0 else mask1
                    nc.vector.tensor_tensor_reduce(out=sm[:, q], in0=ps[3 + q // 2][:, (q % 2) * KW:(q % 2 + 1) * KW], in1=mask,
                                                   scale=-SCALE, scalar=3e38, op0=ALU.add, op1=ALU.min,
                                                   accum_out=mn[:, q:q + 1])
                dve.drain().then_inc(sm_done, 1)

            def inverse(h):
                upto(dve, pe_done, h)
                upto(dve, pn_done, h - 1)
                nc.vector.reciprocal(ri, rs).then_inc(rs_done, 1)

            def probs_out(h):
                upto(dve, pt_ps, 2 * h + 1)
                upto(dve, ot_ps, h - 1)
                nc.vector.tensor_copy(pT[:, 1, 0:2 * KW], ps[6][:, 0:2 * KW]).then_inc(pt_rd[1], 1)

            for h in range(2):
                cosine(h, 0)
                cosine(h, 1)
                turned(h, h, 0)
                turned(h, h, 1)
            masked(0)
            inverse(0)

            def shared_low(n):
                dve.wait_ge(hi_done, 4 * UNITS + n + 1)
                nc.vector.scalar_tensor_tensor(sgw16[:, n, 1], sgw[:, n], UP_W, sgw16[:, n, 0], ALU.mult, ALU.subtract).then_inc(lo_done, 1)

            def pair(i, last_pair):
                for k in range(2 * GH):
                    h, n, gg, hh = 2 * GH * i + k, 2 * i + k // GH, k // GH, k % GH
                    ahead = not (last_pair and k >= 2 * GH - 2)
                    if ahead:
                        cosine(h + 2, 0)
                        cosine(h + 2, 1)
                    else:
                        shared_low(2 * (k - (2 * GH - 2)))
                    if not (last_pair and k == 2 * GH - 1):
                        masked(h + 1)
                    probs_out(h)
                    if ahead:
                        turned(h + 2, k % 2, 0)
                        turned(h + 2, k % 2, 1)
                    if not (last_pair and k == 2 * GH - 1):
                        inverse(h + 1)
                    if not ahead:
                        shared_low(2 * (k - (2 * GH - 2)) + 1)
                    upto(dve, ot_ps, h)
                    nc.vector.tensor_scalar(oT[gg][:, 0, hh], ps[7][:, :], UP_X, None, ALU.mult)
                    dve.drain()
                    nc.vector.scalar_tensor_tensor(oT[gg][:, 1, hh], ps[7][:, :], UP_X, oT[gg][:, 0, hh], ALU.mult, ALU.subtract)\
                        .then_inc(ot_rd, 1)
                    if hh == GH - 1:
                        for half in range(2):
                            upto(dve, op_ps, 2 * n + half)
                            a = s_sb[:, bass.ds(i // 2 * TPB + 2 * half, 2), :]
                            nc.vector.scalar_tensor_tensor(a, ps[2 if half == 0 else 7][:, :].rearrange("p (a d) -> p a d", a=2), DOWN, a,
                                                           ALU.mult, ALU.add)\
                                .then_inc(op_rd, 1)
                            dve.drain()

            by_pairs(dve, pair)
            stage_end(dve, 5)

            def shared_product(b, c):
                n, rows = FC * b + c, min(P, FS - c * P)
                upto(dve, sgs_ready, n)
                upto(dve, ys_ps, TPB * b - 1)
                nc.vector.scalar_tensor_tensor(hsT[0:rows, c], ps[2 * (c % 2) + 1][0:rows, :], DOWN, sgs[0:rows, c % 2], ALU.mult, ALU.mult).then_inc(hs_ready, 1)

            for c in range(FC):
                shared_product(0, c)
                for e in SPLIT_AFTER[c]:
                    dve.wait_ge(hi_done, 4 * UNITS + SGU + e + 1)
                    nc.vector.scalar_tensor_tensor(w13[:, e, 1], flat(w13_raw[:, e]), UP_W, w13[:, e, 0], ALU.mult, ALU.subtract)\
                        .then_inc(lo_done, 1)
            for k in range(TPB):
                upto(dve, ys_ps, k)
                nc.vector.tensor_copy(sh0[:, k], ps[4 + k][:, 0:D]).then_inc(ys_rd, 1)

            def rows_low(j, u):
                upto(dve, xsT_rd, j)
                nc.vector.scalar_tensor_tensor(xsT[:, u, 1], ps[0][:, 0:D], UP_X, xsT[:, u, 0], ALU.mult, ALU.subtract).then_inc(xs_lo, 1)

            def product(s_in, s_free, s_out, j, u):
                upto(dve, s_in, j)
                upto(dve, s_free, j - 2)
                nc.vector.scalar_tensor_tensor(h1[:, u % 2], ps[1 + u][:, F1:2 * F1], DOWN, sg1[:, u % 2], ALU.mult, ALU.mult).then_inc(s_out, 1)

            def routed(i, k, last_tiles):
                j = 4 * i + k
                if not (last_tiles and k >= 1):
                    rows_low(j + 3, (k + 3) % 4)
                if not (last_tiles and k >= 2):
                    product(sg1_ready, h1T_ps, h1_ready, j + 2, (k + 2) % 4)
                upto(dve, y1_ps, j)
                y1_out.free(dve, j, k)
                nc.vector.tensor_copy(y1s[:, k], ps[6 + k % 2][:, 0:D]).then_inc(y1_rd, 1)

            for j in range(3):
                rows_low(j, j)
            for j in range(2):
                product(sg1_ready, h1T_ps, h1_ready, j, j)
            with dve.Fori(0, XT // 4 - 1) as i:
                for k in range(4):
                    routed(i, k, False)
            for k in range(4):
                routed(XT // 4 - 1, k, True)

            def routed_sum(t, k):
                u = k % 2
                dve.wait_ge(yr_in[u], 16 * K1 // 2 * (t - u) + 16 * K1)
                free(dve, g1_ready, t)
                nc.vector.tensor_scalar(mix1[:, u], yr[:, u, 0], w4[:, t, 0:1], None, ALU.mult)
                for j in range(1, K1):
                    dve.drain()
                    nc.vector.scalar_tensor_tensor(mix1[:, u], yr[:, u, j], w4[:, t, j:j + 1], mix1[:, u], ALU.mult, ALU.add)
                dve.drain().then_inc(yr_used, 1)

            def shared_sum(t, k):
                u = k % 2
                if t >= TPB:
                    upto(dve, ys_ps, t)
                src = sh0[:, k] if t < TPB else ps[4 + k][:, 0:D]
                nc.vector.scalar_tensor_tensor(mix1[:, u], src, gate1[:, t:t + 1], mix1[:, u], ALU.mult, ALU.add).then_inc(sum_done, 1)

            def sum_up(t, k):
                routed_sum(t, k)
                shared_sum(t, k)

            def result(t, k):
                u = k % 2
                done(dve, g1_ready, t)
                out_done.free(dve, t, u)
                nc.vector.tensor_tensor(g1[:, u], g1[:, u], s_sb[:, t], ALU.mult)
                dve.drain()
                nc.vector.tensor_tensor(fin[:, u], x_sb[:, t], g1[:, u], ALU.add).then_inc(fin_ready, 1)

            for b in range(1, NB):
                t0 = TPB * (b - 1)
                for c in range(FC + 1):
                    if c < FC:
                        shared_product(b, c)
                    for k in range(TPB):
                        if c == SUM_AFTER[b == 1][k]:
                            if t0 + k:
                                result(t0 + k - 1, (k - 1) % TPB)
                            sum_up(t0 + k, k)
                    if c == SUM_AFTER[b == 1][TPB - 1] + 1:
                        result(t0 + TPB - 1, TPB - 1)
                    if b > 1 and c in (3, 4):
                        routed_sum(TPB * b + c - 3, c - 3)
                if b == 1:
                    routed_sum(TPB * b, 0)
                shared_sum(TPB * b, 0)
                if b == 1:
                    routed_sum(TPB * b + 1, 1)
                result(TPB * b, 0)
                if b == NB - 1:
                    routed_sum(NT - 2, 2)
                shared_sum(TPB * b + 1, 1)
            result(NT - 3, 1)
            shared_sum(NT - 2, 2)
            routed_sum(NT - 1, 3)
            result(NT - 2, 2)
            shared_sum(NT - 1, 3)
            result(NT - 1, 3)

        @block.gpsimd
        def _(pool):
            credit(pool, "pool")
            stage_end(pool, 0)
            with pool.Fori(0, NT // 2) as i:
                for u in range(2):
                    t = 2 * i + u
                    done(pool, qkv_rd, t)
                    free(pool, ss_ready, t)
                    a = row(qkv[:, bass.ds(t, 1), :])
                    rest(pool, "pool")
                    nc.gpsimd.tensor_tensor(sq[:, u], a, a, ALU.mult).then_inc(sq_ready, 1)
            stage_end(pool, 1)

            def normalise(t, u):
                a = row(qkv[:, bass.ds(t, 1), :]).rearrange("p (h k) -> p h k", k=HD0)
                nc.gpsimd.tensor_tensor(a, a, row(ss[:, bass.ds(t, 1), :]).unsqueeze(2).to_broadcast([P, 2 * H0, HD0]), ALU.mult)\
                    .then_inc(qkn_ready, 1)

            def products(t, u):
                upto(pool, cum_rd, t)
                upto(pool, yT_ps, t - 2)
                rest(pool, "pool")
                v4 = lambda a: a.rearrange("p (h c k) -> p h c k", h=H0, c=2)
                q = row(qkv[:, bass.ds(t, 1), 0:D])
                q4, c4, a4, b4, y4 = v4(q), v4(cs[:, u]), v4(pa), v4(pb), v4(yy[:, u])
                nc.gpsimd.tensor_tensor(pa, q, cs[:, u], ALU.mult)
                nc.gpsimd.tensor_tensor(b4[:, :, 0], q4[:, :, 1], c4[:, :, 0], ALU.mult)
                nc.gpsimd.tensor_tensor(b4[:, :, 1], q4[:, :, 0], c4[:, :, 1], ALU.mult)
                pool.drain()
                nc.gpsimd.tensor_tensor(y4[:, :, 0], a4[:, :, 0], a4[:, :, 1], ALU.subtract)
                nc.gpsimd.tensor_tensor(y4[:, :, 1], b4[:, :, 0], b4[:, :, 1], ALU.add)
                pool.drain()
                nc.gpsimd.tensor_copy(y4[:, :, :, 0], a4[:, :, :, 0])
                pool.drain().then_inc(y_ready, 1)

            normalise(0, 0)
            normalise(1, 1)
            with pool.Fori(0, NT // 2 - 1) as i:
                for u in range(2):
                    normalise(2 * i + u + 2, u)
                    products(2 * i + u, u)
            for u in range(2):
                products(NT - 2 + u, u)
            stage_end(pool, 2)

            with pool.Fori(0, PAIRS // 4) as i:
                for u in range(4):
                    j = 4 * i + u
                    upto(pool, xgT_ps, j - 4)
                    rest(pool, "pool")
                    nc.gpsimd.tensor_copy(ic3[:, u], idx0[:, bass.ds(j, 1)]).then_inc(ic_ready, 1)
                    upto(pool, ic_ready, j)
                    rest(pool, "pool")
                    pool.indirect_dma_start(xg[:, u], None, xn_d, bass.IndirectOffsetOnAxis(ap=ic3[:, u], axis=0)).then_inc(xg_in[u], 16)
            stage_end(pool, 3)

            pool.wait_ge(zeroed, 2)
            with pool.Fori(0, NT // 4) as i:
                for u in range(4):
                    t = 4 * i + u
                    upto(pool, mix_done, t - 4)
                    rest(pool, "pool")
                    nc.gpsimd.tensor_copy(ic4[:, u * K0:(u + 1) * K0].rearrange("p a b -> p (a b)"),
                                          row(dest[:, bass.ds(t, 1), :])).then_inc(ic4_ready, 1)
                    upto(pool, ic4_ready, t)
                    rest(pool, "pool")
                    for k in range(K0):
                        pool.indirect_dma_start(yg[:, u, k], None, y0_d, bass.IndirectOffsetOnAxis(ap=ic4[:, u * K0 + k], axis=0),
                                                bounds_check=SLOTS - 1, oob_is_err=False).then_inc(yg_in[u], 16)
            pool.wait_ge(ohhi_ready, 1)
            nc.gpsimd.tensor_tensor(tab5[:, 0:HC1, XT:2 * XT], ohhiA[:, 0:HC1], tileA[:, 0:HC1].unsqueeze(2).to_broadcast([P, HC1, XT]), ALU.mult)\
                .then_inc(table_in, 1)
            stage_end(pool, 4)

            pool.wait_ge(tabs_in, 64)

            def sine(h):
                for s in range(2):
                    upto(pool, swap_rd, 2 * h + s)
                    rest(pool, "pool")
                    nc.gpsimd.tensor_tensor(qk_s[:, s], qk_s[:, s], sin, ALU.mult).then_inc(sin_done, 1)

            def normalized(h, u):
                upto(pool, rs_done, h)
                rest(pool, "pool")
                a = pp[u][:, :, P - WIN:2 * P]
                nc.gpsimd.tensor_tensor(a, a, ri.unsqueeze(2).to_broadcast([P, TPB, KW]), ALU.mult).then_inc(pn_done, 1)

            sine(0)
            sine(1)
            normalized(0, 0)

            def pair(i, last_pair):
                for k in range(2 * GH):
                    h = 2 * GH * i + k
                    if not (last_pair and k >= 2 * GH - 2):
                        sine(h + 2)
                    if not (last_pair and k == 2 * GH - 1):
                        normalized(h + 1, (k + 1) % 2)

            by_pairs(pool, pair)
            stage_end(pool, 5)

            with pool.Fori(0, XT // 4) as i:
                for u in range(4):
                    j = 4 * i + u
                    upto(pool, xsT_ps, j - 4)
                    rest(pool, "pool")
                    nc.gpsimd.tensor_copy(ic7[:, u:u + 1], idx1[:, bass.ds(j, 1)]).then_inc(ic7_ready, 1)
                    upto(pool, ic7_ready, j)
                    rest(pool, "pool")
                    pool.indirect_dma_start(xs[:, u], None, xn2_d, bass.IndirectOffsetOnAxis(ap=ic7[:, u:u + 1], axis=0)).then_inc(xs_in[u], 16)
            pool.wait_ge(y1_kept, 1)

            with pool.Fori(0, NT // 2) as i:
                for u in range(2):
                    t = 2 * i + u
                    free(pool, yr_used, t)
                    rest(pool, "pool")
                    nc.gpsimd.tensor_copy(ic8[:, u], row(dest1[:, bass.ds(t, 1), :])).then_inc(ic8_ready, 1)
                    done(pool, ic8_ready, t)
                    rest(pool, "pool")
                    for k in range(K1):
                        pool.indirect_dma_start(yr[:, u, k], None, y1_d, bass.IndirectOffsetOnAxis(ap=ic8[:, u, k:k + 1], axis=0)).then_inc(yr_in[u], 16)


DEBUG = ()


def kernel(**inputs):
    import concourse.bacc as bacc
    from concourse.bass_utils import run_bass_kernel_spmd

    a = {k: np.ascontiguousarray(v) for k, v in inputs.items()}
    laid = {
        "x": a["L0_attn_x"].reshape(T, D),
        "wq0": a["L0_attn_W_q"], "wkv0": a["L0_attn_W_kv"], "wo0T": a["L0_attn_W_o"].T,
        "rtT": a["L0_ffn_router_w"].T, "w_gate": a["L0_ffn_w_gate"], "w_up": a["L0_ffn_w_up"], "w_down": a["L0_ffn_w_down"],
        "norm_w": a["L1_attn_norm_w"].reshape(DC, P).T,
        "wqT": a["L1_attn_wq"].T, "wkT": a["L1_attn_wk"].T, "wvT": a["L1_attn_wv"].T, "woT": a["L1_attn_wo"].T,
        "qA": a["L1_attn_qA"], "kA": a["L1_attn_kA"], "vA": a["L1_attn_vA"], "oA": a["L1_attn_oA"],
        "qBT": a["L1_attn_qB"].T, "kBT": a["L1_attn_kB"].T, "vBT": a["L1_attn_vB"].T, "oBT": a["L1_attn_oB"].T,
        "gtT": np.concatenate([a["L1_ffn_gate_w"], a["L1_ffn_sgate_w"]], 0).T,
        "w13T": a["L1_ffn_w13"].transpose(2, 0, 1), "w2T": a["L1_ffn_w2"].transpose(0, 2, 1),
        "sguT": a["L1_ffn_shared_gate_up_w"].T, "sdT": a["L1_ffn_shared_down_w"].T,
    }
    laid.update(constants())
    laid = {k: np.ascontiguousarray(v) for k, v in laid.items()}
    nc = bacc.Bacc("TRN2", target_bir_lowering=False, num_devices=1)
    io = {k: nc.dram_tensor(f"in_{k}", v.shape, F32, kind="ExternalInput").ap() for k, v in laid.items()}
    io["out"] = nc.dram_tensor("out", (T, D), F32, kind="ExternalOutput").ap()
    build(nc, io, DEBUG)
    r = run_bass_kernel_spmd(nc, [{f"in_{k}": v for k, v in laid.items()}], core_ids=[0])
    return r.results[0]["out"].reshape(NB, SEQ, D)
```
